# Optimizing a Trainium2 kernel written in Bass

```python
import numpy as np
import jax
import jax.numpy as jnp

def _softmax(x, axis=-1):
    return jax.nn.softmax(x, axis=axis)

def _gelu(x):
    return jax.nn.gelu(x, approximate=True)

def _silu(x):
    return jax.nn.silu(x)

def _sigmoid(x):
    return jax.nn.sigmoid(x)

def _layernorm(x, axis=-1, eps=1e-05):
    m = jnp.mean(x, axis=axis, keepdims=True)
    v = jnp.var(x, axis=axis, keepdims=True)
    return (x - m) / jnp.sqrt(v + eps)

def _scatter_add(tgt, idx, src, axis=0):
    return tgt.at[idx].add(src)

def _segment_sum(src, seg, n):
    return jax.ops.segment_sum(src, seg, n)
kernel_name = 'mk_adaln_d1_jaxref_r8_e65401'

def setup_inputs(seed: int=0):
    np.random.seed(seed)
    _w = jnp.asarray

    def _L0_attn_setup():
        import jax, jax.numpy as jnp
        import numpy as np
        BLOCK = 32
        EPS = 1e-06

        def _silu(x):
            return x * jax.nn.sigmoid(x)
        key = jax.random.key(seed)
        k1, k2, k3, k4 = jax.random.split(key, 4)
        embed_dim, hidden_dim = (256, 256)
        b, n, h = (2, 512, 16)
        x = jax.random.normal(k1, (b, n, embed_dim), dtype=jnp.float32)
        slope_rate = jax.random.uniform(k2, (h, 1, 1), dtype=jnp.float32, minval=0.01, maxval=1.0)
        W_qkvu = jax.random.normal(k3, (4 * hidden_dim, embed_dim), dtype=jnp.float32) / np.sqrt(embed_dim)
        W_out = jax.random.normal(k4, (embed_dim, hidden_dim), dtype=jnp.float32) / np.sqrt(hidden_dim)
        return {'x': x, 'slope_rate': slope_rate, 'W_qkvu': W_qkvu, 'W_out': W_out}
    _L0_attn_in = _L0_attn_setup()

    def _L0_ffn_setup():
        import jax, jax.numpy as jnp
        import numpy as np
        NUM_EXPERTS = 8
        TOP_K = 2
        HID = 256
        FF = 512
        B, S = (2, 128)
        SCALE = 0.02

        def _gated_mlp(x, w_gate, w_up, w_down):
            h = jax.nn.silu(x @ w_gate.T) * (x @ w_up.T)
            return h @ w_down.T
        key = jax.random.key(seed)
        ks = jax.random.split(key, 8)
        return {'hidden_states': jax.random.normal(ks[0], (B, S, HID), dtype=jnp.float32), 'wg': jax.random.normal(ks[1], (NUM_EXPERTS, HID), dtype=jnp.float32) * SCALE, 'sh_gate': jax.random.normal(ks[2], (FF, HID), dtype=jnp.float32) * SCALE, 'sh_up': jax.random.normal(ks[3], (FF, HID), dtype=jnp.float32) * SCALE, 'sh_down': jax.random.normal(ks[4], (HID, FF), dtype=jnp.float32) * SCALE, 'ex_gate': jax.random.normal(ks[5], (NUM_EXPERTS, FF, HID), dtype=jnp.float32) * SCALE, 'ex_up': jax.random.normal(ks[6], (NUM_EXPERTS, FF, HID), dtype=jnp.float32) * SCALE, 'ex_down': jax.random.normal(ks[7], (NUM_EXPERTS, HID, FF), dtype=jnp.float32) * SCALE}
    _L0_ffn_in = _L0_ffn_setup()
    _L0_c = _w((lambda *s: np.random.randn(*s).astype(np.float32) * 0.05)(2, 256))
    _L0_wmod = _w((lambda *s: np.random.randn(*s).astype(np.float32) * 0.05)(256, 6 * 256) * 256 ** (-0.5))
    _d = {'L0_attn_x': _L0_attn_in['x'], 'L0_attn_slope_rate': _L0_attn_in['slope_rate'], 'L0_attn_W_qkvu': _L0_attn_in['W_qkvu'], 'L0_attn_W_out': _L0_attn_in['W_out'], 'L0_ffn_wg': _L0_ffn_in['wg'], 'L0_ffn_sh_gate': _L0_ffn_in['sh_gate'], 'L0_ffn_sh_up': _L0_ffn_in['sh_up'], 'L0_ffn_sh_down': _L0_ffn_in['sh_down'], 'L0_ffn_ex_gate': _L0_ffn_in['ex_gate'], 'L0_ffn_ex_up': _L0_ffn_in['ex_up'], 'L0_ffn_ex_down': _L0_ffn_in['ex_down'], 'L0_c': _L0_c, 'L0_wmod': _L0_wmod}
    _x0 = _d['L0_attn_x']
    _d['L0_attn_x'] = jax.random.normal(jax.random.fold_in(jax.random.key(seed), 1), (2, 1024, 256), dtype=_x0.dtype)
    del _x0
    return _d

def reference(L0_attn_x, L0_attn_slope_rate, L0_attn_W_qkvu, L0_attn_W_out, L0_ffn_wg, L0_ffn_sh_gate, L0_ffn_sh_up, L0_ffn_sh_down, L0_ffn_ex_gate, L0_ffn_ex_up, L0_ffn_ex_down, L0_c, L0_wmod):

    def _L0_attn_ref(x, slope_rate, W_qkvu, W_out):
        import jax, jax.numpy as jnp
        import numpy as np
        BLOCK = 32
        EPS = 1e-06

        def _silu(x):
            return x * jax.nn.sigmoid(x)
        b, n, embed_dim = x.shape
        h = slope_rate.shape[0]
        hidden_dim = W_qkvu.shape[0] // 4
        d = hidden_dim // h
        NB = n // BLOCK
        qkvu = x @ W_qkvu.T
        q, k, v, u = jnp.split(qkvu, 4, axis=-1)

        def to_heads(t):
            return t.reshape(b, n, h, d).transpose(0, 2, 1, 3)
        q = _silu(to_heads(q))
        k = _silu(to_heads(k))
        v = to_heads(v)
        s = slope_rate
        arr = jnp.arange(1, BLOCK + 1, dtype=x.dtype)
        q_decay = jnp.exp(-s * arr[:, None])
        k_decay = jnp.exp(-s * (BLOCK - arr[:, None]))
        idx = arr[:, None] - arr[None, :]
        diag_decay = jnp.exp(jnp.where(idx >= 0, -s * idx, -jnp.inf))
        block_decay = jnp.exp(-s * BLOCK)

        def blk(t):
            return t.reshape(b, h, NB, BLOCK, d).transpose(2, 0, 1, 3, 4)
        qb, kb, vb = (blk(q), blk(k), blk(v))

        def step(kv, inp):
            qi, ki, vi = inp
            qkv_none_diag = jnp.einsum('bhmd,bhde->bhme', qi * q_decay, kv)
            qk = jnp.einsum('bhmd,bhsd->bhms', qi, ki) * diag_decay
            qkv_diag = jnp.einsum('bhms,bhse->bhme', qk, vi)
            kv_new = block_decay * kv + jnp.einsum('bhsd,bhse->bhde', ki * k_decay, vi)
            return (kv_new, qkv_none_diag + qkv_diag)
        kv0 = jnp.zeros((b, h, d, d), dtype=jnp.float32)
        _, outs = jax.lax.scan(step, kv0, (qb, kb, vb))
        o = outs.transpose(1, 2, 0, 3, 4).reshape(b, h, n, d)
        o = o.transpose(0, 2, 1, 3).reshape(b, n, hidden_dim)
        o = o * jax.lax.rsqrt(jnp.mean(o * o, axis=-1, keepdims=True) + EPS)
        o = u * o
        return o @ W_out.T

    def _L0_ffn_ref(hidden_states, wg, sh_gate, sh_up, sh_down, ex_gate, ex_up, ex_down):
        import jax, jax.numpy as jnp
        import numpy as np
        NUM_EXPERTS = 8
        TOP_K = 2
        HID = 256
        FF = 512
        B, S = (2, 128)
        SCALE = 0.02

        def _gated_mlp(x, w_gate, w_up, w_down):
            h = jax.nn.silu(x @ w_gate.T) * (x @ w_up.T)
            return h @ w_down.T
        bsz, seq, dim = hidden_states.shape
        x = hidden_states.reshape(-1, dim)
        shared_out = _gated_mlp(x, sh_gate, sh_up, sh_down)
        logits = x.astype(jnp.float32) @ wg.T
        probs = jax.nn.softmax(logits, axis=-1)
        top_w, top_idx = jax.lax.top_k(probs, TOP_K)
        top_w = top_w / jnp.sum(top_w, axis=-1, keepdims=True)
        top_w = top_w.astype(hidden_states.dtype)
        comb = jnp.sum(jax.nn.one_hot(top_idx, NUM_EXPERTS, dtype=top_w.dtype) * top_w[..., None], axis=1)
        out = jnp.zeros_like(x)
        for e in range(NUM_EXPERTS):
            h = jax.nn.silu(x @ ex_gate[e].T) * (x @ ex_up[e].T)
            out = out + h @ ex_down[e].T * comb[:, e:e + 1]
        return (out + shared_out).reshape(bsz, seq, dim)
    x = L0_attn_x
    mod = (_silu(L0_c) @ L0_wmod).reshape(L0_c.shape[0], 6, 1, -1)
    sa, ca, ga, sb, cb, gb = (mod[:, 0], mod[:, 1], mod[:, 2], mod[:, 3], mod[:, 4], mod[:, 5])
    ga = (2 * (ga >= 0) - 1) * jnp.maximum(jnp.abs(ga), 0.25)
    gb = (2 * (gb >= 0) - 1) * jnp.maximum(jnp.abs(gb), 0.25)
    h = _layernorm(x, axis=-1) * (1 + ca) + sa
    x = x + ga * _L0_attn_ref(h, L0_attn_slope_rate, L0_attn_W_qkvu, L0_attn_W_out)
    h = _layernorm(x, axis=-1) * (1 + cb) + sb
    x = x + gb * _L0_ffn_ref(h, L0_ffn_wg, L0_ffn_sh_gate, L0_ffn_sh_up, L0_ffn_sh_down, L0_ffn_ex_gate, L0_ffn_ex_up, L0_ffn_ex_down)
    return x

_drawn_inputs = setup_inputs


def setup_inputs(seed=0):
    import zlib

    import numpy as np

    out = dict(_drawn_inputs(seed))
    spreads = {}
    factors = {'L0_ffn_wg': 8.0,
     'L0_ffn_sh_gate': 8.0,
     'L0_ffn_sh_up': 8.0,
     'L0_ffn_sh_down': 8.0,
     'L0_ffn_ex_gate': 8.0,
     'L0_ffn_ex_up': 8.0,
     'L0_ffn_ex_down': 8.0}
    for name, (base, spread) in spreads.items():
        noise = np.random.default_rng([zlib.crc32(name.encode()), seed]).standard_normal(out[name].shape)
        drawn = base * np.exp(spread * noise) if base else spread * noise
        out[name] = jnp.asarray(drawn.astype(out[name].dtype))
    for name, factor in factors.items():
        out[name] = (out[name] * factor).astype(out[name].dtype)
    return out
```

```python
import numpy as np
from contextlib import ExitStack

import concourse.bass as bass
from concourse import mybir

P = 128
B, S, D = 2, 1024, 256
KD = D // P
NH, DH = 16, 16
HP = P // DH
NT = B * S // P
NC = S // P
NE, FF, NSH = 8, 512, 8
KF = FF // P
TOP = 2
PIECE = KD * FF
NPIECE = 3
SLOT = 2 * NPIECE * PIECE
NG = TOP * NT + NE - 1
ROW = 2 * D + 4
ACC = B * S + P
LN_EPS, RMS_EPS = 1e-5, 1e-6
QSTRIDE = 4
RT_PICKED, RT_DONE = 17, 35


def build(nc, t):
    f32, bf16, i32, u32 = mybir.dt.float32, mybir.dt.bfloat16, mybir.dt.int32, mybir.dt.uint32
    ALU, ACT, AX = mybir.AluOpType, mybir.ActivationFunctionType, mybir.AxisListType
    ctx = ExitStack()
    with ctx:
        def sb(name, shape, dt=f32):
            return ctx.enter_context(nc.sbuf_tensor(name, shape, dt))

        def sem(name):
            return ctx.enter_context(nc.semaphore(name))

        wx = sb("wx", [P, (NE + 1) * SLOT], bf16)
        att = wx[:, 0:NE * SLOT].bitcast(f32)
        at = [0]

        def in_att(n):
            at[0] += n
            return att[:, at[0] - n:at[0]]

        qT = in_att(KD * B * S).rearrange("p (k n) -> p k n", k=KD)
        uT = in_att(KD * B * S).rearrange("p (k n) -> p k n", k=KD)
        khT = in_att(2 * KD * B * S).rearrange("p (k n) -> p k n", k=2 * KD)
        kT, hT = khT[:, 0:KD], khT[:, KD:2 * KD]
        qbd = [in_att(KD * HP * P).rearrange("p (k h n) -> p k h n", k=KD, h=HP) for _ in range(2)]
        vbd = [in_att(NH * P).rearrange("p (h n) -> p h n", h=NH) for _ in range(2)]
        xres = sb("xres", [P, NT, D])
        h2s = sb("h2s", [P, NT, ROW], bf16)
        wqkvu = sb("wqkvu", [P, KD, 4 * D])
        kh = [wqkvu[:, b, 0:2 * D].rearrange("p (k n) -> p k n", n=P) for b in range(2)]
        woutg = sb("woutg", [P, B, KD, D])
        wg = sb("wg", [P, KD, P])
        ident = sb("ident", [P, P])
        identb = sb("identb", [P, P], bf16)
        ones = sb("ones", [P, P])
        cT = sb("cT", [P, KD, B])
        cs = sb("cs", [P, KD, B])
        modc = sb("modc", [P, 2, KD, B])
        modr = sb("modr", [P, B, 4, D])
        slr = sb("slr", [P, NH])
        slc = sb("slc", [P, KD])
        headm = sb("headm", [P, KD, P])
        dq = sb("dq", [P, KD, P])
        dk = sb("dk", [P, NH, DH])
        nsl = sb("nsl", [P, NH + KD])
        npos = sb("npos", [P, 1])
        bdec = sb("bdec", [P, KD])
        st1 = sb("st1", [P, NT, 6])
        mv1 = sb("mv1", [P, NT, 2])
        rs1 = sb("rs1", [P, 3, NT])
        st2 = sb("st2", [P, 2, 6])
        mv2 = sb("mv2", [P, 2, 2])
        rs2 = sb("rs2", [P, 2, 6])
        logit = sb("logit", [P, NT, NE])
        wmod = h2s[:].rearrange("p t d -> p (t d)").bitcast(f32)[:, 0:KD * 6 * D].rearrange("p (k n) -> p k n", k=KD)
        epst = sb("epst", [P, 2])
        tmp = sb("tmp", [P, 11 * 2 * D + D])
        used = [0]

        def carve(n, dt=f32):
            words = n if dt == f32 else n // 2
            used[0] += words
            return tmp[:, used[0] - words:used[0]] if dt == f32 else tmp[:, used[0] - words:used[0]].bitcast(dt)

        def two(n=D):
            return carve(2 * n).rearrange("p (a n) -> p a n", a=2)

        def two_t():
            return carve(2 * D).rearrange("p (a k n) -> p a k n", a=2, k=KD)

        xn, kdec, vtok, xn2, h2 = two(), two(), two(), two(), two()
        qdec, oT, sq, yT, h2T, kv = two_t(), two_t(), two_t(), two_t(), two_t(), two_t()
        um = carve(D).rearrange("p (k n) -> p k n", k=KD)
        used[0] = 0
        xg = [carve(ROW, bf16) for _ in range(2)]
        xT = [carve(2 * D, bf16) for _ in range(2)]
        sg = [carve(FF) for _ in range(2)]
        hf = [carve(FF) for _ in range(2)]
        hs = [carve(2 * FF, bf16) for _ in range(2)]
        hsT = [carve(2 * FF, bf16) for _ in range(2)]
        yb = [carve(D) for _ in range(2)]
        back = [wx[:, 0:NT * 2 * D].bitcast(f32)[:, 2 * i * D:2 * (i + 1) * D].rearrange("p (t d) -> p t d", t=2)
                for i in range(NT // 2)]
        score = sb("score", [P, 2 * NH * P])
        decay = score[:, 0:NH * P].rearrange("p (h n) -> p h n", h=NH)
        sd = score[:, NH * P:2 * NH * P].rearrange("p (j h n) -> p j h n", j=4, h=4)
        stage = [score[:, q * PIECE:(q + 1) * PIECE] for q in range(NPIECE)]
        early_stage = qT.rearrange("p k n -> p (k n)")
        rt = wqkvu[:].rearrange("p k n -> p (k n)")
        rused = [0]

        def route(n, dt=f32):
            rused[0] += n
            a = rt[:, rused[0] - n:rused[0]]
            return a if dt == f32 else a.bitcast(dt)

        def route3(dt=f32):
            return route(NT * NE, dt).rearrange("p (t e) -> p t e", t=NT)

        lm, ex, pr, eq, pick, m1, m2, pr2, pos = (route3() for _ in range(9))
        mx, sm, rsm, p1, f1, p2, f2, den, rden = (route(NT) for _ in range(9))
        pool_w2 = route(2 * NT).rearrange("p (t a) -> p t a", t=NT)
        idx1, idx2 = route(NT, u32), route(NT, u32)
        picked = route(NT * NE // 2).bitcast(bf16)
        tiles_i, tiles_s = route(NE, i32), route(NE, i32)
        tiles_f, tiles_end, base = route(NE), route(NE), route(NE)
        gej = route(NG * NE).rearrange("p (j e) -> p j e", j=NG)
        slot_f = route(NG)
        slot_of = sb("slot_of", [1, NT + NG], i32)
        metaw = sb("metaw", [P, NG])
        zer = sb("zer", [P, 2])
        dst_i = sb("dst_i", [P, NG], u32)
        ustrict = sb("ustrict", [P, P], bf16)
        onesb = sb("onesb", [P, P], bf16)
        rev = sb("rev", [P, NE])
        tok1 = sb("tok1", [P, NT])
        dummy = sb("spare", [P, 1])
        jt = sb("jt", [1, NG])
        cbc = h2s[:].rearrange("p t d -> p (t d)").bitcast(f32)[:, KD * 6 * D:KD * (6 * D + B * P)].rearrange(
            "p (k b n) -> p k b n", k=KD, b=B)
        wout = h2s[:].rearrange("p t d -> p (t d)").bitcast(f32)[:, KD * (6 * D + B * P):KD * (7 * D + B * P)].rearrange(
            "p (k n) -> p k n", k=KD)

        def diag_ap(t_, k):
            flat = t_.rearrange("p h n -> p (h n)")
            n0 = k * HP * P
            part = flat[:, n0:n0 + HP * P]
            return bass.AP(part.tensor, part.offset, [part.ap[0], [P + DH, HP], [1, DH]])

        ps = ctx.enter_context(nc.psum_tensor("ps", [P, 8, 512], f32))

        tabs = h2T.rearrange("p a k n -> p (a k n)")
        lag, causal, posn = tabs[:, 0:P], tabs[:, P:2 * P], tabs[:, 2 * P:3 * P + 1]
        early = sd.rearrange("p j h n -> p (j h n)").rearrange("p (a b c n) -> p a b c n", a=2, b=B, c=2)
        sgn, mag = early[:, 0], early[:, 1]

        def half(bank, at, n=P):
            return ps[:, bank, at:at + n]

        names = ("x w c mod z0 z1 lz v0 a0 v1 a1 v2 p2 v3 mc mr vm va st mv sdv rs nm xn tp he "
                 "qkp kh qkr qe ue "
                 "vp vr vb kp kd qd s sdm sg oe u umm kvv in_ sq y a r0 r x1 bs mv2 sd2 rc2 nm2 xn2 ha h h2 hi lo "
                 "tb hte lg le out cc ccb ge "
                 "cva fill ws wh wl cvl cvh rt rex rp sc1 sc2 mt2 "
                 "xt xe g u2 sl hh hi2 lo2 ht he2 yd ye acc fa meta0").split()
        s = {n: sem("s_" + n) for n in names}
        s_xg = [sem(f"s_xg{i}") for i in range(2)]
        s_st = [sem(f"s_st{i}") for i in range(2)]
        s_ld = [sem(f"s_ld{q}") for q in range(NPIECE)]
        s_fl = [sem(f"s_fl{i}") for i in range(NT // 2)]
        s_qb = [sem(f"s_qb{i}") for i in range(2)]
        block = ctx.enter_context(nc.Block())

        def late(c, b, k):
            if k == 1:
                c, b = (c - 1, 1) if b == 0 else (c, 0)
            elif k == 2:
                c = c - 1
            if isinstance(c, int) and not (0 <= c < NC):
                return None
            return 2 * c + b, c + NC * b, b

        def steps(eng, step):
            for c in range(2):
                for b in range(2):
                    step(c, b)
            with eng.Fori(2, NC) as c:
                for b in range(2):
                    step(c, b)
            for b in range(2):
                step(NC, b)

        def wait(eng, name, value):
            if not isinstance(value, int) or value > 0:
                eng.wait_ge(s[name] if isinstance(name, str) else name, value)

        def loop(eng, count, body):
            body(0)
            with eng.Fori(1, count) as i:
                body(i)

        def cols(tile):
            return bass.ts(tile, P)

        NF = NT + NG
        LO, MID, HI = 6, NT, NT + 4
        LAST = NF - (NF - HI) % 2

        def attention_over(e):
            e.wait_ge(s["le"], NT)
            e.wait_ge(s["lo"], NT)
            e.wait_ge(s["kvv"], KD * NT)

        def pipeline(eng, step, between=None):
            for f in range(-1, LO):
                step(f, f % 2)
                if between:
                    between(f)
            with eng.Fori(LO, MID, 2) as f:
                for j in range(2):
                    step(f + j, j, False)
            for f in range(MID, HI):
                step(f, f % 2)
            with eng.Fori(HI, LAST, 2) as f:
                for j in range(2):
                    step(f + j, j, True)
            for f in range(LAST, NF + 3):
                step(f, f % 2)

        def tile_at(f, k, p, routed):
            if isinstance(f, int):
                g = f - k
                return (g, g % 2, g >= NT) if 0 <= g < NF else None
            return f - k, (p - k) % 2, routed

        def place(g, p):
            c = (g - p) // 2
            return c + NC * p

        def weights(part, low):
            return low * NPIECE * PIECE + part * PIECE

        @block.sync
        def _(e):
            xin = t["x"].rearrange("(t p) d -> p t d", p=P)
            for g in range(4):
                e.dma_start(xres[:, 4 * g:4 * g + 4, :], xin[:, 4 * g:4 * g + 4, :]).then_inc(s["x"], 16)
            for q in range(NPIECE):
                e.dma_start(early_stage[:, q * PIECE:(q + 1) * PIECE], t["wexp"][NSH, :, q, :]).then_inc(s["ws"], 16)
            e.wait_ge(s["z0"], 2)
            zeros = qbd[0].rearrange("p k h n -> p (k h n)").bitcast(u32)
            rows = t["xg"].rearrange("(j p) d -> p j d", p=P)
            per = KD * HP * P * 2 // ROW
            nfill = 0
            for j in range(0, NG, per):
                m = min(per, NG - j)
                e.dma_start(rows[:, j:j + m, :], zeros[:, 0:m * ROW // 2].rearrange("p (j d) -> p j d", j=m)).then_inc(s["fill"], 16)
                nfill += 16
            e.dma_start(t["acc"][B * S:ACC, :], zeros[:, 0:D].bitcast(f32)).then_inc(s["fill"], 16)
            e.wait_ge(s["fill"], nfill + 16)
            def step(c, b):
                me = late(c, b, 0)
                if me is None:
                    return
                n, tile, _ = me
                if isinstance(c, int) and n == 0:
                    e.wait_ge(s["qe"], 2 * KD * NT // QSTRIDE)
                    e.wait_ge(s["z0"], 2)
                wait(e, "sg", 4 * n - 4)
                for h in range(HP):
                    rows = slice(h * DH, (h + 1) * DH)
                    e.dma_start(qbd[b][rows, :, h, :], qT[rows, :, cols(tile)]).then_inc(s_qb[b], 16)
            steps(e, step)
            attention_over(e)

            def load_expert(x):
                for q in range(NPIECE):
                    if x:
                        e.wait_ge(s["cvl"], NPIECE * x)
                    e.dma_start(stage[q], t["wexp"][x, :, q, :]).then_inc(s_ld[q], 16)

            def load_rows(g, p, routed):
                if routed:
                    row = g - NT if isinstance(g, int) else e.snap(g - NT)
                    if isinstance(g, int) and g < NT + 2:
                        e.wait_ge(s["xe"], g - 1)
                    else:
                        wait(e, "meta0", g - 2 - NT + 1)
                    e.dma_start(xg[p].bitcast(u32).unsqueeze(1),
                                t["xg"].rearrange("(j p) d -> p j d", p=P)[:, bass.ds(row, 1), :]).then_inc(s_xg[p], 16)
                else:
                    wait(e, "xe", g - 1)
                    e.dma_start(xg[p][:, 0:2 * D].unsqueeze(1), h2s[:, bass.ds(place(g, p), 1), 0:2 * D]).then_inc(s_xg[p], 16)

            def store_shared(g, p):
                wait(e, "ye", g + 1)
                e.dma_start(t["acc"][0:B * S, :].rearrange("(t p) d -> p t d", p=P)[:, bass.ds(place(g, p), 1), :],
                            yb[p].unsqueeze(1)).then_inc(s_st[p], 16)

            load_expert(0)
            load_rows(0, 0, False)
            load_rows(1, 1, False)
            for x in range(NE):
                for g in range(2 * x + 2, 2 * x + 4):
                    if g < NT:
                        load_rows(g, g % 2, False)
                for g in range(2 * x - 4, 2 * x - 2):
                    if g >= 0:
                        store_shared(g, g % 2)
                if x + 1 < NE:
                    load_expert(x + 1)
            e.wait_ge(s["sc1"], 16 * NT)
            e.wait_ge(s["sc2"], 16 * NT)
            for g in range(NT, NT + 4):
                load_rows(g, g % 2, True)
                store_shared(g - 4, g % 2)
            end = NF - (NF - NT) % 2
            with e.Fori(NT + 4, end, 2) as g:
                for j in range(2):
                    load_rows(g + j, j, True)
            for g in range(end, NF):
                load_rows(g, g % 2, True)
            e.wait_ge(s["acc"], 16 * NG)
            e.wait_ge(s["yd"], NF)
            accr = t["acc"][0:B * S, :].rearrange("(t p) d -> p t d", p=P)
            outr = t["out"].rearrange("(t p) d -> p t d", p=P)
            for i in range(NT // 2):
                e.dma_start(back[i], accr[:, 2 * i:2 * i + 2, :]).then_inc(s_fl[i], 16)
            for i in range(NT // 2):
                e.wait_ge(s["fa"], 2 * i + 2)
                e.dma_start(outr[:, 2 * i:2 * i + 2, :], back[i]).then_inc(s["out"], 16)
            e.wait_ge(s["out"], 16 * (NT // 2))

        @block.gpsimd
        def _(e):
            for b in range(2):
                e.memset(qbd[b], 0.0).then_inc(s["z0"], 1)
            for b in range(2):
                e.memset(vbd[b], 0.0).then_inc(s["z1"], 1)
            e.memset(kv, 0.0).then_inc(s["z1"], 1)
            for q in range(NPIECE):
                e.wait_ge(s["wh"], q + 1)
                at_ = NSH * SLOT
                e.tensor_tensor(wx[:, at_ + weights(q, 1):at_ + weights(q, 1) + PIECE],
                                early_stage[:, q * PIECE:(q + 1) * PIECE],
                                wx[:, at_ + weights(q, 0):at_ + weights(q, 0) + PIECE], ALU.subtract).then_inc(s["wl"], 1)

            def step(c, b):
                if (me := late(c, b, 0)) is not None:
                    n, tile, _ = me
                    if isinstance(c, int) and n == 0:
                        e.wait_ge(s["qe"], 2 * KD * NT // QSTRIDE)
                        e.wait_ge(s["ue"], KD * NT // QSTRIDE)
                        e.wait_ge(s["p2"], 1)
                    wait(e, "sg", 4 * n - 4)
                    e.tensor_copy(kh[b], khT[:, :, cols(tile)]).then_inc(s["kh"], 1)
                    e.tensor_tensor(qdec[:, b], qT[:, :, cols(tile)], dq[:, :, :], ALU.mult).then_inc(s["qd"], 1)
                if (me := late(c, b, 1)) is not None:
                    n, tile, p = me
                    wait(e, "oe", n + 1)
                    if isinstance(c, int) and n == 0:
                        e.wait_ge(s["ue"], KD * NT // QSTRIDE)
                    wait(e, "a", n - 1)
                    e.tensor_tensor(yT[:, p], oT[:, p], uT[:, :, cols(tile)], ALU.mult).then_inc(s["y"], 1)
                if (me := late(c, b, 2)) is not None:
                    n, tile, p = me
                    wait(e, "xn2", n + 1)
                    e.tensor_tensor(xn2[:, p], xn2[:, p], modr[:, p, 2], ALU.mult).then_inc(s["ha"], 1)
                    wait(e, "ha", n + 1)
                    wait(e, "tb", n - 1)
                    wait(e, "hi", n - 1)
                    e.tensor_tensor(h2[:, p], xn2[:, p], modr[:, p, 1], ALU.add).then_inc(s["h2"], 1)
                    wait(e, "hi", n + 1)
                    wait(e, "h2", n + 1)
                    e.tensor_tensor(h2s[:, bass.ds(tile, 1), D:2 * D], h2[:, p:p + 1, :],
                                    h2s[:, bass.ds(tile, 1), 0:D], ALU.subtract).then_inc(s["lo"], 1)
            steps(e, step)

            attention_over(e)
            e.memset(dst_i[:], 0)

            def split_low(x):
                q = NPIECE - 1
                e.wait_ge(s["cvh"], NPIECE * (x + 1))
                at_ = x * SLOT
                e.tensor_tensor(wx[:, at_ + weights(q, 1):at_ + weights(q, 1) + PIECE], stage[q],
                                wx[:, at_ + weights(q, 0):at_ + weights(q, 0) + PIECE], ALU.subtract).then_inc(s["cvl"], 1)

            def dispatch(which, tiles):
                for n in tiles:
                    e.indirect_dma_start(t["xg"], bass.IndirectOffsetOnAxis(ap=(idx1, idx2)[which][:, n:n + 1], axis=0),
                                         h2s[:, n, :].bitcast(u32), None).then_inc(s[("sc1", "sc2")[which]], 16)

            for x in range(2):
                split_low(x)
            e.wait_ge(s["rt"], RT_DONE)
            split_low(2)
            dispatch(0, range(0, 6))
            split_low(3)
            dispatch(0, range(6, 12))
            split_low(4)
            dispatch(0, range(12, NT))
            split_low(5)
            e.wait_ge(s["sc1"], 16 * NT)
            e.tensor_copy(h2s[:, :, 2 * D:ROW].bitcast(f32), pool_w2).then_inc(s["mt2"], 1)
            e.wait_ge(s["mt2"], 1)
            dispatch(1, range(0, 6))
            split_low(6)
            dispatch(1, range(6, NT))
            split_low(7)
            e.wait_ge(s_st[0], 16 * NT // 2)
            e.wait_ge(s_st[1], 16 * NT // 2)
            for g in range(NG):
                e.wait_ge(s["meta0"], g + 1)
                e.wait_ge(s["ye"], NT + g + 1)
                if g:
                    e.wait_ge(s["acc"], 16 * g)
                e.indirect_dma_start(t["acc"], bass.IndirectOffsetOnAxis(ap=dst_i[:, g:g + 1], axis=0),
                                     yb[g % 2], None, compute_op=ALU.add).then_inc(s["acc"], 16)

        @block.scalar
        def _(e):
            for dst, name in ((cT, "cT"), (slr, "slr"), (slc, "slc"), (lag, "lag"), (causal, "causal"),
                              (posn, "posn"), (headm, "headm"), (ident, "ident"),
                              (ones, "ones")):
                e.dma_start(dst if name in ("lag", "causal", "posn", "wout") else dst[:], t[name]).then_inc(s["c"], 16)
            NCONST = 144
            e.dma_start(wmod[:], t["wmod"]).then_inc(s["mod"], 16)
            for dst, name in ((wqkvu, "wqkvu"), (wout, "wout")):
                e.dma_start(dst if name in ("lag", "causal", "posn", "wout") else dst[:], t[name]).then_inc(s["w"], 16)
            e.dma_start(wg[:], t["wg"]).then_inc(s["w"], 16)
            for dst, name in ((rev, "rev"), (tok1, "tok1"),
                              (dummy, "dummy"), (jt, "jt")):
                e.dma_start(dst[:], t[name]).then_inc(s["cc"], 16)
            e.wait_ge(s["ws"], 16 * NPIECE)
            for q in range(NPIECE):
                at_ = NSH * SLOT
                e.activation(wx[:, at_ + weights(q, 0):at_ + weights(q, 0) + PIECE],
                             early_stage[:, q * PIECE:(q + 1) * PIECE], ACT.Copy).then_inc(s["wh"], 1)
            e.wait_ge(s["c"], NCONST)
            e.activation(cs[:], cT[:], ACT.Silu).then_inc(s["a0"], 1)
            e.wait_ge(s["v0"], 6)
            e.wait_ge(s["v1"], 2)
            for h in range(NH):
                e.activation(decay[:, h, :], lag[:, :], ACT.Exp, scale=nsl[:, h:h + 1]).then_inc(s["a1"], 1)
            for k in range(KD):
                e.activation(dq[:, k, :], posn[:, 0:P], ACT.Exp, scale=nsl[:, NH + k:NH + k + 1])
                e.activation(bdec[:, k:k + 1], posn[:, P - 1:P], ACT.Exp, scale=nsl[:, NH + k:NH + k + 1]).then_inc(s["a1"], 1)
            e.activation(dk[:, :, :], slr[:, :].unsqueeze(2).to_broadcast([P, NH, DH]), ACT.Exp,
                         scale=npos[:, 0:1]).then_inc(s["p2"], 1)
            e.wait_ge(s["mv"], NT)
            e.activation(rs1[:, 0, :], mv1[:, :, 1], ACT.Sqrt, bias=epst[:, 0:1]).then_inc(s["sdv"], 1)
            e.wait_ge(s["mc"], 1)
            for b in range(B):
                with e.Fori(0, NC // 2) as i:
                    for j in range(2):
                        n = 2 * i + j + NC * b
                        e.wait_ge(s["tp"], n + 1)
                        for k in range(KD):
                            ins = e.activation(hT[:, k, cols(n)], half(j, k * P), ACT.Identity,
                                               scale=modc[:, 1, k, b:b + 1], bias=modc[:, 0, k, b:b + 1])
                        ins.then_inc(s["he"], 1)
            e.wait_ge(s["wl"], NPIECE)
            with e.Fori(0, NT // QSTRIDE) as g:
                for j in range(2 * KD):
                    e.wait_ge(s["qkp"], 3 * KD * g + j + 1)
                    dst = (qT, kT)[j // KD]
                    e.activation(dst[:, j % KD, bass.ts(g, QSTRIDE * P)], ps[:, j, :], ACT.Silu).then_inc(s["qe"], 1)

            e.wait_ge(s["z1"], 3)

            def step(c, b):
                if (me := late(c, b, 1)) is not None:
                    n, tile, p = me
                    wait(e, "sg", 4 * n + 4)
                    wait(e, "y", n - 1)
                    wait(e, "sq", n - 1)
                    e.activation(oT[:, p], half(5, 0, D).rearrange("p (k n) -> p k n", k=KD), ACT.Copy).then_inc(s["oe"], 1)
                if (me := late(c, b, 0)) is not None:
                    n, tile, p = me
                    wait(e, "vp", n + 1)
                    wait(e, "sg", 4 * n - 4)
                    diag = vbd[p].rearrange("p h n -> p (h n)")[:, 0:NH * P].rearrange(
                        "p (k r) -> p k r", k=KD)
                    e.activation(vtok[:, p, :], half(0, 0, D), ACT.Copy).then_inc(s["vr"], 1)
                    for k in range(KD):
                        dst = diag_ap(vbd[p], k)
                        e.activation(dst, half(0, k * P).rearrange("p (h n) -> p h n", h=HP), ACT.Copy).then_inc(s["vr"], 1)
                if (me := late(c, b, 1)) is not None:
                    n, tile, p = me
                    wait(e, "oe", n + 1)
                    wait(e, "a", n - 1)
                    e.activation(sq[:, p], oT[:, p], ACT.Square).then_inc(s["sq"], 1)
                    wait(e, "a", n + 1)
                    e.activation(rs2[:, p, 0:1], ps[:, 7, D:D + 1], ACT.Sqrt, scale=1.0 / D, bias=epst[:, 1:2]).then_inc(s["r0"], 1)
                if (me := late(c, b, 2)) is not None:
                    n, tile, p = me
                    wait(e, "h2", n + 1)
                    e.activation(h2s[:, bass.ds(tile, 1), 0:D], h2[:, p:p + 1, :], ACT.Copy).then_inc(s["hi"], 1)
                if (me := late(c, b, 1)) is not None:
                    n, tile, p = me
                    wait(e, "mv2", n + 1)
                    e.activation(rs2[:, p, 2:3], mv2[:, p, 1:2], ACT.Sqrt, bias=epst[:, 0:1]).then_inc(s["sd2"], 1)
                if (me := late(c, b, 2)) is not None:
                    n, tile, p = me
                    wait(e, "tb", n + 1)
                    wait(e, "lg", n - 1)
                    e.activation(h2T[:, p], half(4, 0, D).rearrange("p (k n) -> p k n", k=KD), ACT.Copy).then_inc(s["hte"], 1)
                    wait(e, "lg", n + 1)
                    e.activation(logit[:, bass.ds(tile, 1), :], half(4, D, NE).unsqueeze(1), ACT.Copy).then_inc(s["le"], 1)
            steps(e, step)

            attention_over(e)
            e.wait_ge(s["rt"], 2)
            e.activation(ex, lm, ACT.Exp).then_inc(s["rex"], 1)

            def finish(g, p, routed):
                wait(e, "yd", g + 1)
                if routed:
                    if isinstance(g, int) and g < NT + 2:
                        e.wait_ge(s_st[p], 16 * NT // 2)
                    else:
                        wait(e, "acc", 16 * (g - 2 - NT + 1))
                    e.activation(yb[p].unsqueeze(1), ps[:, 6 + p, 0:D].unsqueeze(1), ACT.Copy, scale=metaw[:, bass.ds(g - NT, 1)]).then_inc(s["ye"], 1)
                else:
                    wait(e, s_st[p], 8 * (g - p))
                    e.activation(yb[p], ps[:, 6 + p, 0:D], ACT.Copy).then_inc(s["ye"], 1)

            def split_high(x):
                for q in range(NPIECE - 1):
                    e.wait_ge(s_ld[q], 16 * (x + 1)) if isinstance(x, int) else e.wait_ge(s_ld[q], 16 * x + 16)
                    e.activation(wx[:, bass.ds(x * SLOT + weights(q, 0), PIECE)], stage[q], ACT.Copy).then_inc(s["cva"], 1)

            def step(f, p, routed=None):
                if (y := tile_at(f, 3, p, routed)):
                    finish(*y)
                if (y := tile_at(f, 2, p, routed)):
                    g, q, _ = y
                    wait(e, "ht", g + 1)
                    wait(e, "yd", g - 1)
                    e.activation(hsT[q], ps[:, 5, :].bitcast(bf16), ACT.Copy).then_inc(s["he2"], 1)
                if (y := tile_at(f, 0, p, routed)):
                    g, q, _ = y
                    wait(e, "g", g + 1)
                    wait(e, "hh", g - 1)
                    e.activation(sg[q], ps[:, 1 + 2 * q, :], ACT.Silu).then_inc(s["sl"], 1)
                    if q == 0 and (g < NT if isinstance(g, int) else not routed):
                        split_high(g // 2)
                    wait(e, "hh", g + 1)
                    wait(e, "ht", g - 1)
                    e.activation(hs[q][:, 0:FF], hf[q], ACT.Copy).then_inc(s["hi2"], 1)
            pipeline(e, step)

        @block.vector
        def _(e):
            e.memset(epst[:, 0:1], LN_EPS).then_inc(s["v1"], 1)
            e.memset(epst[:, 1:2], RMS_EPS).then_inc(s["v1"], 1)
            e.wait_ge(s["c"], 144)
            e.tensor_copy(identb[:], ident[:]).then_inc(s["v0"], 1)
            e.tensor_copy(onesb[:], ones[:]).then_inc(s["v0"], 1)
            e.tensor_scalar(ustrict[:], lag, 1.0, None, ALU.is_ge).then_inc(s["v0"], 1)
            e.tensor_scalar(nsl[:, 0:NH], slr[:, :], -1.0, None, ALU.mult).then_inc(s["v0"], 1)
            e.tensor_scalar(nsl[:, NH:NH + KD], slc[:, :], -1.0, None, ALU.mult).then_inc(s["v0"], 1)
            e.tensor_scalar(npos[:, :], posn[:, P:P + 1], -1.0, None, ALU.mult).then_inc(s["v0"], 1)
            e.wait_ge(s["a0"], 1)
            e.tensor_copy(cbc, cs[:].unsqueeze(3).to_broadcast([P, KD, B, P])).then_inc(s["ccb"], 1)
            e.wait_ge(s["x"], 64)
            with e.Fori(0, NT) as i:
                e.bn_stats(st1[:, bass.ds(i, 1), :], xres[:, bass.ds(i, 1), :]).then_inc(s["st"], 1)
            e.wait_ge(s["st"], NT)
            for i in range(NT):
                e.bn_aggr(mv1[:, i, :], st1[:, i, :]).then_inc(s["mv"], 1)
            e.wait_ge(s["sdv"], 1)
            e.reciprocal(rs1[:, 1, :], rs1[:, 0, :]).then_inc(s["rs"], 1)
            e.wait_ge(s["rs"], 1)
            e.scalar_tensor_tensor(out=rs1[:, 2, :], in0=mv1[:, :, 0], scalar=-1.0, in1=rs1[:, 1, :],
                                   op0=ALU.mult, op1=ALU.mult).then_inc(s["nm"], 1)
            e.wait_ge(s["mr"], 1)
            pm = half(6, 0, 2 * KD * B).rearrange("p (a k b) -> p a k b", a=2, k=KD)
            e.tensor_copy(modc[:, 0], pm[:, 0])
            e.tensor_scalar(modc[:, 1], pm[:, 1], 1.0, None, ALU.add).then_inc(s["mc"], 1)
            e.wait_ge(s["nm"], 1)

            def normalise(i):
                for j in range(2):
                    n = 2 * i + j
                    wait(e, "tp", n - 1)
                    e.tensor_scalar(xn[:, j:j + 1, :], xres[:, bass.ds(n, 1), :], rs1[:, 1, bass.ds(n, 1)],
                                    rs1[:, 2, bass.ds(n, 1)], ALU.mult, ALU.add).then_inc(s["xn"], 1)
            loop(e, NT // 2, normalise)
            e.wait_ge(s["mr"], 2)
            for b in range(B):
                src = ps[:, 2 + 2 * b:4 + 2 * b, :].rearrange("p a (c n) -> p (a c) n", c=2)
                e.tensor_copy(modr[:, b, 1:2, :], src[:, 1:2])
                e.tensor_scalar(modr[:, b, 2:3, :], src[:, 2:3], 1.0, None, ALU.add).then_inc(s["vm"], 1)
                for j in (0, 3):
                    e.tensor_scalar(sgn[:, b, j // 3, :], src[:, j], 0.0, 2.0, ALU.is_ge, ALU.mult).then_inc(s["va"], 1)
                    e.wait_ge(s["va"], 2 * b + j // 3 + 1)
                    e.scalar_tensor_tensor(out=mag[:, b, j // 3, :], in0=sgn[:, b, j // 3, :], scalar=-1.0,
                                           in1=src[:, j], op0=ALU.add, op1=ALU.mult).then_inc(s["vb"], 1)
            e.wait_ge(s["vb"], 2 * B)
            e.tensor_scalar(mag, mag, 0.25, None, ALU.max).then_inc(s["vb"], 1)
            e.wait_ge(s["vb"], 2 * B + 1)
            for b in range(B):
                for j in (0, 3):
                    e.scalar_tensor_tensor(out=modr[:, b, j, :], in0=sgn[:, b, j // 3, :], scalar=-1.0,
                                           in1=mag[:, b, j // 3, :], op0=ALU.add, op1=ALU.mult).then_inc(s["vm"], 1)
            e.wait_ge(s["vm"], 3 * B)
            e.wait_ge(s["w"], 48)
            for b in range(B):
                e.tensor_tensor(woutg[:, b], wout, modr[:, b, 0:1, :].to_broadcast([P, KD, D]), ALU.mult).then_inc(s["v3"], 1)
            e.wait_ge(s["a1"], NH)
            e.tensor_tensor(decay, decay, causal[:, :].unsqueeze(1).to_broadcast([P, NH, P]), ALU.mult).then_inc(s["lz"], 1)
            with e.Fori(0, NT // QSTRIDE) as g:
                for k in range(KD):
                    e.wait_ge(s["qkp"], 3 * KD * g + 2 * KD + k + 1)
                    e.tensor_copy(uT[:, k, bass.ts(g, QSTRIDE * P)], ps[:, 2 * KD + k, :]).then_inc(s["ue"], 1)
            e.wait_ge(s["lz"], 1)
            e.wait_ge(s["p2"], 1)
            e.wait_ge(s["z1"], 3)

            def scores(n, j):
                wait(e, "s", 4 * n + j + 1)
                wait(e, "sg", 4 * n + j - 3)
                e.tensor_tensor(sd[:, j], ps[:, 2 + j % 2, :].rearrange("p (h n) -> p h n", h=4),
                                decay[:, 4 * j:4 * j + 4, :], ALU.mult).then_inc(s["sdm"], 1)

            def step(c, b):
                me, pr = late(c, b, 0), late(c, b, 1)
                if me is not None:
                    n, tile, p = me
                    wait(e, "kp", n + 1)
                    wait(e, "sg", 4 * n - 4)
                    e.tensor_tensor(kdec[:, p, :], half(1, 0, D), dk[:].rearrange("p h d -> p (h d)"), ALU.mult).then_inc(s["kd"], 1)
                    scores(n, 0)
                    scores(n, 1)
                if pr is not None:
                    m, mt, q = pr
                    wait(e, "r0", m + 1)
                    e.reciprocal(rs2[:, q, 1:2], rs2[:, q, 0:1]).then_inc(s["r"], 1)
                    wait(e, "r", m + 1)
                    e.scalar_tensor_tensor(out=xres[:, bass.ds(mt, 1), :], in0=half(7, 0, D).unsqueeze(1), scalar=rs2[:, q, 1:2],
                                           in1=xres[:, bass.ds(mt, 1), :], op0=ALU.mult, op1=ALU.add).then_inc(s["x1"], 1)
                if pr is not None:
                    wait(e, "x1", m + 1)
                if me is not None:
                    scores(n, 2)
                if pr is not None:
                    e.bn_stats(st2[:, q, :], xres[:, bass.ds(mt, 1), :]).then_inc(s["bs"], 1)
                    wait(e, "bs", m + 1)
                    wait(e, "nm2", m - 1)
                if me is not None:
                    scores(n, 3)
                if pr is not None:
                    e.bn_aggr(mv2[:, q, :], st2[:, q, :]).then_inc(s["mv2"], 1)
                    wait(e, "sd2", m + 1)
                    e.reciprocal(rs2[:, q, 3:4], rs2[:, q, 2:3]).then_inc(s["rc2"], 1)
                if me is not None:
                    wait(e, "u", n + 1)
                    e.tensor_tensor(um, half(6, 0, D).rearrange("p (k n) -> p k n", k=KD), headm[:], ALU.mult).then_inc(s["umm"], 1)
                if pr is not None:
                    wait(e, "rc2", m + 1)
                    e.scalar_tensor_tensor(out=rs2[:, q, 4:5], in0=mv2[:, q, 0:1], scalar=-1.0, in1=rs2[:, q, 3:4],
                                           op0=ALU.mult, op1=ALU.mult).then_inc(s["nm2"], 1)
                if me is not None:
                    wait(e, "umm", n + 1)
                    wait(e, "in_", n + 1)
                    for k in range(KD):
                        e.scalar_tensor_tensor(out=kv[:, p, k, :], in0=kv[:, p, k, :], scalar=bdec[:, k:k + 1],
                                               in1=um[:, k, :], op0=ALU.mult, op1=ALU.add).then_inc(s["kvv"], 1)
                if pr is not None:
                    wait(e, "nm2", m + 1)
                    wait(e, "h2", m - 1)
                    e.tensor_scalar(xn2[:, q:q + 1, :], xres[:, bass.ds(mt, 1), :], rs2[:, q, 3:4], rs2[:, q, 4:5],
                                    ALU.mult, ALU.add).then_inc(s["xn2"], 1)
            steps(e, step)

            attention_over(e)
            e.wait_ge(s["cc"], 64)
            count = [0]

            def link(ins):
                ins.then_inc(s["rt"], 1)
                count[0] += 1
                e.wait_ge(s["rt"], count[0])

            def over(a):
                return a.unsqueeze(2).to_broadcast([P, NT, NE])

            revb = rev[:, :].unsqueeze(1).to_broadcast([P, NT, NE])
            link(e.tensor_reduce(mx, logit[:], AX.X, ALU.max))
            link(e.tensor_tensor(lm, logit[:], over(mx), ALU.subtract))
            e.wait_ge(s["rex"], 1)
            link(e.tensor_reduce(sm, ex, AX.X, ALU.add))
            link(e.reciprocal(rsm, sm))
            link(e.tensor_tensor(pr, ex, over(rsm), ALU.mult))

            def first_largest(probs, largest, mark, onehot):
                link(e.tensor_reduce(largest, probs, AX.X, ALU.max))
                link(e.tensor_tensor(eq, probs, over(largest), ALU.is_equal))
                link(e.tensor_tensor(pick, eq, revb, ALU.mult))
                link(e.tensor_reduce(mark, pick, AX.X, ALU.max))
                link(e.tensor_tensor(onehot, revb, over(mark), ALU.is_equal))

            first_largest(pr, p1, f1, m1)
            link(e.scalar_tensor_tensor(out=pr2, in0=m1, scalar=-2.0, in1=pr, op0=ALU.mult, op1=ALU.add))
            first_largest(pr2, p2, f2, m2)
            link(e.tensor_tensor(picked, m1.rearrange("p t e -> p (t e)"), m2.rearrange("p t e -> p (t e)"), ALU.add))
            link(e.tensor_tensor(den, p1, p2, ALU.add))
            link(e.reciprocal(rden, den))
            meta = h2s[:, :, 2 * D:ROW].bitcast(f32)
            e.tensor_tensor(meta[:, :, 0], p1, rden, ALU.mult)
            e.tensor_copy(meta[:, :, 1], tok1[:])
            e.tensor_tensor(pool_w2[:, :, 0], p2, rden, ALU.mult)
            link(e.tensor_copy(pool_w2[:, :, 1], tok1[:]))
            def places(f):
                if f != 0:
                    return
                e.wait_ge(s["rp"], 1)
                link(e.tensor_scalar(tiles_i, half(7, NT * NE, NE), float(P - 1), None, ALU.add))
                link(e.tensor_scalar(tiles_s, tiles_i, 7, None, ALU.arith_shift_right))
                link(e.tensor_copy(tiles_f, tiles_s))
                link(e.tensor_tensor_scan(tiles_end, ones[:, 0:NE], tiles_f, 0.0, ALU.mult, ALU.add))
                link(e.tensor_tensor(base, tiles_end, tiles_f, ALU.subtract))
                link(e.tensor_scalar(base, base, float(P), None, ALU.mult))
                link(e.tensor_tensor(pos, half(7, 0, NT * NE).rearrange("p (t e) -> p t e", t=NT),
                                     base.unsqueeze(1).to_broadcast([P, NT, NE]), ALU.add))
                link(e.tensor_tensor(eq, pos, m1, ALU.mult))
                e.tensor_reduce(mx, eq, AX.X, ALU.add)
                link(e.tensor_tensor(pick, pos, m2, ALU.mult))
                link(e.tensor_reduce(sm, pick, AX.X, ALU.add))
                e.tensor_copy(idx1, mx)
                link(e.tensor_copy(idx2, sm))
                link(e.tensor_tensor(gej[0:1], jt[:, :].unsqueeze(2).to_broadcast([1, NG, NE]),
                                     tiles_end[0:1].unsqueeze(1).to_broadcast([1, NG, NE]), ALU.is_ge))
                link(e.tensor_reduce(slot_f[0:1], gej[0:1], AX.X, ALU.add))
                link(e.tensor_scalar(slot_f[0:1], slot_f[0:1], float(NE - 1), float(SLOT), ALU.min, ALU.mult))
                e.memset(slot_of[:, 0:NT], NSH * SLOT)
                link(e.tensor_copy(slot_of[:, NT:NT + NG], slot_f[0:1]))
                assert count[0] == RT_DONE, count[0]


            def split(x):
                q = NPIECE - 1
                e.wait_ge(s_ld[q], 16 * x + 16)
                e.wait_ge(s["cva"], 2 * x + 2)
                e.tensor_copy(wx[:, bass.ds(x * SLOT + weights(q, 0), PIECE)], stage[q]).then_inc(s["cvh"], NPIECE)
                for q in range(NPIECE - 1):
                    e.tensor_tensor(wx[:, bass.ds(x * SLOT + weights(q, 1), PIECE)], stage[q],
                                    wx[:, bass.ds(x * SLOT + weights(q, 0), PIECE)], ALU.subtract).then_inc(s["cvl"], 1)

            def step(f, p, routed=None):
                if (y := tile_at(f, -1, p, routed)):
                    g, q, _ = y
                    wait(e, "xt", g + 1)
                    wait(e, "u2", g - 1)
                    e.tensor_copy(xT[q], ps[:, 0, 0:D].bitcast(bf16)).then_inc(s["xe"], 1)
                if (y := tile_at(f, 0, p, routed)) and y[2]:
                    g, q, _ = y
                    m = xg[q][:, 2 * D:ROW].bitcast(f32)
                    j = bass.ds(g - NT, 1)
                    wait(e, s_xg[q], 8 * (g - q) + 16)
                    wait(e, "meta0", g - NT)
                    e.tensor_scalar(zer[:, 0:1], m[:, 1:2], 0.0, dummy[:, 0:1], ALU.is_equal, ALU.mult).then_inc(s["ge"], 1)
                    e.tensor_copy(metaw[:, j], m[:, 0:1])
                    wait(e, "ge", g - NT + 1)
                    e.scalar_tensor_tensor(out=dst_i[:, j], in0=m[:, 1:2], scalar=-1.0, in1=zer[:, 0:1],
                                           op0=ALU.add, op1=ALU.add).then_inc(s["meta0"], 1)
                if (y := tile_at(f, 1, p, routed)):
                    g, q, _ = y
                    wait(e, "hi2", g + 1)
                    wait(e, "ht", g - 1)
                    e.tensor_tensor(hs[q][:, FF:2 * FF], hf[q], hs[q][:, 0:FF], ALU.subtract).then_inc(s["lo2"], 1)
                if (y := tile_at(f, 0, p, routed)):
                    g, q, _ = y
                    if q == 1 and (g < NT if isinstance(g, int) else not routed):
                        split((g - 1) // 2)
                    wait(e, "u2", g + 1)
                    wait(e, "sl", g + 1)
                    e.tensor_tensor(hf[q], ps[:, 2 + 2 * q, :], sg[q], ALU.mult).then_inc(s["hh"], 1)
            pipeline(e, step, places)

            for i in range(NT // 2):
                e.wait_ge(s_fl[i], 16)
                e.tensor_tensor(back[i], back[i], modr[:, i // (NC // 2), 3:4, :].to_broadcast([P, 2, D]), ALU.mult).then_inc(s["fa"], 1)
                e.wait_ge(s["fa"], 2 * i + 1)
                e.tensor_tensor(back[i], back[i], xres[:, 2 * i:2 * i + 2, :], ALU.add).then_inc(s["fa"], 1)

        @block.tensor
        def _(e):
            e.wait_ge(s["mod"], 16)
            e.wait_ge(s["a0"], 1)
            for a in range(2):
                for k in range(KD):
                    for kk in range(KD):
                        ins = e.matmul(half(6, (a * KD + k) * B, B), wmod[:, kk, (a * KD + k) * P:(a * KD + k + 1) * P],
                                       cs[:, kk, :], start=kk == 0, stop=kk == KD - 1)
            ins.then_inc(s["mr"], 1)
            e.wait_ge(s["ccb"], 1)
            for b in range(B):
                for a in range(2):
                    for kk in range(KD):
                        ins = e.matmul(ps[:, 2 + 2 * b + a, :], cbc[:, kk, b, :],
                                       wmod[:, kk, 2 * D + 512 * a:2 * D + 512 * (a + 1)], start=kk == 0, stop=kk == KD - 1)
            ins.then_inc(s["mr"], 1)

            def turn(i):
                for j in range(2):
                    n = 2 * i + j
                    e.wait_ge(s["xn"], n + 1)
                    wait(e, "he", n - 1)
                    for k in range(KD):
                        ins = e.transpose(half(j, k * P), xn[:, j, k * P:(k + 1) * P], ident[:])
                    ins.then_inc(s["tp"], 1)
            loop(e, NT // 2, turn)
            e.wait_ge(s["w"], 48)
            e.wait_ge(s["he"], NT)
            e.wait_ge(s["vm"], 3 * B)

            def project(g):
                for j in range(3 * KD):
                    if not isinstance(g, int):
                        if j < 2 * KD:
                            e.wait_ge(s["qe"], 2 * KD * g - 2 * KD + j + 1)
                        else:
                            e.wait_ge(s["ue"], KD * g - KD + (j - 2 * KD) + 1)
                    col = j * P if j < 2 * KD else 3 * D + (j - 2 * KD) * P
                    for kk in range(KD):
                        ins = e.matmul(ps[:, j, :], wqkvu[:, kk, col:col + P], hT[:, kk, bass.ts(g, QSTRIDE * P)],
                                       start=kk == 0, stop=kk == KD - 1)
                    ins.then_inc(s["qkp"], 1)
            loop(e, NT // QSTRIDE, project)
            e.wait_ge(s["qe"], 2 * KD * NT // QSTRIDE)
            e.wait_ge(s["ue"], KD * NT // QSTRIDE)
            e.wait_ge(s["v3"], B)

            def qk(n, tile, p, j):
                wait(e, "sdm", 4 * n + j - 1)
                if j == 0:
                    wait(e, s_qb[p], 16 * HP * (tile - NC * p + 1))
                k = j // 2
                e.matmul(ps[:, 2 + j % 2, :], kh[p][:, k, :],
                         qbd[p][:, k, 4 * (j % 2):4 * (j % 2) + 4, :].rearrange("p h n -> p (h n)"),
                         start=True, stop=True).then_inc(s["s"], 1)

            def inter(n, p, k):
                if k == 0:
                    wait(e, "oe", n)
                    wait(e, "qd", n + 1)
                    wait(e, "kvv", KD * (n - 1))
                ins = e.matmul(half(5, k * P), kv[:, p, k, :], qdec[:, p, k, :], start=True, stop=False)
                if k == 1:
                    ins.then_inc(s["in_"], 1)

            def values(n, p, j):
                wait(e, "sdm", 4 * n + j + 1)
                k = j // 2
                for h in range(4):
                    ins = e.matmul(half(5, k * P), vbd[p][:, 4 * j + h, :], sd[:, j, h, :],
                                   start=False, stop=j % 2 == 1 and h == 3)
                ins.then_inc(s["sg"], 1)

            def step(c, b):
                me, pr, pp = late(c, b, 0), late(c, b, 1), late(c, b, 2)
                if me is not None:
                    n, tile, p = me
                    wait(e, "vr", 3 * n)
                    wait(e, "kh", n + 1)
                    for kk in range(KD):
                        ins = e.matmul(half(0, 0, D), kh[p][:, KD + kk, :], wqkvu[:, kk, 2 * D:3 * D],
                                       start=kk == 0, stop=kk == KD - 1)
                    ins.then_inc(s["vp"], 1)
                    wait(e, "kd", n)
                    for k in range(KD):
                        ins = e.transpose(half(1, k * P), kh[p][:, k, :], ident[:])
                    ins.then_inc(s["kp"], 1)
                    qk(n, tile, p, 0)
                    qk(n, tile, p, 1)
                if pr is not None:
                    m, mt, q = pr
                    wait(e, "sq", m + 1)
                    wait(e, "y", m + 1)
                    wait(e, "x1", m)
                    for k in range(KD):
                        e.matmul(half(7, D), sq[:, q, k, :], ones[:], start=k == 0, stop=k == KD - 1)
                    for k in range(KD):
                        ins = e.matmul(half(7, 0, D), yT[:, q, k, :], woutg[:, q, k, :], start=k == 0, stop=k == KD - 1)
                    ins.then_inc(s["a"], 1)
                if me is not None:
                    inter(n, p, 0)
                    wait(e, "vr", 3 * n + 3)
                    values(n, p, 0)
                    qk(n, tile, p, 2)
                    values(n, p, 1)
                    qk(n, tile, p, 3)
                if pp is not None:
                    m2, _, q2 = pp
                    wait(e, "h2", m2 + 1)
                    wait(e, "le", m2)
                    for k in range(KD):
                        ins = e.transpose(half(4, k * P), h2[:, q2, k * P:(k + 1) * P], ident[:])
                    ins.then_inc(s["tb"], 1)
                if me is not None:
                    wait(e, "kd", n + 1)
                    wait(e, "umm", n)
                    for k in range(KD):
                        ins = e.matmul(half(6, k * P), kdec[:, p, k * P:(k + 1) * P], vtok[:, p, k * P:(k + 1) * P],
                                       start=True, stop=True)
                    ins.then_inc(s["u"], 1)
                    inter(n, p, 1)
                    values(n, p, 2)
                    values(n, p, 3)
                if pp is not None:
                    wait(e, "hte", m2 + 1)
                    for k in range(KD):
                        ins = e.matmul(half(4, D), h2T[:, q2, k, :], wg[:, k, :], start=k == 0, stop=k == KD - 1)
                    ins.then_inc(s["lg"], 1)
            steps(e, step)

            attention_over(e)

            def turn_rows(g, p, routed):
                wait(e, s_xg[p], 8 * (g - p) + 16)
                wait(e, "xe", g)
                for m in range(4):
                    ins = e.transpose(ps[:, 0, 0:D].bitcast(bf16)[:, m * P:(m + 1) * P], xg[p][:, m * P:(m + 1) * P], identb[:])
                ins.then_inc(s["xt"], 1)

            def slot(g, routed):
                if not routed:
                    return NSH * SLOT
                return e.value_load(slot_of[0:1, bass.ds(g, 1)], min_val=0, max_val=NSH * SLOT)

            PASSES = ((0, 0), (0, 1), (1, 0))

            def gate_up(g, p, routed):
                at_ = slot(g, routed)
                wait(e, "xe", g + 1)
                for part, name, free in ((0, "g", "sl"), (1, "u2", "hh")):
                    wait(e, free, g - 1)
                    n = 0
                    for k in range(KD):
                        for a, w in PASSES:
                            ins = e.matmul(ps[:, 1 + 2 * p + part, :], xT[p][:, (2 * a + k) * P:(2 * a + k + 1) * P],
                                           wx[:, bass.ds(at_ + weights(part, w) + k * FF, FF)],
                                           start=n == 0, stop=n == 3 * KD - 1)
                            n += 1
                    ins.then_inc(s[name], 1)

            def turn_inner(g, p):
                wait(e, "lo2", g + 1)
                wait(e, "he2", g)
                for m in range(2 * KF):
                    ins = e.transpose(ps[:, 5, :].bitcast(bf16)[:, m * P:(m + 1) * P], hs[p][:, m * P:(m + 1) * P], identb[:])
                ins.then_inc(s["ht"], 1)

            def down(g, p, routed):
                at_ = slot(g, routed)
                wait(e, "he2", g + 1)
                wait(e, "ye", g - 1)
                n = 0
                for k in range(KF):
                    for a, w in PASSES:
                        ins = e.matmul(ps[:, 6 + p, 0:D], hsT[p][:, (KF * a + k) * P:(KF * a + k + 1) * P],
                                       wx[:, bass.ds(at_ + weights(2, w) + k * D, D)],
                                       start=n == 0, stop=n == 3 * KF - 1)
                        n += 1
                ins.then_inc(s["yd"], 1)

            def step(f, p, routed=None):
                if (y := tile_at(f, -1, p, routed)):
                    turn_rows(*y)
                if (y := tile_at(f, 0, p, routed)):
                    if isinstance(f, int) and f == NT:
                        e.wait_ge(s["cvl"], NPIECE * NE)
                        e.wait_ge(s["rt"], RT_DONE)
                    gate_up(*y)
                if (y := tile_at(f, 2, p, routed)):
                    if isinstance(f, int) and f == 3:
                        e.wait_ge(s["rt"], RT_DONE)
                    down(*y)
                if (y := tile_at(f, 1, p, routed)):
                    turn_inner(y[0], y[1])

            def rank(f):
                if f != 0:
                    return
                e.wait_ge(s["rt"], RT_PICKED)
                e.matmul(half(7, 0, NT * NE), ustrict[:], picked, start=True, stop=False, skip_group_check=True)
                for k in range(1, NT):
                    e.matmul(half(7, k * NE, (NT - k) * NE), onesb[:], picked[:, 0:(NT - k) * NE],
                             start=False, stop=False, skip_group_check=True)
                for k in range(NT):
                    ins = e.matmul(half(7, NT * NE, NE), onesb[:], picked[:, k * NE:(k + 1) * NE],
                                   start=False, stop=k == NT - 1, skip_group_check=True)
                ins.then_inc(s["rp"], 1)
            pipeline(e, step, rank)



def constants():
    f = np.float32
    m = np.arange(P)
    same = (m[:, None] // DH == m[None, :] // DH).astype(f)
    return dict(
        lag=np.maximum(m[None, :] - m[:, None], 0).astype(f),
        causal=(m[None, :] >= m[:, None]).astype(f),
        posn=np.concatenate([np.tile(m + 1, (P, 1)), (P - 1 - m)[:, None]], 1).astype(f),
        headm=np.stack([same] * KD, 1),
        ident=np.eye(P, dtype=f),
        ones=np.ones((P, P), f),
        rev=np.tile(NE - np.arange(NE), (P, 1)).astype(f),
        tok1=(np.arange(NT)[None, :] * P + m[:, None] + 1).astype(f),
        dummy=(B * S + 1 + m)[:, None].astype(f),
        jt=np.arange(NG)[None, :].astype(f),
    )


def layout(i):
    def rows(w):
        return np.ascontiguousarray(w.reshape(-1, P, w.shape[-1]).transpose(1, 0, 2))

    slope = i["L0_attn_slope_rate"].reshape(NH)
    a = dict(
        x=i["L0_attn_x"].reshape(B * S, D),
        cT=rows(i["L0_c"].T),
        slr=np.ascontiguousarray(np.broadcast_to(slope, (P, NH))),
        slc=np.ascontiguousarray(np.repeat(slope, DH).reshape(KD, P).T),
        wmod=rows(i["L0_wmod"]),
        wqkvu=rows(i["L0_attn_W_qkvu"].T),
        wout=rows(i["L0_attn_W_out"].T),
    )
    a["wg"] = np.zeros((P, KD, P), np.float32)
    a["wg"][:, :, 0:NE] = rows(i["L0_ffn_wg"].T)
    gate = [*i["L0_ffn_ex_gate"], i["L0_ffn_sh_gate"]]
    up = [*i["L0_ffn_ex_up"], i["L0_ffn_sh_up"]]
    down = [*i["L0_ffn_ex_down"], i["L0_ffn_sh_down"]]
    a["wexp"] = np.stack([np.stack([rows(w.T).reshape(P, PIECE) for w in three], 1)
                          for three in zip(gate, up, down)])
    a.update(constants())
    return a


def kernel(**inputs):
    import concourse.bacc as bacc
    from concourse.bass_utils import run_bass_kernel_spmd

    nc = bacc.Bacc("TRN2", target_bir_lowering=False, num_devices=1)
    arrays = layout({k: np.asarray(v) for k, v in inputs.items()})
    t = {n: nc.dram_tensor("in_" + n, a.shape, mybir.dt.from_np(a.dtype), kind="ExternalInput").ap()
         for n, a in arrays.items()}
    t["xg"] = nc.dram_tensor("dispatched", [NG * P, ROW // 2], mybir.dt.uint32).ap()
    t["acc"] = nc.dram_tensor("expert_sum", [ACC, D], mybir.dt.float32).ap()
    t["out"] = nc.dram_tensor("out", [B * S, D], mybir.dt.float32, kind="ExternalOutput").ap()
    build(nc, t)
    r = run_bass_kernel_spmd(nc, [{"in_" + n: a for n, a in arrays.items()}], core_ids=[0])
    return r.results[0]["out"].reshape(B, S, D)
```

```python
import numpy as np
from contextlib import ExitStack

import concourse.bass as bass
from concourse import mybir

P = 128
B, S, D = 2, 1024, 256
KD = D // P
NH, DH = 16, 16
HP = P // DH
NT = B * S // P
NC = S // P
NE, FF, NSH = 8, 512, 8
KF = FF // P
TOP = 2
PIECE = KD * FF
NPIECE = 3
SLOT = 2 * NPIECE * PIECE
SHARED_AT = NE * SLOT + 4 * NH * P
NG = TOP * NT + NE - 1
ROW = 2 * D + 4
ACC = B * S + P
LN_EPS, RMS_EPS = 1e-5, 1e-6
GT = 4
XPOOL = 3
RT_PICKED, RT_DONE = 17, 35


def build(nc, t):
    f32, bf16, i32, u32 = mybir.dt.float32, mybir.dt.bfloat16, mybir.dt.int32, mybir.dt.uint32
    ALU, ACT, AX = mybir.AluOpType, mybir.ActivationFunctionType, mybir.AxisListType
    ctx = ExitStack()
    with ctx:
        def sb(name, shape, dt=f32):
            return ctx.enter_context(nc.sbuf_tensor(name, shape, dt))

        def sem(name):
            return ctx.enter_context(nc.semaphore(name))

        wx = sb("wx", [P, SHARED_AT + SLOT], bf16)
        att = wx[:, 0:NE * SLOT].bitcast(f32)
        at = [0]

        def in_att(n):
            at[0] += n
            return att[:, at[0] - n:at[0]]

        qT = in_att(KD * B * S).rearrange("p (k n) -> p k n", k=KD)
        uT = in_att(KD * B * S).rearrange("p (k n) -> p k n", k=KD)
        khT = in_att(2 * KD * B * S).rearrange("p (k n) -> p k n", k=2 * KD)
        kT, hT = khT[:, 0:KD], khT[:, KD:2 * KD]
        qbd = [in_att(KD * HP * P).rearrange("p (k h n) -> p k h n", k=KD, h=HP) for _ in range(2)]
        vbd = [in_att(NH * P).rearrange("p (h n) -> p h n", h=NH) for _ in range(2)]
        xres = sb("xres", [P, NT, D])
        h2s = sb("h2s", [P, NT, ROW], bf16)
        wqkvu = sb("wqkvu", [P, KD, 4 * D])
        kh = [wqkvu[:, b, 0:2 * D].rearrange("p (k n) -> p k n", n=P) for b in range(2)]
        woutg = sb("woutg", [P, B, KD, D])
        kept = sb("kept", [P, KEPT])
        kept_at = dict(zip(KEPT_PARTS, np.cumsum([0, *KEPT_PARTS.values()]).tolist()))

        def keep(name):
            return kept[:, kept_at[name]:kept_at[name] + KEPT_PARTS[name]]

        ident, ones, rev, tok1, dummy = (keep(n) for n in ("ident", "ones", "rev", "tok1", "dummy"))
        slr, slc = keep("slr"), keep("slc")
        headm = keep("headm").rearrange("p (k n) -> p k n", k=KD)
        wg = keep("wg").rearrange("p (k n) -> p k n", k=KD)
        identb = sb("identb", [P, P], bf16)
        cT = sb("cT", [P, KD, B])
        cs = sb("cs", [P, KD, B])
        modc = sb("modc", [P, 2, KD, B])
        modr = sb("modr", [P, B, 4, D])
        dq = sb("dq", [P, KD, P])
        dk = sb("dk", [P, NH, DH])
        nsl = sb("nsl", [P, NH + KD])
        npos = sb("npos", [P, 1])
        bdec = sb("bdec", [P, KD])
        st1 = sb("st1", [P, NT, 6])
        mv1 = sb("mv1", [P, NT, 2])
        rs1 = sb("rs1", [P, 3, NT])
        st2 = sb("st2", [P, 2, 6])
        mv2 = sb("mv2", [P, 2, 2])
        rs2 = sb("rs2", [P, 2, 6])
        logit = sb("logit", [P, NT, NE])
        wmod = h2s[:].rearrange("p t d -> p (t d)").bitcast(f32)[:, 0:KD * 6 * D].rearrange("p (k n) -> p k n", k=KD)
        epst = sb("epst", [P, 2])
        tmp = sb("tmp", [P, 11 * 2 * D + D + ROW - 2 * D])
        used = [0]

        def carve(n, dt=f32):
            words = n if dt == f32 else n // 2
            used[0] += words
            return tmp[:, used[0] - words:used[0]] if dt == f32 else tmp[:, used[0] - words:used[0]].bitcast(dt)

        def two(n=D):
            return carve(2 * n).rearrange("p (a n) -> p a n", a=2)

        def two_t():
            return carve(2 * D).rearrange("p (a k n) -> p a k n", a=2, k=KD)

        xn = two()
        carve(ROW - 2 * D)
        kdec, vtok, qdec, kv = two(), two(), two_t(), two_t()
        um = carve(D).rearrange("p (k n) -> p k n", k=KD)
        oT, sq, yT, xn2, h2, h2T = two_t(), two_t(), two_t(), two(), two(), two_t()
        used[0] = 0
        xg = [carve(ROW, bf16) for _ in range(2)]
        xT = [carve(2 * D, bf16) for _ in range(2)]
        sg = [carve(FF) for _ in range(2)]
        hf = [carve(FF) for _ in range(2)]
        hs = [carve(2 * FF, bf16) for _ in range(2)]
        yb = [carve(D) for _ in range(2)]
        hsT = [carve(2 * FF, bf16) for _ in range(2)]
        score = wx[:, NE * SLOT:SHARED_AT].bitcast(f32)
        decay = score[:, 0:NH * P].rearrange("p (h n) -> p h n", h=NH)
        sd = score[:, NH * P:2 * NH * P].rearrange("p (j h n) -> p j h n", j=4, h=4)

        def stage(x, q):
            if isinstance(x, int):
                at_ = (x + 1) * SLOT + 2 * q * PIECE
                return wx[:, at_:at_ + 2 * PIECE].bitcast(f32)
            return wx[:].bitcast(f32)[:, bass.ds((x + 1) * (SLOT // 2) + q * PIECE, PIECE)]

        early_stage = qT.rearrange("p k n -> p (k n)")
        rt = wqkvu[:].rearrange("p k n -> p (k n)")
        rused = [0]

        def route(n, dt=f32):
            rused[0] += n
            a = rt[:, rused[0] - n:rused[0]]
            return a if dt == f32 else a.bitcast(dt)

        def route3(dt=f32):
            return route(NT * NE, dt).rearrange("p (t e) -> p t e", t=NT)

        lm, ex, pr, eq, pick, m1, m2, pr2, pos = (route3() for _ in range(9))
        gbw = [rt[:, i * D:(i + 1) * D] for i in range(2)]
        mx, sm, rsm, p1, f1, p2, f2, den, rden = (route(NT) for _ in range(9))
        pool_w2 = route(2 * NT).rearrange("p (t a) -> p t a", t=NT)
        idx1, idx2 = route(NT, u32), route(NT, u32)
        picked = route(NT * NE // 2).bitcast(bf16)
        tiles_i, tiles_s = route(NE, i32), route(NE, i32)
        tiles_f, tiles_end, base = route(NE), route(NE), route(NE)
        gej = route(NG * NE).rearrange("p (j e) -> p j e", j=NG)
        slot_f = route(NG)
        slot_of = sb("slot_of", [1, NG], i32)
        wrow = sb("wrow", [P, B, NG])
        zer = sb("zer", [P, 2])
        dst_i = sb("dst_i", [P, NG], u32)
        ustrict = sb("ustrict", [P, P], bf16)
        onesb = sb("onesb", [P, P], bf16)
        jt = sb("jt", [1, NG])
        cbc = h2s[:].rearrange("p t d -> p (t d)").bitcast(f32)[:, KD * 6 * D:KD * (6 * D + B * P)].rearrange(
            "p (k b n) -> p k b n", k=KD, b=B)
        wout = h2s[:].rearrange("p t d -> p (t d)").bitcast(f32)[:, KD * (6 * D + B * P):KD * (7 * D + B * P)].rearrange(
            "p (k n) -> p k n", k=KD)

        def diag_ap(t_, k):
            flat = t_.rearrange("p h n -> p (h n)")
            n0 = k * HP * P
            part = flat[:, n0:n0 + HP * P]
            return bass.AP(part.tensor, part.offset, [part.ap[0], [P + DH, HP], [1, DH]])

        ps = ctx.enter_context(nc.psum_tensor("ps", [P, 8, 512], f32))

        tabs = h2T.rearrange("p a k n -> p (a k n)")
        lag, causal, posn = tabs[:, 0:P], tabs[:, P:2 * P], tabs[:, 2 * P:3 * P + 1]
        early = sd.rearrange("p j h n -> p (j h n)").rearrange("p (a b c n) -> p a b c n", a=2, b=B, c=2)
        sgn, mag = early[:, 0], early[:, 1]

        def half(bank, at, n=P):
            return ps[:, bank, at:at + n]

        names = ("w c0 c mod z0 z1 lz v0 a0 v1 a1 v2 p2 v3 mc mr vm va st mv sdv rs nm xn tp he "
                 "qkp kh qkr qe ue "
                 "vp vr vb kp kd qd s sdm sg oe u umm kvv in_ sq y a r0 r x1 bs mv2 sd2 rc2 nm2 xn2 ha h h2 hi lo "
                 "tb hte lg le out cc ccb ge "
                 "cva cvd cvp fill ws wh wl rt rex rp sc1 sc2 mt2 "
                 "xt xe g u2 sl hh hi2 lo2 ht he2 yd ye acc gw gy meta0").split()
        s = {n: sem("s_" + n) for n in names}
        s_xg = [sem(f"s_xg{i}") for i in range(2)]
        s_x = [sem(f"s_xin{g}") for g in range(NT // GT)]
        s_st = [sem(f"s_st{i}") for i in range(2)]
        s_ld = [sem(f"s_ld{q}") for q in range(NPIECE)]
        s_qb = [sem(f"s_qb{i}") for i in range(2)]
        block = ctx.enter_context(nc.Block())

        def late(c, b, k):
            if k == 1:
                c, b = (c - 1, 1) if b == 0 else (c, 0)
            elif k == 2:
                c = c - 1
            if isinstance(c, int) and not (0 <= c < NC):
                return None
            return 2 * c + b, c + NC * b, b

        def steps(eng, step, ahead=None):
            for c in range(2):
                for b in range(2):
                    step(c, b)
            with eng.Fori(2, NC) as c:
                for b in range(2):
                    step(c, b)
            step(NC, 0)
            if ahead:
                ahead()
            step(NC, 1)

        def wait(eng, name, value):
            if not isinstance(value, int) or value > 0:
                eng.wait_ge(s[name] if isinstance(name, str) else name, value)

        def loop(eng, count, body):
            body(0)
            with eng.Fori(1, count) as i:
                body(i)

        def cols(tile):
            return bass.ts(tile, P)

        NF = NT + NG
        LO, MID, HI = 6, NT - 2, NT + 6
        LAST = HI + (NF - HI - 2) // 2 * 2

        def attention_over(e):
            e.wait_ge(s["le"], NT)
            e.wait_ge(s["lo"], NT)
            e.wait_ge(s["kvv"], KD * NT)

        def pipeline(eng, step, between=None, begin=-1):
            for f in range(-1, LO):
                if f >= begin:
                    step(f, f % 2)
                if between:
                    between(f)
            with eng.Fori(LO, MID, 2) as f:
                for j in range(2):
                    step(f + j, j, False)
            for f in range(MID, HI):
                step(f, f % 2)
            with eng.Fori(HI, LAST, 2) as f:
                for j in range(2):
                    step(f + j, j, True)
            for f in range(LAST, NF + 3):
                step(f, f % 2)

        def tile_at(f, k, p, routed):
            if isinstance(f, int):
                g = f - k
                return (g, g % 2, g >= NT) if 0 <= g < NF else None
            return f - k, (p - k) % 2, routed

        def late_rows(f):
            return isinstance(f, int) and f == NT - 1

        def inner_free(e, g, routed):
            if routed and not (isinstance(g, int) and g < NT + 2):
                wait(e, "ht", g - NT - 1)
            else:
                wait(e, "yd", g - 1)

        def place(g, p):
            c = (g - p) // 2
            return c + NC * p

        def weights(part, low):
            return low * NPIECE * PIECE + part * PIECE

        @block.sync
        def _(e):
            e.dma_start(wmod[:], t["wmod"]).then_inc(s["mod"], 16)
            xin = t["x"].rearrange("(t p) d -> p t d", p=P)
            for g in range(NT // GT):
                e.dma_start(xres[:, GT * g:GT * (g + 1), :], xin[:, GT * g:GT * (g + 1), :]).then_inc(s_x[g], 16)
            e.dma_start(wqkvu[:], t["wqkvu"]).then_inc(s["w"], 16)
            e.dma_start(wout, t["wout"]).then_inc(s["w"], 16)
            for q in range(NPIECE):
                e.dma_start(early_stage[:, q * PIECE:(q + 1) * PIECE], t["wexp"][NSH, :, q, :]).then_inc(s["ws"], 16)
            e.wait_ge(s["ws"], 16 * NPIECE)
            e.wait_ge(s["z0"], 2)
            zeros = qbd[0].rearrange("p k h n -> p (k h n)").bitcast(u32)
            rows = t["xg"].rearrange("(j p) d -> p j d", p=P)
            per = KD * HP * P * 2 // ROW
            nfill = 0
            for j in range(0, NG, per):
                m = min(per, NG - j)
                e.dma_start(rows[:, j:j + m, :], zeros[:, 0:m * ROW // 2].rearrange("p (j d) -> p j d", j=m)).then_inc(s["fill"], 16)
                nfill += 16
            e.dma_start(t["acc"][B * S:ACC, :], zeros[:, 0:D].bitcast(f32)).then_inc(s["fill"], 16)
            e.wait_ge(s["fill"], nfill + 16)
            def step(c, b):
                me = late(c, b, 0)
                if me is None:
                    return
                n, tile, _ = me
                if isinstance(c, int) and n == 0:
                    e.wait_ge(s["qe"], 2 * KD * NT // GT)
                    e.wait_ge(s["z0"], 2)
                wait(e, "sg", 4 * n - 4)
                for h in range(HP):
                    rows = slice(h * DH, (h + 1) * DH)
                    e.dma_start(qbd[b][rows, :, h, :], qT[rows, :, cols(tile)]).then_inc(s_qb[b], 16)
            steps(e, step)

            def load_expert(x):
                for q in range(NPIECE):
                    if x:
                        e.wait_ge(s_ld[q], 16 * x)
                    e.dma_start(stage(x, q), t["wexp"][x, :, q, :]).then_inc(s_ld[q], 16)

            def load_rows(g, p, routed):
                if routed:
                    row = g - NT if isinstance(g, int) else e.snap(g - NT)
                    if isinstance(g, int) and g < NT + 2:
                        e.wait_ge(s["xe"], g - 1)
                    else:
                        wait(e, "meta0", g - 2 - NT + 1)
                    e.dma_start(xg[p].bitcast(u32).unsqueeze(1),
                                t["xg"].rearrange("(j p) d -> p j d", p=P)[:, bass.ds(row, 1), :]).then_inc(s_xg[p], 16)
                else:
                    if isinstance(g, int) and g < 2:
                        e.wait_ge(s["lo"], g + 1)
                        e.wait_ge(s["tp"], NT)
                    wait(e, "xe", g - 1)
                    e.dma_start(xg[p][:, 0:2 * D].unsqueeze(1), h2s[:, bass.ds(place(g, p), 1), 0:2 * D]).then_inc(s_xg[p], 16)

            def store_shared(g, p):
                wait(e, "ye", g + 1)
                e.dma_start(t["acc"][0:B * S, :].rearrange("(t p) d -> p t d", p=P)[:, bass.ds(place(g, p), 1), :],
                            yb[p].unsqueeze(1)).then_inc(s_st[p], 16)

            load_rows(0, 0, False)
            load_rows(1, 1, False)
            e.wait_ge(s["kh"], NT)
            e.wait_ge(s["qd"], NT)
            e.wait_ge(s["y"], NT)
            e.wait_ge(s["sg"], 4 * NT)
            load_expert(0)
            load_expert(1)
            e.wait_ge(s["lo"], NT)
            for x in range(NE):
                for g in range(2 * x + 2, 2 * x + 4):
                    if g < NT:
                        load_rows(g, g % 2, False)
                for g in range(2 * x - 4, 2 * x - 2):
                    if g >= 0:
                        store_shared(g, g % 2)
                if x + 2 < NE:
                    load_expert(x + 2)
            e.wait_ge(s["sc1"], 16 * NT)
            e.wait_ge(s["sc2"], 16 * NT)
            for g, done in ((0, None), (1, None), (2, 4), (3, 3), (4, 2), (5, 1)):
                load_rows(NT + g, g % 2, True)
                if done:
                    store_shared(NT - done, done % 2)
            end = NF - (NF - NT) % 2
            with e.Fori(NT + 6, end, 2) as g:
                for j in range(2):
                    load_rows(g + j, j, True)
            for g in range(end, NF):
                load_rows(g, g % 2, True)
            e.wait_ge(s["acc"], 16 * NG)
            for i in range(2):
                half_rows = slice(i * S, (i + 1) * S)
                e.dma_start(t["out"][half_rows, :], t["acc"][half_rows, :]).then_inc(s["out"], 16)
            e.wait_ge(s["out"], 32)

        @block.gpsimd
        def _(e):
            for b in range(2):
                e.memset(qbd[b], 0.0).then_inc(s["z0"], 1)
            for b in range(2):
                e.memset(vbd[b], 0.0).then_inc(s["z1"], 1)
            e.memset(kv, 0.0).then_inc(s["z1"], 1)
            for q in range(NPIECE):
                e.wait_ge(s["wh"], q + 1)
                at_ = SHARED_AT
                e.tensor_tensor(wx[:, at_ + weights(q, 1):at_ + weights(q, 1) + PIECE],
                                early_stage[:, q * PIECE:(q + 1) * PIECE],
                                wx[:, at_ + weights(q, 0):at_ + weights(q, 0) + PIECE], ALU.subtract).then_inc(s["wl"], 1)

            def step(c, b):
                if (me := late(c, b, 0)) is not None:
                    n, tile, _ = me
                    if isinstance(c, int) and n == 0:
                        e.wait_ge(s["qe"], 2 * KD * NT // GT)
                        e.wait_ge(s["ue"], KD * NT // GT)
                        e.wait_ge(s["p2"], 1)
                    wait(e, "sg", 4 * n - 4)
                    e.tensor_copy(kh[b], khT[:, :, cols(tile)]).then_inc(s["kh"], 1)
                    e.tensor_tensor(qdec[:, b], qT[:, :, cols(tile)], dq[:, :, :], ALU.mult).then_inc(s["qd"], 1)
                if (me := late(c, b, 1)) is not None:
                    n, tile, p = me
                    wait(e, "oe", n + 1)
                    if isinstance(c, int) and n == 0:
                        e.wait_ge(s["ue"], KD * NT // GT)
                    wait(e, "a", n - 1)
                    e.tensor_tensor(yT[:, p], oT[:, p], uT[:, :, cols(tile)], ALU.mult).then_inc(s["y"], 1)
                if (me := late(c, b, 2)) is not None:
                    n, tile, p = me
                    wait(e, "xn2", n + 1)
                    e.tensor_tensor(xn2[:, p], xn2[:, p], modr[:, p, 2], ALU.mult).then_inc(s["ha"], 1)
                    wait(e, "ha", n + 1)
                    wait(e, "tb", n - 1)
                    wait(e, "hi", n - 1)
                    e.tensor_tensor(h2[:, p], xn2[:, p], modr[:, p, 1], ALU.add).then_inc(s["h2"], 1)
                    wait(e, "hi", n + 1)
                    wait(e, "h2", n + 1)
                    e.tensor_tensor(h2s[:, bass.ds(tile, 1), D:2 * D], h2[:, p:p + 1, :],
                                    h2s[:, bass.ds(tile, 1), 0:D], ALU.subtract).then_inc(s["lo"], 1)
            steps(e, step)

            attention_over(e)
            e.memset(dst_i[:], 0)

            def split_low(x):
                q = NPIECE - 1
                e.wait_ge(s["cva"], NPIECE * (x + 1))
                wait(e, "cvp", x)
                at_ = x * SLOT
                e.tensor_tensor(wx[:, at_ + weights(q, 1):at_ + weights(q, 1) + PIECE], stage(x, q),
                                wx[:, at_ + weights(q, 0):at_ + weights(q, 0) + PIECE], ALU.subtract).then_inc(s["cvp"], 1)

            def dispatch(which, tiles):
                for n in tiles:
                    e.indirect_dma_start(t["xg"], bass.IndirectOffsetOnAxis(ap=(idx1, idx2)[which][:, n:n + 1], axis=0),
                                         h2s[:, n, :].bitcast(u32), None).then_inc(s[("sc1", "sc2")[which]], 16)

            for x in range(XPOOL):
                split_low(x)
            e.wait_ge(s["rt"], RT_DONE)
            dispatch(0, range(NT))
            e.wait_ge(s["sc1"], 16 * NT)
            e.tensor_copy(h2s[:, :, 2 * D:ROW].bitcast(f32), pool_w2).then_inc(s["mt2"], 1)
            e.wait_ge(s["mt2"], 1)
            dispatch(1, range(NT))
            e.wait_ge(s_st[0], 16 * NT // 2)
            e.wait_ge(s_st[1], 16 * NT // 2)
            for g in range(NG):
                e.wait_ge(s["meta0"], g + 1)
                e.wait_ge(s["ye"], NT + g + 1)
                if g:
                    e.wait_ge(s["acc"], 16 * g)
                e.indirect_dma_start(t["acc"], bass.IndirectOffsetOnAxis(ap=dst_i[:, g:g + 1], axis=0),
                                     yb[g % 2], None, compute_op=ALU.add).then_inc(s["acc"], 16)

        @block.scalar
        def _(e):
            e.dma_start(cT[:], t["cT"]).then_inc(s["c0"], 16)
            e.dma_start(kept[:], t["kept"]).then_inc(s["c"], 16)
            e.dma_start(tabs[:, 0:3 * P + 1], t["decay_tables"]).then_inc(s["c"], 16)
            e.dma_start(jt[:], t["jt"]).then_inc(s["cc"], 16)
            e.wait_ge(s["c0"], 16)
            e.activation(cs[:], cT[:], ACT.Silu).then_inc(s["a0"], 1)
            e.wait_ge(s["v0"], 6)
            e.wait_ge(s["v1"], 2)
            for h in range(NH):
                e.activation(decay[:, h, :], lag[:, :], ACT.Exp, scale=nsl[:, h:h + 1]).then_inc(s["a1"], 1)
            for k in range(KD):
                e.activation(dq[:, k, :], posn[:, 0:P], ACT.Exp, scale=nsl[:, NH + k:NH + k + 1])
                e.activation(bdec[:, k:k + 1], posn[:, P - 1:P], ACT.Exp, scale=nsl[:, NH + k:NH + k + 1]).then_inc(s["a1"], 1)
            e.activation(dk[:, :, :], slr.unsqueeze(2).to_broadcast([P, NH, DH]), ACT.Exp,
                         scale=npos[:, 0:1]).then_inc(s["p2"], 1)
            e.wait_ge(s["ws"], 16 * NPIECE)
            for q in range(NPIECE):
                at_ = SHARED_AT
                e.activation(wx[:, at_ + weights(q, 0):at_ + weights(q, 0) + PIECE],
                             early_stage[:, q * PIECE:(q + 1) * PIECE], ACT.Copy).then_inc(s["wh"], 1)
            e.wait_ge(s["mv"], NT)
            e.activation(rs1[:, 0, :], mv1[:, :, 1], ACT.Sqrt, bias=epst[:, 0:1]).then_inc(s["sdv"], 1)
            e.wait_ge(s["mc"], 1)
            with e.Fori(0, NT // GT // B) as i:
                for b in range(B):
                    g = i + NT // GT // B * b
                    e.wait_ge(s["tp"], GT * (B * i + b) + GT)
                    for k in range(KD):
                        ins = e.activation(hT[:, k, bass.ts(g, GT * P)], ps[:, 6 * b + k, :], ACT.Identity,
                                           scale=modc[:, 1, k, b:b + 1], bias=modc[:, 0, k, b:b + 1])
                    ins.then_inc(s["he"], 1)
            e.wait_ge(s["wl"], NPIECE)
            with e.Fori(0, NT // GT // B) as i:
                for b in range(B):
                    g = i + NT // GT // B * b
                    for j in range(2 * KD):
                        e.wait_ge(s["qkp"], 3 * KD * (B * i + b) + j + 1)
                        dst = (qT, kT)[j // KD]
                        e.activation(dst[:, j % KD, bass.ts(g, GT * P)], ps[:, j, :], ACT.Silu).then_inc(s["qe"], 1)

            e.wait_ge(s["z1"], 3)

            def step_attention(c, b):
                if (me := late(c, b, 1)) is not None:
                    n, tile, p = me
                    wait(e, "sg", 4 * n + 4)
                    wait(e, "y", n - 1)
                    wait(e, "sq", n - 1)
                    e.activation(oT[:, p], half(5, 0, D).rearrange("p (k n) -> p k n", k=KD), ACT.Copy).then_inc(s["oe"], 1)
                if (me := late(c, b, 0)) is not None:
                    n, tile, p = me
                    wait(e, "vp", n + 1)
                    wait(e, "sg", 4 * n - 4)
                    diag = vbd[p].rearrange("p h n -> p (h n)")[:, 0:NH * P].rearrange(
                        "p (k r) -> p k r", k=KD)
                    e.activation(vtok[:, p, :], half(0, 0, D), ACT.Copy).then_inc(s["vr"], 1)
                    for k in range(KD):
                        dst = diag_ap(vbd[p], k)
                        e.activation(dst, half(0, k * P).rearrange("p (h n) -> p h n", h=HP), ACT.Copy).then_inc(s["vr"], 1)
                if (me := late(c, b, 1)) is not None:
                    n, tile, p = me
                    wait(e, "oe", n + 1)
                    wait(e, "a", n - 1)
                    e.activation(sq[:, p], oT[:, p], ACT.Square).then_inc(s["sq"], 1)
                    wait(e, "a", n + 1)
                    e.activation(rs2[:, p, 0:1], ps[:, 7, D:D + 1], ACT.Sqrt, scale=1.0 / D, bias=epst[:, 1:2]).then_inc(s["r0"], 1)
                if (me := late(c, b, 2)) is not None:
                    n, tile, p = me
                    wait(e, "h2", n + 1)
                    e.activation(h2s[:, bass.ds(tile, 1), 0:D], h2[:, p:p + 1, :], ACT.Copy).then_inc(s["hi"], 1)
                if (me := late(c, b, 1)) is not None:
                    n, tile, p = me
                    wait(e, "mv2", n + 1)
                    e.activation(rs2[:, p, 2:3], mv2[:, p, 1:2], ACT.Sqrt, bias=epst[:, 0:1]).then_inc(s["sd2"], 1)
                if (me := late(c, b, 2)) is not None:
                    n, tile, p = me
                    wait(e, "tb", n + 1)
                    wait(e, "lg", n - 1)
                    e.activation(h2T[:, p], half(4, 0, D).rearrange("p (k n) -> p k n", k=KD), ACT.Copy).then_inc(s["hte"], 1)
                    wait(e, "lg", n + 1)
                    e.activation(logit[:, bass.ds(tile, 1), :], half(4, D, NE).unsqueeze(1), ACT.Copy).then_inc(s["le"], 1)


            def split_high(x, q):
                wait(e, "cvd", NPIECE * x)
                e.wait_ge(s_ld[q], 16 * x + 16)
                e.activation(wx[:, bass.ds(x * SLOT + weights(q, 0), PIECE)], stage(x, q), ACT.Copy).then_inc(s["cva"], 1)

            def step(f, p, routed=None):
                if (y := tile_at(f, 2, p, routed)) and y[2]:
                    g, q, _ = y
                    wait(e, "ht", g - NT + 1)
                    if not isinstance(g, int) or g >= NT + 2:
                        wait(e, "yd", g - 1)
                    e.activation(hsT[q], ps[:, 5, :].bitcast(bf16), ACT.Copy).then_inc(s["he2"], 1)
                if (y := tile_at(f, 2, p, routed)) and y[2]:
                    g, q, _ = y
                    wait(e, "meta0", g - NT + 1)
                    if not isinstance(g, int) or g >= NT + 2:
                        wait(e, "ye", g - 1)
                    e.activation(gbw[q].unsqueeze(1), modr[:, 0, 3:4, :], ACT.Copy,
                                 scale=wrow[:, 0, bass.ds(g - NT, 1)]).then_inc(s["gw"], 1)
                if (y := tile_at(f, 0, p, routed)):
                    g, q, _ = y
                    shared = not y[2]
                    wait(e, "g", g + 1)
                    wait(e, "hh", g - 1)
                    e.activation(sg[q], ps[:, 1 + 2 * q, :], ACT.Silu).then_inc(s["sl"], 1)
                    if shared and q == 1:
                        split_high((g - 1) // 2, 2)
                    elif shared and not (isinstance(g, int) and g == 0):
                        split_high(g // 2, 0)
                    wait(e, "hh", g + 1)
                    inner_free(e, g, y[2])
                    if isinstance(g, int) and g == 0:
                        e.wait_ge(s["a"], NT)
                    e.activation(hs[q][:, 0:FF], hf[q], ACT.Copy).then_inc(s["hi2"], 1)
                    if shared and q == 0 and not (isinstance(g, int) and g == 0):
                        split_high(g // 2, 1)

            def ahead():
                e.wait_ge(s["u"], NT)
                e.wait_ge(s["in_"], NT)
                step(-1, 1)
                step(0, 0)

            def extra(f):
                if f == -1:
                    e.wait_ge(s["rt"], 2)
                    e.activation(ex, lm, ACT.Exp).then_inc(s["rex"], 1)
                if f == 0:
                    split_high(0, 0)
                    split_high(0, 1)
            steps(e, step_attention, ahead)
            pipeline(e, step, extra, begin=1)

        @block.vector
        def _(e):
            e.memset(epst[:, 0:1], LN_EPS).then_inc(s["v1"], 1)
            e.memset(epst[:, 1:2], RMS_EPS).then_inc(s["v1"], 1)
            e.wait_ge(s["c"], 32)
            e.tensor_copy(identb[:], ident[:]).then_inc(s["v0"], 1)
            e.tensor_copy(onesb[:], ones[:]).then_inc(s["v0"], 1)
            e.tensor_scalar(ustrict[:], lag, 1.0, None, ALU.is_ge).then_inc(s["v0"], 1)
            e.tensor_scalar(nsl[:, 0:NH], slr[:, :], -1.0, None, ALU.mult).then_inc(s["v0"], 1)
            e.tensor_scalar(nsl[:, NH:NH + KD], slc[:, :], -1.0, None, ALU.mult).then_inc(s["v0"], 1)
            e.tensor_scalar(npos[:, :], posn[:, P:P + 1], -1.0, None, ALU.mult).then_inc(s["v0"], 1)
            e.wait_ge(s["a0"], 1)
            e.tensor_copy(cbc, cs[:].unsqueeze(3).to_broadcast([P, KD, B, P])).then_inc(s["ccb"], 1)
            e.wait_ge(s["mr"], 1)
            pm = half(6, 0, 2 * KD * B).rearrange("p (a k b) -> p a k b", a=2, k=KD)
            e.tensor_copy(modc[:, 0], pm[:, 0])
            e.tensor_scalar(modc[:, 1], pm[:, 1], 1.0, None, ALU.add).then_inc(s["mc"], 1)
            for g in range(NT // GT):
                e.wait_ge(s_x[g], 16)
                for i in range(GT * g, GT * (g + 1)):
                    e.bn_stats(st1[:, i, :], xres[:, i, :]).then_inc(s["st"], 1)
            e.wait_ge(s["st"], NT)
            for i in range(NT):
                e.bn_aggr(mv1[:, i, :], st1[:, i, :]).then_inc(s["mv"], 1)
            e.wait_ge(s["sdv"], 1)
            e.reciprocal(rs1[:, 1, :], rs1[:, 0, :]).then_inc(s["rs"], 1)
            e.wait_ge(s["rs"], 1)
            e.scalar_tensor_tensor(out=rs1[:, 2, :], in0=mv1[:, :, 0], scalar=-1.0, in1=rs1[:, 1, :],
                                   op0=ALU.mult, op1=ALU.mult).then_inc(s["nm"], 1)
            e.wait_ge(s["nm"], 1)

            def normalise(i):
                for b in range(B):
                    for j in range(GT):
                        n = GT * (B * i + b) + j
                        tile = GT * (i + NT // GT // B * b) + j
                        wait(e, "tp", n - 1)
                        e.tensor_scalar(xn[:, j % 2:j % 2 + 1, :], xres[:, bass.ds(tile, 1), :], rs1[:, 1, bass.ds(tile, 1)],
                                        rs1[:, 2, bass.ds(tile, 1)], ALU.mult, ALU.add).then_inc(s["xn"], 1)
            loop(e, NT // GT // B, normalise)
            e.wait_ge(s["mr"], 2)
            for b in range(B):
                src = ps[:, 2 + 2 * b:4 + 2 * b, :].rearrange("p a (c n) -> p (a c) n", c=2)
                e.tensor_copy(modr[:, b, 1:2, :], src[:, 1:2])
                e.tensor_scalar(modr[:, b, 2:3, :], src[:, 2:3], 1.0, None, ALU.add).then_inc(s["vm"], 1)
                for j in (0, 3):
                    e.tensor_scalar(sgn[:, b, j // 3, :], src[:, j], 0.0, 2.0, ALU.is_ge, ALU.mult).then_inc(s["va"], 1)
                    e.wait_ge(s["va"], 2 * b + j // 3 + 1)
                    e.scalar_tensor_tensor(out=mag[:, b, j // 3, :], in0=sgn[:, b, j // 3, :], scalar=-1.0,
                                           in1=src[:, j], op0=ALU.add, op1=ALU.mult).then_inc(s["vb"], 1)
            e.wait_ge(s["vb"], 2 * B)
            e.tensor_scalar(mag, mag, 0.25, None, ALU.max).then_inc(s["vb"], 1)
            e.wait_ge(s["vb"], 2 * B + 1)
            for b in range(B):
                for j in (0, 3):
                    e.scalar_tensor_tensor(out=modr[:, b, j, :], in0=sgn[:, b, j // 3, :], scalar=-1.0,
                                           in1=mag[:, b, j // 3, :], op0=ALU.add, op1=ALU.mult).then_inc(s["vm"], 1)
            e.wait_ge(s["vm"], 3 * B)
            e.wait_ge(s["w"], 32)
            for b in range(B):
                e.tensor_tensor(woutg[:, b], wout, modr[:, b, 0:1, :].to_broadcast([P, KD, D]), ALU.mult).then_inc(s["v3"], 1)
            e.wait_ge(s["a1"], NH)
            e.tensor_tensor(decay, decay, causal[:, :].unsqueeze(1).to_broadcast([P, NH, P]), ALU.mult).then_inc(s["lz"], 1)
            with e.Fori(0, NT // GT // B) as i:
                for b in range(B):
                    g = i + NT // GT // B * b
                    for k in range(KD):
                        e.wait_ge(s["qkp"], 3 * KD * (B * i + b) + 2 * KD + k + 1)
                        e.tensor_copy(uT[:, k, bass.ts(g, GT * P)], ps[:, 2 * KD + k, :]).then_inc(s["ue"], 1)
            e.wait_ge(s["lz"], 1)
            e.wait_ge(s["p2"], 1)
            e.wait_ge(s["z1"], 3)

            def scores(n, j):
                wait(e, "s", 4 * n + j + 1)
                wait(e, "sg", 4 * n + j - 3)
                e.tensor_tensor(sd[:, j], ps[:, 2 + j % 2, :].rearrange("p (h n) -> p h n", h=4),
                                decay[:, 4 * j:4 * j + 4, :], ALU.mult).then_inc(s["sdm"], 1)

            def step_attention(c, b):
                me, pr = late(c, b, 0), late(c, b, 1)
                if me is not None:
                    n, tile, p = me
                    wait(e, "kp", n + 1)
                    wait(e, "sg", 4 * n - 4)
                    e.tensor_tensor(kdec[:, p, :], half(1, 0, D), dk[:].rearrange("p h d -> p (h d)"), ALU.mult).then_inc(s["kd"], 1)
                    scores(n, 0)
                    scores(n, 1)
                if pr is not None:
                    m, mt, q = pr
                    wait(e, "r0", m + 1)
                    e.reciprocal(rs2[:, q, 1:2], rs2[:, q, 0:1]).then_inc(s["r"], 1)
                    wait(e, "r", m + 1)
                    e.scalar_tensor_tensor(out=xres[:, bass.ds(mt, 1), :], in0=half(7, 0, D).unsqueeze(1), scalar=rs2[:, q, 1:2],
                                           in1=xres[:, bass.ds(mt, 1), :], op0=ALU.mult, op1=ALU.add).then_inc(s["x1"], 1)
                if pr is not None:
                    wait(e, "x1", m + 1)
                if me is not None:
                    scores(n, 2)
                if pr is not None:
                    e.bn_stats(st2[:, q, :], xres[:, bass.ds(mt, 1), :]).then_inc(s["bs"], 1)
                    wait(e, "bs", m + 1)
                    wait(e, "nm2", m - 1)
                if me is not None:
                    scores(n, 3)
                if pr is not None:
                    e.bn_aggr(mv2[:, q, :], st2[:, q, :]).then_inc(s["mv2"], 1)
                    wait(e, "sd2", m + 1)
                    e.reciprocal(rs2[:, q, 3:4], rs2[:, q, 2:3]).then_inc(s["rc2"], 1)
                if me is not None:
                    wait(e, "u", n + 1)
                    e.tensor_tensor(um, half(6, 0, D).rearrange("p (k n) -> p k n", k=KD), headm[:], ALU.mult).then_inc(s["umm"], 1)
                if pr is not None:
                    wait(e, "rc2", m + 1)
                    e.scalar_tensor_tensor(out=rs2[:, q, 4:5], in0=mv2[:, q, 0:1], scalar=-1.0, in1=rs2[:, q, 3:4],
                                           op0=ALU.mult, op1=ALU.mult).then_inc(s["nm2"], 1)
                if me is not None:
                    wait(e, "umm", n + 1)
                    wait(e, "in_", n + 1)
                    for k in range(KD):
                        e.scalar_tensor_tensor(out=kv[:, p, k, :], in0=kv[:, p, k, :], scalar=bdec[:, k:k + 1],
                                               in1=um[:, k, :], op0=ALU.mult, op1=ALU.add).then_inc(s["kvv"], 1)
                if pr is not None:
                    wait(e, "nm2", m + 1)
                    wait(e, "h2", m - 1)
                    e.tensor_scalar(xn2[:, q:q + 1, :], xres[:, bass.ds(mt, 1), :], rs2[:, q, 3:4], rs2[:, q, 4:5],
                                    ALU.mult, ALU.add).then_inc(s["xn2"], 1)
            count = [0]

            def link(ins):
                ins.then_inc(s["rt"], 1)
                count[0] += 1
                e.wait_ge(s["rt"], count[0])

            def over(a):
                return a.unsqueeze(2).to_broadcast([P, NT, NE])

            def routing():
                revb = rev[:, :].unsqueeze(1).to_broadcast([P, NT, NE])
                yield link(e.tensor_reduce(mx, logit[:], AX.X, ALU.max))
                yield link(e.tensor_tensor(lm, logit[:], over(mx), ALU.subtract))
                e.wait_ge(s["rex"], 1)
                yield link(e.tensor_reduce(sm, ex, AX.X, ALU.add))
                yield link(e.reciprocal(rsm, sm))
                yield link(e.tensor_tensor(pr, ex, over(rsm), ALU.mult))

                def first_largest(probs, largest, mark, onehot):
                    yield link(e.tensor_reduce(largest, probs, AX.X, ALU.max))
                    yield link(e.tensor_tensor(eq, probs, over(largest), ALU.is_equal))
                    yield link(e.tensor_tensor(pick, eq, revb, ALU.mult))
                    yield link(e.tensor_reduce(mark, pick, AX.X, ALU.max))
                    yield link(e.tensor_tensor(onehot, revb, over(mark), ALU.is_equal))

                yield from first_largest(pr, p1, f1, m1)
                yield link(e.scalar_tensor_tensor(out=pr2, in0=m1, scalar=-2.0, in1=pr, op0=ALU.mult, op1=ALU.add))
                yield from first_largest(pr2, p2, f2, m2)
                yield link(e.tensor_tensor(picked, m1.rearrange("p t e -> p (t e)"), m2.rearrange("p t e -> p (t e)"), ALU.add))
                yield link(e.tensor_tensor(den, p1, p2, ALU.add))
                yield link(e.reciprocal(rden, den))
                meta = h2s[:, :, 2 * D:ROW].bitcast(f32)
                e.tensor_tensor(meta[:, :, 0], p1, rden, ALU.mult)
                e.tensor_copy(meta[:, :, 1], tok1[:])
                e.tensor_tensor(pool_w2[:, :, 0], p2, rden, ALU.mult)
                yield link(e.tensor_copy(pool_w2[:, :, 1], tok1[:]))
                e.wait_ge(s["rp"], 1)
                yield link(e.tensor_scalar(tiles_i, half(5, NT * NE, NE), float(P - 1), None, ALU.add))
                yield link(e.tensor_scalar(tiles_s, tiles_i, 7, None, ALU.arith_shift_right))
                yield link(e.tensor_copy(tiles_f, tiles_s))
                yield link(e.tensor_tensor_scan(tiles_end, ones[:, 0:NE], tiles_f, 0.0, ALU.mult, ALU.add))
                yield link(e.tensor_tensor(base, tiles_end, tiles_f, ALU.subtract))
                yield link(e.tensor_scalar(base, base, float(P), None, ALU.mult))
                yield link(e.tensor_tensor(pos, half(5, 0, NT * NE).rearrange("p (t e) -> p t e", t=NT),
                                     base.unsqueeze(1).to_broadcast([P, NT, NE]), ALU.add))
                yield link(e.tensor_tensor(eq, pos, m1, ALU.mult))
                e.tensor_reduce(mx, eq, AX.X, ALU.add)
                yield link(e.tensor_tensor(pick, pos, m2, ALU.mult))
                yield link(e.tensor_reduce(sm, pick, AX.X, ALU.add))
                e.tensor_copy(idx1, mx)
                yield link(e.tensor_copy(idx2, sm))
                yield link(e.tensor_tensor(gej[0:1], jt[:, :].unsqueeze(2).to_broadcast([1, NG, NE]),
                                     tiles_end[0:1].unsqueeze(1).to_broadcast([1, NG, NE]), ALU.is_ge))
                yield link(e.tensor_reduce(slot_f[0:1], gej[0:1], AX.X, ALU.add))
                yield link(e.tensor_scalar(slot_f[0:1], slot_f[0:1], float(NE - 1), float(SLOT), ALU.min, ALU.mult))
                yield link(e.tensor_copy(slot_of[:], slot_f[0:1]))
                assert count[0] == RT_DONE, count[0]

            def split_low(x, q):
                wait(e, "cvd", NPIECE * x)
                e.wait_ge(s["cva"], NPIECE * x + q + 1)
                if q == 1:
                    wait(e, "cvp", min(x, XPOOL) if isinstance(x, int) else XPOOL)
                e.tensor_tensor(wx[:, bass.ds(x * SLOT + weights(q, 1), PIECE)], stage(x, q),
                                wx[:, bass.ds(x * SLOT + weights(q, 0), PIECE)], ALU.subtract).then_inc(
                                    s["cvd"], 2 if q == 1 and isinstance(x, int) and x < XPOOL else 1)

            def take_rows(f, p, routed):
                if (y := tile_at(f, -1, p, routed)):
                    g, q, _ = y
                    wait(e, "xt", g + 1)
                    wait(e, "u2", g - 1)
                    e.tensor_copy(xT[q].bitcast(u32), ps[:, 0, 0:D].bitcast(u32)).then_inc(s["xe"], 1)
                if (y := tile_at(f, -1, p, routed)) and y[2]:
                    g, q, _ = y
                    m = xg[q][:, 2 * D:ROW].bitcast(f32)
                    j = bass.ds(g - NT, 1)
                    wait(e, s_xg[q], 8 * (g - q) + 16)
                    wait(e, "meta0", g - NT)
                    e.tensor_scalar(zer[:, 0:1], m[:, 1:2], 0.0, dummy[:, 0:1], ALU.is_equal, ALU.mult).then_inc(s["ge"], 1)
                    e.tensor_scalar(wrow[:, 1, j], m[:, 1:2], float(S), m[:, 0:1], ALU.is_gt, ALU.mult).then_inc(s["ge"], 1)
                    wait(e, "ge", 2 * (g - NT + 1))
                    e.tensor_tensor(wrow[:, 0, j], m[:, 0:1], wrow[:, 1, j], ALU.subtract)
                    e.scalar_tensor_tensor(out=dst_i[:, j], in0=m[:, 1:2], scalar=-1.0, in1=zer[:, 0:1],
                                           op0=ALU.add, op1=ALU.add).then_inc(s["meta0"], 1)

            def step(f, p, routed=None):
                if not late_rows(f):
                    take_rows(f, p, routed)
                if (y := tile_at(f, 1, p, routed)):
                    g, q, _ = y
                    wait(e, "hi2", g + 1)
                    e.tensor_tensor(hs[q][:, FF:2 * FF], hf[q], hs[q][:, 0:FF], ALU.subtract).then_inc(s["lo2"], 1)
                if (y := tile_at(f, 0, p, routed)):
                    g, q, _ = y
                    shared = not y[2]
                    if shared and q == 1:
                        split_low((g - 1) // 2, 1)
                    wait(e, "u2", g + 1)
                    wait(e, "sl", g + 1)
                    e.tensor_tensor(hf[q], ps[:, 2 + 2 * q, :], sg[q], ALU.mult).then_inc(s["hh"], 1)
                    if shared and q == 0 and not (isinstance(g, int) and g == 0):
                        split_low(g // 2, 0)
                    if shared and q == 1 and not (isinstance(g, int) and g < 2 * XPOOL):
                        split_low((g - 1) // 2, 2)
                if (y := tile_at(f, 3, p, routed)):
                    g, q, _ = y
                    if y[2]:
                        r = g - NT
                        wait(e, "gw", r + 1)
                        e.scalar_tensor_tensor(out=gbw[q].unsqueeze(1), in0=modr[:, 1, 3:4, :], scalar=wrow[:, 1, bass.ds(r, 1)],
                                               in1=gbw[q].unsqueeze(1), op0=ALU.mult, op1=ALU.add).then_inc(s["gy"], 1)
                        wait(e, "yd", g + 1)
                        wait(e, "gy", g + 1)
                        if isinstance(g, int) and g < NT + 2:
                            e.wait_ge(s_st[q], 16 * NT // 2)
                        else:
                            wait(e, "acc", 16 * (g - 2 - NT + 1))
                        e.tensor_tensor(yb[q], ps[:, 6 + q, 0:D], gbw[q], ALU.mult).then_inc(s["ye"], 1)
                    else:
                        wait(e, s_st[q], 8 * (g - q))
                        wait(e, "yd", g + 1)
                        if isinstance(g, int) and g == 0:
                            e.wait_ge(s["h2"], NT)
                        e.tensor_tensor(yb[q], ps[:, 6 + q, 0:D], modr[:, q, 3, :], ALU.mult).then_inc(s["gy"], 1)
                        wait(e, "gy", g + 1)
                        e.tensor_tensor(yb[q].unsqueeze(1), yb[q].unsqueeze(1), xres[:, bass.ds(place(g, q), 1), :],
                                        ALU.add).then_inc(s["ye"], 1)
                if late_rows(f):
                    take_rows(f, p, routed)

            def ahead():
                e.wait_ge(s["u"], NT)
                e.wait_ge(s["in_"], NT)
                e.wait_ge(s["kvv"], KD * NT)
                step(-1, 1)
                step(0, 0)
            steps(e, step_attention, ahead)
            attention_over(e)
            e.wait_ge(s["cc"], 16)
            todo = routing()
            share = {-1: 8, 0: 9, 1: 6, 2: 6, 3: 6, 4: 2, 5: 2}

            def extra(f):
                for _ in range(share[f]):
                    next(todo, None)
                if f == 0:
                    split_low(0, 0)
            pipeline(e, step, extra, begin=1)
            assert not list(todo)

        @block.tensor
        def _(e):
            e.wait_ge(s["a0"], 1)
            e.wait_ge(s["mod"], 16)
            for a in range(2):
                for k in range(KD):
                    for kk in range(KD):
                        ins = e.matmul(half(6, (a * KD + k) * B, B), wmod[:, kk, (a * KD + k) * P:(a * KD + k + 1) * P],
                                       cs[:, kk, :], start=kk == 0, stop=kk == KD - 1)
            ins.then_inc(s["mr"], 1)
            e.wait_ge(s["ccb"], 1)
            for b in range(B):
                for a in range(2):
                    for kk in range(KD):
                        ins = e.matmul(ps[:, 2 + 2 * b + a, :], cbc[:, kk, b, :],
                                       wmod[:, kk, 2 * D + 512 * a:2 * D + 512 * (a + 1)], start=kk == 0, stop=kk == KD - 1)
            ins.then_inc(s["mr"], 1)

            def turn(i):
                for b in range(B):
                    for j in range(GT):
                        n = GT * (B * i + b) + j
                        e.wait_ge(s["xn"], n + 1)
                        if j == 0:
                            wait(e, "he", B * i + b - 1)
                        for k in range(KD):
                            ins = e.transpose(half(6 * b + k, j * P), xn[:, j % 2, k * P:(k + 1) * P], ident[:])
                        ins.then_inc(s["tp"], 1)
            e.wait_ge(s["c"], 32)
            e.wait_ge(s["mc"], 1)
            loop(e, NT // GT // B, turn)
            e.wait_ge(s["w"], 32)
            e.wait_ge(s["he"], NT // GT)
            e.wait_ge(s["vm"], 3 * B)

            def project(i):
                for b in range(B):
                    g = i + NT // GT // B * b
                    for j in range(3 * KD):
                        done = B * i + b
                        if j < 2 * KD:
                            wait(e, "qe", 2 * KD * done - 2 * KD + j + 1 if not isinstance(done, int) or done else 0)
                        else:
                            wait(e, "ue", KD * done - KD + (j - 2 * KD) + 1 if not isinstance(done, int) or done else 0)
                        col = j * P if j < 2 * KD else 3 * D + (j - 2 * KD) * P
                        for kk in range(KD):
                            ins = e.matmul(ps[:, j, :], wqkvu[:, kk, col:col + P], hT[:, kk, bass.ts(g, GT * P)],
                                           start=kk == 0, stop=kk == KD - 1)
                        ins.then_inc(s["qkp"], 1)
            loop(e, NT // GT // B, project)
            e.wait_ge(s["qe"], 2 * KD * NT // GT)
            e.wait_ge(s["ue"], KD * NT // GT)
            e.wait_ge(s["v3"], B)

            def qk(n, tile, p, j):
                wait(e, "sdm", 4 * n + j - 1)
                if j == 0:
                    wait(e, s_qb[p], 16 * HP * (tile - NC * p + 1))
                k = j // 2
                e.matmul(ps[:, 2 + j % 2, :], kh[p][:, k, :],
                         qbd[p][:, k, 4 * (j % 2):4 * (j % 2) + 4, :].rearrange("p h n -> p (h n)"),
                         start=True, stop=True).then_inc(s["s"], 1)

            def inter(n, p, k):
                if k == 0:
                    wait(e, "oe", n)
                    wait(e, "qd", n + 1)
                    wait(e, "kvv", KD * (n - 1))
                ins = e.matmul(half(5, k * P), kv[:, p, k, :], qdec[:, p, k, :], start=True, stop=False)
                if k == 1:
                    ins.then_inc(s["in_"], 1)

            def values(n, p, j):
                wait(e, "sdm", 4 * n + j + 1)
                k = j // 2
                for h in range(4):
                    ins = e.matmul(half(5, k * P), vbd[p][:, 4 * j + h, :], sd[:, j, h, :],
                                   start=False, stop=j % 2 == 1 and h == 3)
                ins.then_inc(s["sg"], 1)

            def step_attention(c, b):
                me, pr, pp = late(c, b, 0), late(c, b, 1), late(c, b, 2)
                if me is not None:
                    n, tile, p = me
                    wait(e, "vr", 3 * n)
                    wait(e, "kh", n + 1)
                    for kk in range(KD):
                        ins = e.matmul(half(0, 0, D), kh[p][:, KD + kk, :], wqkvu[:, kk, 2 * D:3 * D],
                                       start=kk == 0, stop=kk == KD - 1)
                    ins.then_inc(s["vp"], 1)
                    wait(e, "kd", n)
                    for k in range(KD):
                        ins = e.transpose(half(1, k * P), kh[p][:, k, :], ident[:])
                    ins.then_inc(s["kp"], 1)
                    qk(n, tile, p, 0)
                    qk(n, tile, p, 1)
                if pr is not None:
                    m, mt, q = pr
                    wait(e, "sq", m + 1)
                    wait(e, "y", m + 1)
                    wait(e, "x1", m)
                    for k in range(KD):
                        e.matmul(half(7, D), sq[:, q, k, :], ones[:], start=k == 0, stop=k == KD - 1)
                    for k in range(KD):
                        ins = e.matmul(half(7, 0, D), yT[:, q, k, :], woutg[:, q, k, :], start=k == 0, stop=k == KD - 1)
                    ins.then_inc(s["a"], 1)
                if me is not None:
                    inter(n, p, 0)
                    wait(e, "vr", 3 * n + 3)
                    values(n, p, 0)
                    qk(n, tile, p, 2)
                    values(n, p, 1)
                    qk(n, tile, p, 3)
                if pp is not None:
                    m2, _, q2 = pp
                    wait(e, "h2", m2 + 1)
                    wait(e, "le", m2)
                    for k in range(KD):
                        ins = e.transpose(half(4, k * P), h2[:, q2, k * P:(k + 1) * P], ident[:])
                    ins.then_inc(s["tb"], 1)
                if me is not None:
                    wait(e, "kd", n + 1)
                    wait(e, "umm", n)
                    for k in range(KD):
                        ins = e.matmul(half(6, k * P), kdec[:, p, k * P:(k + 1) * P], vtok[:, p, k * P:(k + 1) * P],
                                       start=True, stop=True)
                    ins.then_inc(s["u"], 1)
                    inter(n, p, 1)
                    values(n, p, 2)
                    values(n, p, 3)
                if pp is not None:
                    wait(e, "hte", m2 + 1)
                    for k in range(KD):
                        ins = e.matmul(half(4, D), h2T[:, q2, k, :], wg[:, k, :], start=k == 0, stop=k == KD - 1)
                    ins.then_inc(s["lg"], 1)


            def turn_rows(g, p, routed):
                wait(e, s_xg[p], 8 * (g - p) + 16)
                wait(e, "xe", g)
                for m in range(4):
                    ins = e.transpose(ps[:, 0, 0:D].bitcast(bf16)[:, m * P:(m + 1) * P], xg[p][:, m * P:(m + 1) * P], identb[:])
                ins.then_inc(s["xt"], 1)

            def slot(g, routed):
                if not routed:
                    return SHARED_AT
                return e.value_load(slot_of[0:1, bass.ds(g - NT, 1)], min_val=0, max_val=(NE - 1) * SLOT)

            PASSES = ((0, 0), (0, 1), (1, 0))

            def gate_up(g, p, routed):
                at_ = slot(g, routed)
                wait(e, "xe", g + 1)
                for part, name, free in ((0, "g", "sl"), (1, "u2", "hh")):
                    wait(e, free, g - 1)
                    n = 0
                    if not routed:
                        for m in range(KF):
                            for n in range(3 * KD):
                                k, (a, w) = n // 3, PASSES[n % 3]
                                off = at_ + weights(part, w) + k * FF + m * P
                                ins = e.matmul(half(1 + 2 * p + part, m * P), wx[:, off:off + P],
                                               xT[p][:, (2 * a + k) * P:(2 * a + k + 1) * P],
                                               start=n == 0, stop=n == 3 * KD - 1)
                        ins.then_inc(s[name], 1)
                        continue
                    for k in range(KD):
                        for a, w in PASSES:
                            ins = e.matmul(ps[:, 1 + 2 * p + part, :], xT[p][:, (2 * a + k) * P:(2 * a + k + 1) * P],
                                           wx[:, bass.ds(at_ + weights(part, w) + k * FF, FF)],
                                           start=n == 0, stop=n == 3 * KD - 1)
                            n += 1
                    ins.then_inc(s[name], 1)

            def turn_inner(g, p):
                wait(e, "lo2", g + 1)
                wait(e, "he2", g - NT)
                for m in range(2 * KF):
                    ins = e.transpose(ps[:, 5, :].bitcast(bf16)[:, m * P:(m + 1) * P], hs[p][:, m * P:(m + 1) * P], identb[:])
                ins.then_inc(s["ht"], 1)

            def down(g, p, routed):
                at_ = slot(g, routed)
                inner = hsT[p] if routed else hs[p]
                if routed:
                    wait(e, "he2", g - NT + 1)
                else:
                    wait(e, "lo2", g + 1)
                wait(e, "ye", g - 1)
                n = 0
                for k in range(KF):
                    for a, w in PASSES:
                        ins = e.matmul(ps[:, 6 + p, 0:D], inner[:, (KF * a + k) * P:(KF * a + k + 1) * P],
                                       wx[:, bass.ds(at_ + weights(2, w) + k * D, D)],
                                       start=n == 0, stop=n == 3 * KF - 1)
                        n += 1
                ins.then_inc(s["yd"], 1)

            def step(f, p, routed=None):
                if (y := tile_at(f, -1, p, routed)) and not late_rows(f):
                    turn_rows(*y)
                if (y := tile_at(f, 0, p, routed)):
                    if isinstance(f, int) and f == NT:
                        e.wait_ge(s["cvd"], NPIECE * NE)
                        e.wait_ge(s["cvp"], XPOOL)
                        e.wait_ge(s["rt"], RT_DONE)
                    gate_up(*y)
                if (y := tile_at(f, 2, p, routed)):
                    down(*y)
                if (y := tile_at(f, 1, p, routed)) and y[2]:
                    turn_inner(y[0], y[1])
                if late_rows(f):
                    turn_rows(NT, NT % 2, True)

            def rank(f):
                if f != 1:
                    return
                e.wait_ge(s["rt"], RT_PICKED)
                e.matmul(half(5, 0, NT * NE), ustrict[:], picked, start=True, stop=False, skip_group_check=True)
                for k in range(1, NT):
                    e.matmul(half(5, k * NE, (NT - k) * NE), onesb[:], picked[:, 0:(NT - k) * NE],
                             start=False, stop=False, skip_group_check=True)
                for k in range(NT):
                    ins = e.matmul(half(5, NT * NE, NE), onesb[:], picked[:, k * NE:(k + 1) * NE],
                                   start=False, stop=k == NT - 1, skip_group_check=True)
                ins.then_inc(s["rp"], 1)

            def ahead():
                e.wait_ge(s["vr"], 3 * NT)
                e.wait_ge(s["kd"], NT)
                e.wait_ge(s["sdm"], 4 * NT)
                step(-1, 1)
                step(0, 0)
            steps(e, step_attention, ahead)
            attention_over(e)
            e.wait_ge(s["x1"], NT)
            pipeline(e, step, rank, begin=1)



KEPT_PARTS = dict(ident=P, ones=P, slr=NH, slc=KD, headm=KD * P, wg=KD * P, rev=NE, tok1=NT, dummy=1)
KEPT = sum(KEPT_PARTS.values())


def constants():
    f = np.float32
    m = np.arange(P)
    same = (m[:, None] // DH == m[None, :] // DH).astype(f)
    return dict(
        lag=np.maximum(m[None, :] - m[:, None], 0).astype(f),
        causal=(m[None, :] >= m[:, None]).astype(f),
        posn=np.concatenate([np.tile(m + 1, (P, 1)), (P - 1 - m)[:, None]], 1).astype(f),
        headm=np.concatenate([same] * KD, 1),
        ident=np.eye(P, dtype=f),
        ones=np.ones((P, P), f),
        rev=np.tile(NE - np.arange(NE), (P, 1)).astype(f),
        tok1=(np.arange(NT)[None, :] * P + m[:, None] + 1).astype(f),
        dummy=(B * S + 1 + m)[:, None].astype(f),
        jt=np.arange(NG)[None, :].astype(f),
    )


def layout(i):
    def rows(w):
        return np.ascontiguousarray(w.reshape(-1, P, w.shape[-1]).transpose(1, 0, 2))

    slope = i["L0_attn_slope_rate"].reshape(NH)
    a = dict(
        x=i["L0_attn_x"].reshape(B * S, D),
        cT=rows(i["L0_c"].T),
        slr=np.ascontiguousarray(np.broadcast_to(slope, (P, NH))),
        slc=np.ascontiguousarray(np.repeat(slope, DH).reshape(KD, P).T),
        wmod=rows(i["L0_wmod"]),
        wqkvu=rows(i["L0_attn_W_qkvu"].T),
        wout=rows(i["L0_attn_W_out"].T),
    )
    a["wg"] = np.zeros((P, KD, P), np.float32)
    a["wg"][:, :, 0:NE] = rows(i["L0_ffn_wg"].T)
    gate = [*i["L0_ffn_ex_gate"], i["L0_ffn_sh_gate"]]
    up = [*i["L0_ffn_ex_up"], i["L0_ffn_sh_up"]]
    down = [*i["L0_ffn_ex_down"], i["L0_ffn_sh_down"]]
    a["wexp"] = np.stack([np.stack([rows(w.T).reshape(P, PIECE) for w in three], 1)
                          for three in zip(gate, up, down)])
    a["wg"] = a["wg"].reshape(P, KD * P)
    a.update(constants())
    a["kept"] = np.concatenate([a.pop(n) for n in KEPT_PARTS], 1)
    a["decay_tables"] = np.concatenate([a.pop(n) for n in ("lag", "causal", "posn")], 1)
    return a


def kernel(**inputs):
    import concourse.bacc as bacc
    from concourse.bass_utils import run_bass_kernel_spmd

    nc = bacc.Bacc("TRN2", target_bir_lowering=False, num_devices=1)
    arrays = layout({k: np.asarray(v) for k, v in inputs.items()})
    t = {n: nc.dram_tensor("in_" + n, a.shape, mybir.dt.from_np(a.dtype), kind="ExternalInput").ap()
         for n, a in arrays.items()}
    t["xg"] = nc.dram_tensor("dispatched", [NG * P, ROW // 2], mybir.dt.uint32).ap()
    t["acc"] = nc.dram_tensor("expert_sum", [ACC, D], mybir.dt.float32).ap()
    t["out"] = nc.dram_tensor("out", [B * S, D], mybir.dt.float32, kind="ExternalOutput").ap()
    build(nc, t)
    r = run_bass_kernel_spmd(nc, [{"in_" + n: a for n, a in arrays.items()}], core_ids=[0])
    return r.results[0]["out"].reshape(B, S, D)
```

```python
import numpy as np
from contextlib import ExitStack

import concourse.bass as bass
from concourse import mybir

P = 128
B, S, D = 2, 1024, 256
KD = D // P
NH, DH = 16, 16
HP = P // DH
NT = B * S // P
NC = S // P
NE, FF, NSH = 8, 512, 8
KF = FF // P
TOP = 2
PIECE = KD * FF
NPIECE = 3
SLOT = 2 * NPIECE * PIECE
SHARED_AT = NE * SLOT + 4 * NH * P
NG = TOP * NT + NE - 1
ROW = 2 * D + 4
ACC = B * S + P
LN_EPS, RMS_EPS = 1e-5, 1e-6
GT = 4
XPOOL = 3
RT_PICKED, RT_PLACED, RT_DONE = 17, 31, 35


def build(nc, t):
    f32, bf16, i32, u32 = mybir.dt.float32, mybir.dt.bfloat16, mybir.dt.int32, mybir.dt.uint32
    ALU, ACT, AX = mybir.AluOpType, mybir.ActivationFunctionType, mybir.AxisListType
    ctx = ExitStack()
    with ctx:
        def sb(name, shape, dt=f32):
            return ctx.enter_context(nc.sbuf_tensor(name, shape, dt))

        def sem(name):
            return ctx.enter_context(nc.semaphore(name))

        wx = sb("wx", [P, SHARED_AT + SLOT], bf16)
        att = wx[:, 0:NE * SLOT].bitcast(f32)
        at = [0]

        def in_att(n):
            at[0] += n
            return att[:, at[0] - n:at[0]]

        q_hl = in_att(KD * B * S).bitcast(bf16).rearrange("p (k t a n) -> p k t a n", k=KD, t=NT, a=2)
        k_hl = in_att(KD * B * S).bitcast(bf16).rearrange("p (a k n) -> p a k n", a=2, k=KD)
        h_hl = in_att(KD * B * S).bitcast(bf16).rearrange("p (a k n) -> p a k n", a=2, k=KD)
        qbd = [in_att(KD * HP * P).bitcast(bf16).rearrange("p (k h a n) -> p k h a n", k=KD, h=HP, a=2) for _ in range(2)]
        whole = in_att(4 * GT * P).rearrange("p (j n) -> p j n", j=4)
        wqkvu = in_att(KD * 4 * D).rearrange("p (k n) -> p k n", k=KD)
        sp = in_att(NH * P).bitcast(bf16).rearrange("p (a j h n) -> p a j h n", a=2, j=4, h=4)
        utok = in_att(2 * D).rearrange("p (a n) -> p a n", a=2)
        vp = in_att(2 * D).bitcast(bf16).rearrange("p (a b n) -> p a b n", a=2, b=2)
        xres = sb("xres", [P, NT, D])
        h2s = sb("h2s", [P, NT, ROW], bf16)
        w_parts = sb("w_hl", [P, KD * 4 * D])
        w_hl = w_parts[:].bitcast(bf16).rearrange("p (a k n) -> p a k n", a=2, k=KD)
        woutg = sb("woutg", [P, B, KD, D])
        kept = sb("kept", [P, KEPT])
        kept_at = dict(zip(KEPT_PARTS, np.cumsum([0, *KEPT_PARTS.values()]).tolist()))

        def keep(name):
            return kept[:, kept_at[name]:kept_at[name] + KEPT_PARTS[name]]

        ident, ones, rev, tok1, spare_row = (keep(n) for n in ("ident", "ones", "rev", "tok1", "spare_row"))
        slr, slc = keep("slr"), keep("slc")
        headm = keep("headm").rearrange("p (k n) -> p k n", k=KD)
        wg = keep("wg").rearrange("p (k n) -> p k n", k=KD)
        identb = sb("identb", [P, P], bf16)
        cT = sb("cT", [P, KD, B])
        cs = sb("cs", [P, KD, B])
        modc = sb("modc", [P, 2, KD, B])
        modr = sb("modr", [P, B, 4, D])
        dq = sb("dq", [P, KD, P])
        dk = sb("dk", [P, NH, DH])
        nsl = sb("nsl", [P, NH + KD])
        npos = sb("npos", [P, 1])
        bdec = sb("bdec", [P, KD])
        st1 = sb("st1", [P, NT, 6])
        mv1 = sb("mv1", [P, NT, 2])
        rs1 = sb("rs1", [P, 3, NT])
        st2 = sb("st2", [P, 2, 6])
        mv2 = sb("mv2", [P, 2, 2])
        rs2 = sb("rs2", [P, 2, 6])
        logit = sb("logit", [P, NT, NE])
        wmod = h2s[:].rearrange("p t d -> p (t d)").bitcast(f32)[:, 0:KD * 6 * D].rearrange("p (k n) -> p k n", k=KD)
        epst = sb("epst", [P, 2])
        tmp = sb("tmp", [P, 11 * 2 * D + D + ROW - 2 * D])
        used = [0]

        def carve(n, dt=f32):
            words = n if dt == f32 else n // 2
            used[0] += words
            return tmp[:, used[0] - words:used[0]] if dt == f32 else tmp[:, used[0] - words:used[0]].bitcast(dt)

        def two(n=D):
            return carve(2 * n).rearrange("p (a n) -> p a n", a=2)

        def two_t():
            return carve(2 * D).rearrange("p (a k n) -> p a k n", a=2, k=KD)

        xn = tmp[:, 0:4 * D].rearrange("p (a n) -> p a n", a=4)
        carve(ROW)
        kdec, vtok, qdec, kv = two(), two(), two_t(), two_t()
        um = carve(D).rearrange("p (k n) -> p k n", k=KD)
        ytok, sq, yT, xn2, h2, h2T = two(), two(), two_t(), two(), two(), two_t()
        used[0] = 0
        xg = [carve(ROW, bf16) for _ in range(2)]
        xT = [carve(2 * D, bf16) for _ in range(2)]
        sg = [carve(FF) for _ in range(2)]
        hf = [carve(FF) for _ in range(2)]
        hs = [carve(2 * FF, bf16) for _ in range(2)]
        yb = [carve(D) for _ in range(2)]
        hsT = [carve(2 * FF, bf16) for _ in range(2)]
        score = wx[:, NE * SLOT:SHARED_AT].bitcast(f32)
        decay = score[:, 0:NH * P].rearrange("p (h n) -> p h n", h=NH)
        sd = score[:, NH * P:2 * NH * P].rearrange("p (j h n) -> p j h n", j=4, h=4)

        def stage(x, q):
            if isinstance(x, int):
                at_ = (x + 1) * SLOT + 2 * q * PIECE
                return wx[:, at_:at_ + 2 * PIECE].bitcast(f32)
            return wx[:].bitcast(f32)[:, bass.ds((x + 1) * (SLOT // 2) + q * PIECE, PIECE)]

        early_stage = att[:, 0:NPIECE * PIECE]
        rt = w_parts[:]
        rused = [0]

        def route(n, dt=f32):
            rused[0] += n
            a = rt[:, rused[0] - n:rused[0]]
            return a if dt == f32 else a.bitcast(dt)

        def route3(dt=f32):
            return route(NT * NE, dt).rearrange("p (t e) -> p t e", t=NT)

        lm, ex, pr, eq, pick, m1, m2, pr2, pos = (route3() for _ in range(9))
        gbw = [rt[:, i * D:(i + 1) * D] for i in range(2)]
        mx, sm, rsm, p1, f1, p2, f2, den, rden = (route(NT) for _ in range(9))
        pool_w2 = route(2 * NT).rearrange("p (t a) -> p t a", t=NT)
        idx1, idx2 = route(NT, u32), route(NT, u32)
        picked = route(NT * NE // 2).bitcast(bf16)
        tiles_i, tiles_s = route(NE, i32), route(NE, i32)
        tiles_f, tiles_end, base = route(NE), route(NE), route(NE)
        gej = route(NG * NE).rearrange("p (j e) -> p j e", j=NG)
        slot_f = route(NG)
        slot_of = sb("slot_of", [1, NG], i32)
        wrow = sb("wrow", [P, B, NG])
        zer = sb("zer", [P, 1])
        dst_i = sb("dst_i", [P, NG], u32)
        ustrict = sb("ustrict", [P, P], bf16)
        onesb = sb("onesb", [P, P], bf16)
        jt = sb("jt", [1, NG])
        cbc = h2s[:].rearrange("p t d -> p (t d)").bitcast(f32)[:, KD * 6 * D:KD * (6 * D + B * P)].rearrange(
            "p (k b n) -> p k b n", k=KD, b=B)
        wout = h2s[:].rearrange("p t d -> p (t d)").bitcast(f32)[:, KD * (6 * D + B * P):KD * (7 * D + B * P)].rearrange(
            "p (k n) -> p k n", k=KD)

        ps = ctx.enter_context(nc.psum_tensor("ps", [P, 8, 512], f32))

        tabs = h2T.rearrange("p a k n -> p (a k n)")
        lag, causal, posn = tabs[:, 0:P], tabs[:, P:2 * P], tabs[:, 2 * P:3 * P + 1]
        early = sd.rearrange("p j h n -> p (j h n)").rearrange("p (a b c n) -> p a b c n", a=2, b=B, c=2)
        sgn, mag = early[:, 0], early[:, 1]

        def half(bank, at, n=P):
            return ps[:, bank, at:at + n]

        names = ("qkvu_loaded wout_loaded c_loaded tables_loaded wmod_cols_loaded wmod_rows_loaded "
                 "qbd_zeroed kv_zeroed decay_masked tables_made c_silu eps_set decays_made key_decay_made "
                 "woutg_made mod_cols mod_products mod_rows mod_sign mod_size ln1_stats ln1_moments "
                 "ln1_root ln1_inverse ln1_shift ln1_rows ln1_turned inputs_high inputs_low qk_product "
                 "qk_whole qk_high qk_low qkvu_high qkvu_low q_summed vu_product vu_taken v_low k_turned "
                 "k_decayed q_decayed y_turned y_taken sd_high sd_low sd_low_pool scores scores_decayed "
                 "values_added kv_product kv_masked kv_updated state_used squares_summed y_gated "
                 "out_product rms_root rms_inverse x1_made ln2_stats ln2_moments ln2_root ln2_inverse "
                 "ln2_shift ln2_rows h2_scaled h2_made h2_high h2_low h2_turned h2_taken logit_product "
                 "logits_taken counts_loaded c_spread row_flags expert_high expert_low expert_low_pool "
                 "dispatched_zeroed shared_loaded shared_high shared_low routing routing_exp ranks "
                 "first_left_0 first_left_1 second_left second_meta rows_turned rows_taken gate_product "
                 "up_product gate_silu inner_made inner_high inner_low inner_turned inner_taken "
                 "down_product result_made result_added gb_weighted result_scaled row_meta").split()
        s = {n: sem("s_" + n) for n in names}
        s_xg = [sem(f"s_xg{i}") for i in range(2)]
        s_x = [sem(f"s_xin{g}") for g in range(NT // GT)]
        s_st = [sem(f"s_st{i}") for i in range(2)]
        s_ld = [sem(f"s_ld{q}") for q in range(NPIECE)]
        s_qb = [sem(f"s_qb{i}") for i in range(2)]
        TURN_BANKS = ((0, 1), (6, 7), (2, 3), (4, 5))
        ROW_BANKS = ((0, 1), (6, 7))
        PROJ_BANKS = (2, 3, 4, 5)
        GATE_BANKS, UP_BANKS, DOWN_BANKS = (1, 3), (2, 6), (4, 7)
        PASSES = ((0, 0), (0, 1), (1, 0))
        block = ctx.enter_context(nc.Block())

        def late(c, b, k):
            c, b = c - (k + 1 - b) // 2, (b + k) % 2
            if isinstance(c, int) and not (0 <= c < NC):
                return None
            return 2 * c + b, c + NC * b, b

        def steps(eng, step, ahead=(), peel=NC):
            for c in range(3):
                for b in range(2):
                    step(c, b)
            with eng.Fori(3, peel) as c:
                for b in range(2):
                    step(c, b)
            for c in range(peel, NC):
                for b in range(2):
                    step(c, b)
            for i, (c, b) in enumerate(((NC, 0), (NC, 1), (NC + 1, 0))):
                if ahead and ahead[i]:
                    ahead[i]()
                step(c, b)

        def wait(eng, name, value):
            if not isinstance(value, int) or value > 0:
                eng.wait_ge(s[name] if isinstance(name, str) else name, value)

        def loop(eng, count, body):
            body(0)
            with eng.Fori(1, count) as i:
                body(i)

        def cols(tile):
            return bass.ts(tile, P)

        def low(eng, n, j):
            wait(eng, "sd_high", 4 * n + j + 1)
            eng.tensor_tensor(sp[:, 1, j], sd[:, j], sp[:, 0, j], ALU.subtract).then_inc(s["sd_low_pool" if j == 1 else "sd_low"], 1)

        def lows_done(eng, n, j):
            if j == 1:
                wait(eng, "sd_low_pool", n + 1)
            else:
                wait(eng, "sd_low", 3 * n + (1, None, 2, 3)[j])

        NF = NT + NG
        LO, MID, HI = 6, NT - 2, NT + 6
        LAST = HI + (NF - HI - 2) // 2 * 2

        def attention_over(e):
            e.wait_ge(s["logits_taken"], NT)
            e.wait_ge(s["h2_low"], NT)
            e.wait_ge(s["kv_updated"], KD * NT)

        def pipeline(eng, step, between=None, begin=-1):
            for f in range(-1, LO):
                if f >= begin:
                    step(f, f % 2)
                if between:
                    between(f)
            with eng.Fori(LO, MID, 2) as f:
                for j in range(2):
                    step(f + j, j, False)
            for f in range(MID, HI):
                step(f, f % 2)
            with eng.Fori(HI, LAST, 2) as f:
                for j in range(2):
                    step(f + j, j, True)
            for f in range(LAST, NF + 3):
                step(f, f % 2)

        def tile_at(f, k, p, routed):
            if isinstance(f, int):
                g = f - k
                return (g, g % 2, g >= NT) if 0 <= g < NF else None
            return f - k, (p - k) % 2, routed

        def by_pool(x):
            return isinstance(x, int) and (x < XPOOL or x == NE - 1)

        def inner_free(e, g, routed):
            if routed and not (isinstance(g, int) and g < NT + 2):
                wait(e, "inner_turned", g - NT - 1)
            else:
                wait(e, "down_product", g - 1)

        def place(g, p):
            c = (g - p) // 2
            return c + NC * p

        def weights(part, low):
            return low * NPIECE * PIECE + part * PIECE

        @block.sync
        def _(e):
            e.dma_start(wmod[:, :, 0:2 * D], t["wmod"][:, :, 0:2 * D]).then_inc(s["wmod_cols_loaded"], 16)
            xin = t["x"].rearrange("(t p) d -> p t d", p=P)
            for g in range(NT // GT):
                e.dma_start(xres[:, GT * g:GT * (g + 1), :], xin[:, GT * g:GT * (g + 1), :]).then_inc(s_x[g], 16)
            e.dma_start(wmod[:, :, 2 * D:6 * D], t["wmod"][:, :, 2 * D:6 * D]).then_inc(s["wmod_rows_loaded"], 16)
            e.dma_start(wqkvu, t["wqkvu"]).then_inc(s["qkvu_loaded"], 16)
            e.dma_start(wout, t["wout"]).then_inc(s["wout_loaded"], 16)
            for q in range(NPIECE):
                e.dma_start(early_stage[:, q * PIECE:(q + 1) * PIECE], t["wexp"][NSH, :, q, :]).then_inc(s["shared_loaded"], 16)
            e.wait_ge(s["shared_loaded"], 16 * NPIECE)
            e.wait_ge(s["qbd_zeroed"], 2)
            zeros = qbd[0].rearrange("p k h a n -> p (k h a n)").bitcast(u32)
            rows = t["xg"].rearrange("(j p) d -> p j d", p=P)
            per = KD * HP * P * 2 // ROW
            nfill = 0
            for j in range(0, NG, per):
                m = min(per, NG - j)
                e.dma_start(rows[:, j:j + m, :], zeros[:, 0:m * ROW // 2].rearrange("p (j d) -> p j d", j=m)).then_inc(s["dispatched_zeroed"], 16)
                nfill += 16
            e.dma_start(t["out"][B * S:ACC, :], zeros[:, 0:D].bitcast(f32)).then_inc(s["dispatched_zeroed"], 16)
            e.wait_ge(s["dispatched_zeroed"], nfill + 16)
            def step(c, b):
                me = late(c, b, 0)
                if me is None:
                    return
                n, tile, _ = me
                if isinstance(c, int) and n == 0:
                    e.wait_ge(s["qk_low"], 2 * KD * B)
                    e.wait_ge(s["qbd_zeroed"], 2)
                if isinstance(c, int) and n == 2:
                    e.wait_ge(s["qk_low"], 2 * KD * NT // GT)
                wait(e, "scores", 4 * n - 4)
                for h in range(HP):
                    rows = slice(h * DH, (h + 1) * DH)
                    e.dma_start(qbd[b][rows, :, h].rearrange("p k a n -> p k (a n)"),
                                q_hl[rows, :, bass.ds(tile, 1)].rearrange("p k t a n -> p k (t a n)")).then_inc(s_qb[b], 16)
            steps(e, step)

            def load_expert(x):
                for q in range(NPIECE):
                    if x:
                        e.wait_ge(s_ld[q], 16 * x)
                    e.dma_start(stage(x, q), t["wexp"][x, :, q, :]).then_inc(s_ld[q], 16)

            def load_rows(g, p, routed):
                if routed:
                    row = g - NT if isinstance(g, int) else e.snap(g - NT)
                    if isinstance(g, int) and g < NT + 2:
                        e.wait_ge(s["rows_taken"], g - 1)
                    else:
                        wait(e, "row_meta", g - 2 - NT + 1)
                    e.dma_start(xg[p].bitcast(u32).unsqueeze(1),
                                t["xg"].rearrange("(j p) d -> p j d", p=P)[:, bass.ds(row, 1), :]).then_inc(s_xg[p], 16)
                else:
                    e.wait_ge(s["h2_low"], g + 1)
                    if g < 2:
                        e.wait_ge(s["ln1_turned"], NT)
                    wait(e, "rows_taken", g - 1)
                    e.dma_start(xg[p][:, 0:2 * D].unsqueeze(1), h2s[:, bass.ds(place(g, p), 1), 0:2 * D]).then_inc(s_xg[p], 16)

            def store_shared(g, p):
                wait(e, "result_made", g + 1)
                e.dma_start(t["out"][0:B * S, :].rearrange("(t p) d -> p t d", p=P)[:, bass.ds(place(g, p), 1), :],
                            yb[p].unsqueeze(1)).then_inc(s_st[p], 16)

            load_rows(0, 0, False)
            load_rows(1, 1, False)
            load_rows(2, 0, False)
            e.wait_ge(s["vu_product"], NT)
            e.wait_ge(s["q_decayed"], NT)
            e.wait_ge(s["y_gated"], NT)
            e.wait_ge(s["values_added"], 4 * NT)
            load_expert(0)
            load_expert(1)
            for x in range(NE):
                for g in range(2 * x + 3, 2 * x + 5):
                    if g < NT:
                        load_rows(g, g % 2, False)
                for g in range(2 * x - 4, 2 * x - 2):
                    if 0 <= g < NT - 6:
                        store_shared(g, g % 2)
                if x + 2 < NE:
                    load_expert(x + 2)
            e.wait_ge(s["first_left_0"], 16 * NT // 2)
            e.wait_ge(s["first_left_1"], 16 * NT // 2)
            e.wait_ge(s["second_left"], 16 * NT)
            for g in range(NT, NT + 6):
                load_rows(g, g % 2, True)
                store_shared(g - 6, g % 2)
            end = NF - (NF - NT) % 2
            with e.Fori(NT + 6, end, 2) as g:
                for j in range(2):
                    load_rows(g + j, j, True)
            for g in range(end, NF):
                load_rows(g, g % 2, True)
            e.wait_ge(s["result_added"], 16 * NG)

        @block.gpsimd
        def _(e):
            for b in range(2):
                e.memset(qbd[b], 0.0).then_inc(s["qbd_zeroed"], 1)
            e.memset(kv, 0.0).then_inc(s["kv_zeroed"], 1)
            for k in range(KD):
                e.wait_ge(s["qkvu_high"], k + 1)
                e.tensor_tensor(w_hl[:, 1, k], wqkvu[:, k], w_hl[:, 0, k], ALU.subtract).then_inc(s["qkvu_low"], 1)
            for q in range(NPIECE):
                e.wait_ge(s["shared_high"], q + 1)
                at_ = SHARED_AT
                e.tensor_tensor(wx[:, at_ + weights(q, 1):at_ + weights(q, 1) + PIECE],
                                early_stage[:, q * PIECE:(q + 1) * PIECE],
                                wx[:, at_ + weights(q, 0):at_ + weights(q, 0) + PIECE], ALU.subtract).then_inc(s["shared_low"], 1)

            e.wait_ge(s["mod_rows"], 3 * B)
            e.wait_ge(s["wout_loaded"], 16)
            for b in range(B):
                e.tensor_tensor(woutg[:, b], wout, modr[:, b, 0:1, :].to_broadcast([P, KD, D]), ALU.mult).then_inc(s["woutg_made"], 1)
            e.wait_ge(s["decays_made"], NH)
            e.tensor_tensor(decay, decay, causal[:, :].unsqueeze(1).to_broadcast([P, NH, P]), ALU.mult).then_inc(s["decay_masked"], 1)

            def prepare(n, tile, p):
                if isinstance(n, int) and n == 2:
                    e.wait_ge(s["qk_low"], 2 * KD * NT // GT)
                wait(e, "state_used", n - 1)
                parts = q_hl[:, :, bass.ds(tile, 1)]
                e.tensor_tensor(qdec[:, p].unsqueeze(2), parts[:, :, :, 0], parts[:, :, :, 1], ALU.add).then_inc(s["q_summed"], 1)
                wait(e, "q_summed", n + 1)
                e.tensor_tensor(qdec[:, p], qdec[:, p], dq[:, :, :], ALU.mult).then_inc(s["q_decayed"], 1)

            def step(c, b):
                nx, me, pp = (late(c, b, k) for k in (-1, 0, 3))
                if me is not None:
                    n, tile, p = me
                    wait(e, "vu_taken", 3 * n + 2)
                    wait(e, "values_added", 4 * n - 4)
                    e.tensor_tensor(vp[:, p, 1], vtok[:, p, :], vp[:, p, 0], ALU.subtract).then_inc(s["v_low"], 1)
                if pp is not None:
                    w, tile, p = pp
                    wait(e, "ln2_rows", w + 1)
                    e.tensor_tensor(xn2[:, p], xn2[:, p], modr[:, p, 2], ALU.mult).then_inc(s["h2_scaled"], 1)
                    wait(e, "h2_scaled", w + 1)
                    wait(e, "h2_turned", w - 1)
                    wait(e, "h2_high", w - 1)
                    e.tensor_tensor(h2[:, p], xn2[:, p], modr[:, p, 1], ALU.add).then_inc(s["h2_made"], 1)
                if me is not None:
                    low(e, n, 1)
                if nx is not None:
                    prepare(*nx)
                if pp is not None:
                    wait(e, "h2_high", w + 1)
                    wait(e, "h2_made", w + 1)
                    e.tensor_tensor(h2s[:, bass.ds(tile, 1), D:2 * D], h2[:, p:p + 1, :],
                                    h2s[:, bass.ds(tile, 1), 0:D], ALU.subtract).then_inc(s["h2_low"], 1)
            e.wait_ge(s["qk_low"], 2 * KD * B)
            e.wait_ge(s["key_decay_made"], 1)
            prepare(0, 0, 0)
            steps(e, step, peel=NC - 1)

            attention_over(e)
            e.memset(dst_i[:], 0)

            def split_low(x):
                q = NPIECE - 1
                e.wait_ge(s["expert_high"], NPIECE * (x + 1))
                wait(e, "expert_low_pool", min(x, XPOOL))
                wait(e, "expert_low", NPIECE * x)
                at_ = x * SLOT
                e.tensor_tensor(wx[:, at_ + weights(q, 1):at_ + weights(q, 1) + PIECE], stage(x, q),
                                wx[:, at_ + weights(q, 0):at_ + weights(q, 0) + PIECE], ALU.subtract).then_inc(s["expert_low_pool"], 1)

            def dispatch(which, half_, name):
                for n in range(half_ * NT // 2, (half_ + 1) * NT // 2):
                    e.indirect_dma_start(t["xg"], bass.IndirectOffsetOnAxis(ap=(idx1, idx2)[which][:, n:n + 1], axis=0),
                                         h2s[:, n, :].bitcast(u32), None).then_inc(s[name], 16)

            split_low(0)
            split_low(1)
            e.wait_ge(s["routing"], RT_PLACED)
            dispatch(0, 0, "first_left_0")
            split_low(2)
            dispatch(0, 1, "first_left_1")
            for h, left in enumerate(("first_left_0", "first_left_1")):
                e.wait_ge(s[left], 16 * NT // 2)
                part = slice(h * NT // 2, (h + 1) * NT // 2)
                e.tensor_copy(h2s[:, part, 2 * D:ROW].bitcast(f32), pool_w2[:, part]).then_inc(s["second_meta"], 1)
                e.wait_ge(s["second_meta"], h + 1)
                dispatch(1, h, "second_left")
            split_low(NE - 1)
            e.wait_ge(s_st[0], 16 * NT // 2)
            e.wait_ge(s_st[1], 16 * NT // 2)
            for g in range(NG):
                e.wait_ge(s["row_meta"], g + 1)
                e.wait_ge(s["result_made"], NT + g + 1)
                if g:
                    e.wait_ge(s["result_added"], 16 * g)
                e.indirect_dma_start(t["out"], bass.IndirectOffsetOnAxis(ap=dst_i[:, g:g + 1], axis=0),
                                     yb[g % 2], None, compute_op=ALU.add).then_inc(s["result_added"], 16)

        @block.scalar
        def _(e):
            e.dma_start(cT[:], t["cT"]).then_inc(s["c_loaded"], 16)
            e.dma_start(kept[:], t["kept"]).then_inc(s["tables_loaded"], 16)
            e.dma_start(tabs[:, 0:3 * P + 1], t["decay_tables"]).then_inc(s["tables_loaded"], 16)
            e.dma_start(jt[:], t["jt"]).then_inc(s["counts_loaded"], 16)
            e.wait_ge(s["c_loaded"], 16)
            e.activation(cs[:], cT[:], ACT.Silu).then_inc(s["c_silu"], 1)
            e.wait_ge(s["tables_made"], 6)
            e.wait_ge(s["eps_set"], 2)
            for h in range(NH):
                e.activation(decay[:, h, :], lag[:, :], ACT.Exp, scale=nsl[:, h:h + 1]).then_inc(s["decays_made"], 1)
            for k in range(KD):
                e.activation(dq[:, k, :], posn[:, 0:P], ACT.Exp, scale=nsl[:, NH + k:NH + k + 1])
                e.activation(bdec[:, k:k + 1], posn[:, P - 1:P], ACT.Exp, scale=nsl[:, NH + k:NH + k + 1]).then_inc(s["decays_made"], 1)
            e.activation(dk[:, :, :], slr.unsqueeze(2).to_broadcast([P, NH, DH]), ACT.Exp,
                         scale=npos[:, 0:1]).then_inc(s["key_decay_made"], 1)
            e.wait_ge(s["ln1_moments"], NT)
            e.activation(rs1[:, 0, :], mv1[:, :, 1], ACT.Sqrt, bias=epst[:, 0:1]).then_inc(s["ln1_root"], 1)
            e.wait_ge(s["mod_cols"], 1)
            for i in range(NT // GT):
                b, g = i % B, i // B + NT // GT // B * (i % B)
                e.wait_ge(s["ln1_turned"], GT * (i + 1))
                for k in range(KD):
                    wait(e, "inputs_low", KD * (i - B) + k + 1 if i >= B else 0)
                    for dst in (whole[:, 2 * b + k], h_hl[:, 0, k, g * GT * P:(g + 1) * GT * P]):
                        e.activation(dst, ps[:, TURN_BANKS[i][k], :], ACT.Identity,
                                     scale=modc[:, 1, k, b:b + 1], bias=modc[:, 0, k, b:b + 1]).then_inc(s["inputs_high"], 1)
                for k in ((), range(KD), (), ())[i]:
                    e.wait_ge(s["qkvu_loaded"], 16)
                    e.activation(w_hl[:, 0, k], wqkvu[:, k], ACT.Copy).then_inc(s["qkvu_high"], 1)
                for q in ((), (), (0,), (1, 2))[i]:
                    at_ = SHARED_AT
                    e.wait_ge(s["shared_loaded"], 16 * NPIECE)
                    e.activation(wx[:, at_ + weights(q, 0):at_ + weights(q, 0) + PIECE],
                                 early_stage[:, q * PIECE:(q + 1) * PIECE], ACT.Copy).then_inc(s["shared_high"], 1)

            e.wait_ge(s["shared_low"], NPIECE)

            def queries_keys(i):
                for b in range(B):
                    g = i + NT // GT // B * b
                    for j in range(2 * KD):
                        e.wait_ge(s["qk_product"], 2 * KD * (B * i + b) + j + 1)
                        src = ps[:, PROJ_BANKS[j], :]
                        done = B * i + b
                        if isinstance(done, int) and not done:
                            e.wait_ge(s["inputs_low"], KD * NT // GT)
                        else:
                            e.wait_ge(s["qk_low"], 2 * KD * done - 2 * KD + j + 1)
                        e.activation(whole[:, j], src, ACT.Silu).then_inc(s["qk_whole"], 1)
                        if j < KD:
                            e.activation(q_hl[:, j, bass.ts(g, GT), 0], src.rearrange("p (t n) -> p t n", t=GT), ACT.Silu).then_inc(s["qk_high"], 1)
                        else:
                            e.activation(k_hl[:, 0, j - KD, bass.ts(g, GT * P)], src, ACT.Silu).then_inc(s["qk_high"], 1)
            loop(e, NT // GT // B, queries_keys)
            e.wait_ge(s["kv_zeroed"], 1)

            def step_attention(c, b):
                me, va, pr, pp = (late(c, b, k) for k in range(4))

                def high(j):
                    if me is not None:
                        wait(e, "scores_decayed", 4 * n + j + 1)
                        wait(e, "values_added", 4 * n + j - 3)
                        e.activation(sp[:, 0, j], sd[:, j], ACT.Copy).then_inc(s["sd_high"], 1)
                if me is not None:
                    n, tile, p = me
                    wait(e, "vu_product", n + 1)
                    wait(e, "values_added", 4 * n - 4)
                    wait(e, "kv_product", n - 1)
                    e.activation(vtok[:, p, :], half(0, 0, D), ACT.Copy).then_inc(s["vu_taken"], 1)
                    e.activation(vp[:, p, 0], half(0, 0, D), ACT.Copy).then_inc(s["vu_taken"], 1)
                    wait(e, "y_gated", n - 1)
                    e.activation(utok[:, p], half(0, D, D), ACT.Copy).then_inc(s["vu_taken"], 1)
                if pr is not None:
                    m, _, q = pr
                    wait(e, "y_turned", m + 1)
                    wait(e, "out_product", m - 1)
                    e.activation(yT[:, q], half(7, D, D).rearrange("p (k n) -> p k n", k=KD), ACT.Copy).then_inc(s["y_taken"], 1)
                high(0)
                if pr is not None:
                    wait(e, "squares_summed", m + 1)
                    e.activation(rs2[:, q, 0:1], rs2[:, q, 5:6], ACT.Sqrt, scale=1.0 / D, bias=epst[:, 1:2]).then_inc(s["rms_root"], 1)
                if pp is not None:
                    w, place_w, r = pp
                    wait(e, "h2_made", w + 1)
                    e.activation(h2s[:, bass.ds(place_w, 1), 0:D], h2[:, r:r + 1, :], ACT.Copy).then_inc(s["h2_high"], 1)
                high(1)
                if pp is not None:
                    wait(e, "h2_turned", w + 1)
                    wait(e, "logit_product", w - 1)
                    e.activation(h2T[:, r], half(4, 0, D).rearrange("p (k n) -> p k n", k=KD), ACT.Copy).then_inc(s["h2_taken"], 1)
                high(2)
                if pr is not None:
                    wait(e, "ln2_moments", m + 1)
                    e.activation(rs2[:, q, 2:3], mv2[:, q, 1:2], ACT.Sqrt, bias=epst[:, 0:1]).then_inc(s["ln2_root"], 1)
                if va is not None:
                    v, _, q = va
                    wait(e, "y_gated", v + 1)
                    wait(e, "rms_root", v - 1)
                    e.activation(sq[:, q], half(5, 0, D), ACT.Square, accum_out=rs2[:, q, 5:6]).then_inc(s["squares_summed"], 1)
                high(3)
                if pr is not None:
                    wait(e, "ln2_shift", m + 1)
                    wait(e, "h2_made", m - 1)
                    e.activation(xn2[:, pr[2]:pr[2] + 1, :], xres[:, bass.ds(pr[1], 1), :], ACT.Identity,
                                 scale=rs2[:, pr[2], 3:4], bias=rs2[:, pr[2], 4:5]).then_inc(s["ln2_rows"], 1)
                if pp is not None:
                    wait(e, "logit_product", w + 1)
                    e.activation(logit[:, bass.ds(place_w, 1), :], half(4, D, NE).unsqueeze(1), ACT.Copy).then_inc(s["logits_taken"], 1)

            def split_high(x, q):
                wait(e, "expert_low", NPIECE * x)
                e.wait_ge(s_ld[q], 16 * x + 16)
                e.activation(wx[:, bass.ds(x * SLOT + weights(q, 0), PIECE)], stage(x, q), ACT.Copy).then_inc(s["expert_high"], 1)

            def step(f, p, routed=None):
                if (y := tile_at(f, 2, p, routed)) and y[2]:
                    g, q, _ = y
                    wait(e, "inner_turned", g - NT + 1)
                    if not isinstance(g, int) or g >= NT + 2:
                        wait(e, "down_product", g - 1)
                    e.activation(hsT[q], ps[:, 5, :].bitcast(bf16), ACT.Copy).then_inc(s["inner_taken"], 1)
                if (y := tile_at(f, 2, p, routed)) and y[2]:
                    g, q, _ = y
                    wait(e, "row_meta", g - NT + 1)
                    if not isinstance(g, int) or g >= NT + 2:
                        wait(e, "result_made", g - 1)
                    e.activation(gbw[q].unsqueeze(1), modr[:, 0, 3:4, :], ACT.Copy,
                                 scale=wrow[:, 0, bass.ds(g - NT, 1)]).then_inc(s["gb_weighted"], 1)
                if (y := tile_at(f, 0, p, routed)):
                    g, q, _ = y
                    shared = not y[2]
                    wait(e, "gate_product", g + 1)
                    wait(e, "inner_made", g - 1)
                    e.activation(sg[q], ps[:, GATE_BANKS[q], :], ACT.Silu).then_inc(s["gate_silu"], 1)
                    if shared and q == 1:
                        split_high((g - 1) // 2, 2)
                    elif shared and not (isinstance(g, int) and g == 0):
                        split_high(g // 2, 0)
                    wait(e, "inner_made", g + 1)
                    inner_free(e, g, y[2])
                    if isinstance(g, int) and g == 0:
                        e.wait_ge(s["out_product"], NT)
                    e.activation(hs[q][:, 0:FF], hf[q], ACT.Copy).then_inc(s["inner_high"], 1)
                    if shared and q == 0 and not (isinstance(g, int) and g == 0):
                        split_high(g // 2, 1)

            def first_inner():
                e.wait_ge(s["kv_product"], NT)
                e.wait_ge(s["state_used"], NT)
                step(0, 0)

            def extra(f):
                if f == -1:
                    e.wait_ge(s["routing"], 2)
                    e.activation(ex, lm, ACT.Exp).then_inc(s["routing_exp"], 1)
                if f == 0:
                    split_high(0, 0)
                    split_high(0, 1)
            steps(e, step_attention, (None, None, first_inner))
            pipeline(e, step, extra, begin=1)

        @block.vector
        def _(e):
            e.memset(epst[:, 0:1], LN_EPS).then_inc(s["eps_set"], 1)
            e.memset(epst[:, 1:2], RMS_EPS).then_inc(s["eps_set"], 1)
            for g in range(NT // GT):
                e.wait_ge(s_x[g], 16)
                for i in range(GT * g, GT * (g + 1)):
                    e.bn_stats(st1[:, i, :], xres[:, i, :]).then_inc(s["ln1_stats"], 1)
                if g == 0:
                    e.wait_ge(s["tables_loaded"], 32)
                    e.tensor_copy(identb[:], ident[:]).then_inc(s["tables_made"], 1)
                    e.tensor_copy(onesb[:], ones[:]).then_inc(s["tables_made"], 1)
                    e.tensor_scalar(ustrict[:], lag, 1.0, None, ALU.is_ge).then_inc(s["tables_made"], 1)
                    e.tensor_scalar(nsl[:, 0:NH], slr[:, :], -1.0, None, ALU.mult).then_inc(s["tables_made"], 1)
                    e.tensor_scalar(nsl[:, NH:NH + KD], slc[:, :], -1.0, None, ALU.mult).then_inc(s["tables_made"], 1)
                    e.tensor_scalar(npos[:, :], posn[:, P:P + 1], -1.0, None, ALU.mult).then_inc(s["tables_made"], 1)
            e.wait_ge(s["ln1_stats"], NT)
            for i in range(NT):
                e.bn_aggr(mv1[:, i, :], st1[:, i, :]).then_inc(s["ln1_moments"], 1)
            e.wait_ge(s["c_silu"], 1)
            e.tensor_copy(cbc, cs[:].unsqueeze(3).to_broadcast([P, KD, B, P])).then_inc(s["c_spread"], 1)
            e.wait_ge(s["mod_products"], 1)
            pm = half(4, 0, 2 * KD * B).rearrange("p (a k b) -> p a k b", a=2, k=KD)
            e.tensor_copy(modc[:, 0], pm[:, 0])
            e.tensor_scalar(modc[:, 1], pm[:, 1], 1.0, None, ALU.add).then_inc(s["mod_cols"], 1)
            e.wait_ge(s["ln1_root"], 1)
            e.reciprocal(rs1[:, 1, :], rs1[:, 0, :]).then_inc(s["ln1_inverse"], 1)
            e.wait_ge(s["ln1_inverse"], 1)
            e.scalar_tensor_tensor(out=rs1[:, 2, :], in0=mv1[:, :, 0], scalar=-1.0, in1=rs1[:, 1, :],
                                   op0=ALU.mult, op1=ALU.mult).then_inc(s["ln1_shift"], 1)
            e.wait_ge(s["ln1_shift"], 1)

            def split_inputs(i):
                b, g = i % B, i // B + NT // GT // B * (i % B)
                for k in range(KD):
                    e.wait_ge(s["inputs_high"], 2 * (KD * i + k + 1))
                    part = slice(g * GT * P, (g + 1) * GT * P)
                    e.tensor_tensor(h_hl[:, 1, k, part], whole[:, 2 * b + k], h_hl[:, 0, k, part], ALU.subtract).then_inc(s["inputs_low"], 1)

            def normalise(i):
                for b in range(B):
                    for j in range(GT):
                        n = GT * (B * i + b) + j
                        tile = GT * (i + NT // GT // B * b) + j
                        wait(e, "ln1_turned", n - 3)
                        e.tensor_scalar(xn[:, j:j + 1, :], xres[:, bass.ds(tile, 1), :], rs1[:, 1, bass.ds(tile, 1)],
                                        rs1[:, 2, bass.ds(tile, 1)], ALU.mult, ALU.add).then_inc(s["ln1_rows"], 1)
            normalise(0)
            normalise(1)
            for i in range(NT // GT):
                split_inputs(i)
            e.wait_ge(s["mod_products"], 2)
            for b in range(B):
                src = ps[:, ROW_BANKS[b][0]:ROW_BANKS[b][1] + 1, :].rearrange("p a (c n) -> p (a c) n", c=2)
                e.tensor_copy(modr[:, b, 1:2, :], src[:, 1:2])
                e.tensor_scalar(modr[:, b, 2:3, :], src[:, 2:3], 1.0, None, ALU.add).then_inc(s["mod_rows"], 1)
                for j in (0, 3):
                    e.tensor_scalar(sgn[:, b, j // 3, :], src[:, j], 0.0, 2.0, ALU.is_ge, ALU.mult).then_inc(s["mod_sign"], 1)
                    e.wait_ge(s["mod_sign"], 2 * b + j // 3 + 1)
                    e.scalar_tensor_tensor(out=mag[:, b, j // 3, :], in0=sgn[:, b, j // 3, :], scalar=-1.0,
                                           in1=src[:, j], op0=ALU.add, op1=ALU.mult).then_inc(s["mod_size"], 1)
            e.wait_ge(s["mod_size"], 2 * B)
            e.tensor_scalar(mag, mag, 0.25, None, ALU.max).then_inc(s["mod_size"], 1)
            e.wait_ge(s["mod_size"], 2 * B + 1)
            for b in range(B):
                for j in (0, 3):
                    e.scalar_tensor_tensor(out=modr[:, b, j, :], in0=sgn[:, b, j // 3, :], scalar=-1.0,
                                           in1=mag[:, b, j // 3, :], op0=ALU.add, op1=ALU.mult).then_inc(s["mod_rows"], 1)
            with e.Fori(0, NT // GT // B) as i:
                for b in range(B):
                    g = i + NT // GT // B * b
                    for j in range(2 * KD):
                        e.wait_ge(s["qk_high"], 2 * KD * (B * i + b) + j + 1)
                        e.wait_ge(s["qk_whole"], 2 * KD * (B * i + b) + j + 1)
                        if j < KD:
                            parts = q_hl[:, j, bass.ts(g, GT)]
                            e.tensor_tensor(parts[:, :, 1], whole[:, j].rearrange("p (t n) -> p t n", t=GT),
                                            parts[:, :, 0], ALU.subtract).then_inc(s["qk_low"], 1)
                        else:
                            e.tensor_tensor(k_hl[:, 1, j - KD, bass.ts(g, GT * P)], whole[:, j],
                                            k_hl[:, 0, j - KD, bass.ts(g, GT * P)], ALU.subtract).then_inc(s["qk_low"], 1)
            e.wait_ge(s["decay_masked"], 1)
            e.wait_ge(s["key_decay_made"], 1)
            e.wait_ge(s["kv_zeroed"], 1)

            def scores(n, j):
                wait(e, "scores", 4 * n + j + 1)
                if not isinstance(n, int) or n:
                    lows_done(e, n - 1, j)
                e.tensor_tensor(sd[:, j], ps[:, 2 + j % 2, :].rearrange("p (h n) -> p h n", h=4),
                                decay[:, 4 * j:4 * j + 4, :], ALU.mult).then_inc(s["scores_decayed"], 1)

            def step_attention(c, b):
                me, va, pr = late(c, b, 0), late(c, b, 1), late(c, b, 2)
                if pr is not None:
                    m, mt, q = pr
                if va is not None:
                    v, _, r = va
                    wait(e, "kv_product", v + 1)
                    e.tensor_tensor(um, half(6, 0, D).rearrange("p (k n) -> p k n", k=KD), headm[:], ALU.mult).then_inc(s["kv_masked"], 1)
                if me is not None:
                    n, tile, p = me
                    wait(e, "k_turned", n + 1)
                    wait(e, "kv_product", n - 1)
                    e.tensor_tensor(kdec[:, p, :], half(1, 0, D), dk[:].rearrange("p h d -> p (h d)"), ALU.mult).then_inc(s["k_decayed"], 1)
                if va is not None:
                    wait(e, "kv_masked", v + 1)
                    wait(e, "state_used", v + 1)
                    for k in range(KD):
                        e.scalar_tensor_tensor(out=kv[:, r, k, :], in0=kv[:, r, k, :], scalar=bdec[:, k:k + 1],
                                               in1=um[:, k, :], op0=ALU.mult, op1=ALU.add).then_inc(s["kv_updated"], 1)
                if me is not None:
                    scores(n, 0)
                    scores(n, 1)
                    low(e, n, 0)
                if pr is not None:
                    wait(e, "rms_root", m + 1)
                    e.reciprocal(rs2[:, q, 1:2], rs2[:, q, 0:1]).then_inc(s["rms_inverse"], 1)
                    wait(e, "rms_inverse", m + 1)
                    wait(e, "out_product", m + 1)
                    e.scalar_tensor_tensor(out=xres[:, bass.ds(mt, 1), :], in0=half(7, 0, D).unsqueeze(1), scalar=rs2[:, q, 1:2],
                                           in1=xres[:, bass.ds(mt, 1), :], op0=ALU.mult, op1=ALU.add).then_inc(s["x1_made"], 1)
                    wait(e, "x1_made", m + 1)
                if me is not None:
                    scores(n, 2)
                if pr is not None:
                    e.bn_stats(st2[:, q, :], xres[:, bass.ds(mt, 1), :]).then_inc(s["ln2_stats"], 1)
                    wait(e, "ln2_stats", m + 1)
                    wait(e, "ln2_shift", m - 1)
                if va is not None:
                    wait(e, "values_added", 4 * v + 4)
                    wait(e, "vu_taken", 3 * v + 3)
                    wait(e, "y_turned", v - 1)
                    e.tensor_tensor(ytok[:, r], half(5, 0, D), utok[:, r], ALU.mult).then_inc(s["y_gated"], 1)
                if pr is not None:
                    e.bn_aggr(mv2[:, q, :], st2[:, q, :]).then_inc(s["ln2_moments"], 1)
                if me is not None:
                    low(e, n, 2)
                if me is not None:
                    scores(n, 3)
                if pr is not None:
                    wait(e, "ln2_root", m + 1)
                    e.reciprocal(rs2[:, q, 3:4], rs2[:, q, 2:3]).then_inc(s["ln2_inverse"], 1)
                    wait(e, "ln2_inverse", m + 1)
                    e.scalar_tensor_tensor(out=rs2[:, q, 4:5], in0=mv2[:, q, 0:1], scalar=-1.0, in1=rs2[:, q, 3:4],
                                           op0=ALU.mult, op1=ALU.mult).then_inc(s["ln2_shift"], 1)
                if me is not None:
                    low(e, n, 3)

            count = [0]

            def link(ins):
                ins.then_inc(s["routing"], 1)
                count[0] += 1
                e.wait_ge(s["routing"], count[0])

            def over(a):
                return a.unsqueeze(2).to_broadcast([P, NT, NE])

            def routing():
                revb = rev[:, :].unsqueeze(1).to_broadcast([P, NT, NE])
                yield link(e.tensor_reduce(mx, logit[:], AX.X, ALU.max))
                yield link(e.tensor_tensor(lm, logit[:], over(mx), ALU.subtract))
                e.wait_ge(s["routing_exp"], 1)
                yield link(e.tensor_reduce(sm, ex, AX.X, ALU.add))
                yield link(e.reciprocal(rsm, sm))
                yield link(e.tensor_tensor(pr, ex, over(rsm), ALU.mult))

                def first_largest(probs, largest, mark, onehot):
                    yield link(e.tensor_reduce(largest, probs, AX.X, ALU.max))
                    yield link(e.tensor_tensor(eq, probs, over(largest), ALU.is_equal))
                    yield link(e.tensor_tensor(pick, eq, revb, ALU.mult))
                    yield link(e.tensor_reduce(mark, pick, AX.X, ALU.max))
                    yield link(e.tensor_tensor(onehot, revb, over(mark), ALU.is_equal))

                yield from first_largest(pr, p1, f1, m1)
                yield link(e.scalar_tensor_tensor(out=pr2, in0=m1, scalar=-2.0, in1=pr, op0=ALU.mult, op1=ALU.add))
                yield from first_largest(pr2, p2, f2, m2)
                yield link(e.tensor_tensor(picked, m1.rearrange("p t e -> p (t e)"), m2.rearrange("p t e -> p (t e)"), ALU.add))
                yield link(e.tensor_tensor(den, p1, p2, ALU.add))
                yield link(e.reciprocal(rden, den))
                meta = h2s[:, :, 2 * D:ROW].bitcast(f32)
                e.tensor_tensor(meta[:, :, 0], p1, rden, ALU.mult)
                e.tensor_copy(meta[:, :, 1], tok1[:])
                e.tensor_tensor(pool_w2[:, :, 0], p2, rden, ALU.mult)
                yield link(e.tensor_copy(pool_w2[:, :, 1], tok1[:]))
                e.wait_ge(s["ranks"], 1)
                yield link(e.tensor_scalar(tiles_i, half(5, NT * NE, NE), float(P - 1), None, ALU.add))
                yield link(e.tensor_scalar(tiles_s, tiles_i, 7, None, ALU.arith_shift_right))
                yield link(e.tensor_copy(tiles_f, tiles_s))
                yield link(e.tensor_tensor_scan(tiles_end, ones[:, 0:NE], tiles_f, 0.0, ALU.mult, ALU.add))
                yield link(e.tensor_tensor(base, tiles_end, tiles_f, ALU.subtract))
                yield link(e.tensor_scalar(base, base, float(P), None, ALU.mult))
                yield link(e.tensor_tensor(pos, half(5, 0, NT * NE).rearrange("p (t e) -> p t e", t=NT),
                                     base.unsqueeze(1).to_broadcast([P, NT, NE]), ALU.add))
                yield link(e.tensor_tensor(eq, pos, m1, ALU.mult))
                e.tensor_reduce(mx, eq, AX.X, ALU.add)
                yield link(e.tensor_tensor(pick, pos, m2, ALU.mult))
                yield link(e.tensor_reduce(sm, pick, AX.X, ALU.add))
                e.tensor_copy(idx1, mx)
                yield link(e.tensor_copy(idx2, sm))
                assert count[0] == RT_PLACED, count[0]
                yield link(e.tensor_tensor(gej[0:1], jt[:, :].unsqueeze(2).to_broadcast([1, NG, NE]),
                                     tiles_end[0:1].unsqueeze(1).to_broadcast([1, NG, NE]), ALU.is_ge))
                yield link(e.tensor_reduce(slot_f[0:1], gej[0:1], AX.X, ALU.add))
                yield link(e.tensor_scalar(slot_f[0:1], slot_f[0:1], float(NE - 1), float(SLOT), ALU.min, ALU.mult))
                yield link(e.tensor_copy(slot_of[:], slot_f[0:1]))
                assert count[0] == RT_DONE, count[0]

            def split_low(x, q):
                wait(e, "expert_low", NPIECE * x)
                e.wait_ge(s["expert_high"], NPIECE * x + q + 1)
                if q == 1:
                    wait(e, "expert_low_pool", min(x, XPOOL) if isinstance(x, int) else XPOOL)
                e.tensor_tensor(wx[:, bass.ds(x * SLOT + weights(q, 1), PIECE)], stage(x, q),
                                wx[:, bass.ds(x * SLOT + weights(q, 0), PIECE)], ALU.subtract).then_inc(
                                    s["expert_low"], 2 if q == 1 and by_pool(x) else 1)

            def take_rows(f, p, routed):
                if (y := tile_at(f, -1, p, routed)):
                    g, q, _ = y
                    wait(e, "rows_turned", g + 1)
                    wait(e, "up_product", g - 1)
                    e.tensor_copy(xT[q].bitcast(u32), ps[:, 0, 0:D].bitcast(u32)).then_inc(s["rows_taken"], 1)
                if (y := tile_at(f, -1, p, routed)) and y[2]:
                    g, q, _ = y
                    m = xg[q][:, 2 * D:ROW].bitcast(f32)
                    j = bass.ds(g - NT, 1)
                    wait(e, s_xg[q], 8 * (g - q) + 16)
                    wait(e, "row_meta", g - NT)
                    e.tensor_scalar(zer[:, 0:1], m[:, 1:2], 0.0, spare_row[:, 0:1], ALU.is_equal, ALU.mult).then_inc(s["row_flags"], 1)
                    e.tensor_scalar(wrow[:, 1, j], m[:, 1:2], float(S), m[:, 0:1], ALU.is_gt, ALU.mult).then_inc(s["row_flags"], 1)
                    wait(e, "row_flags", 2 * (g - NT + 1))
                    e.tensor_tensor(wrow[:, 0, j], m[:, 0:1], wrow[:, 1, j], ALU.subtract)
                    e.scalar_tensor_tensor(out=dst_i[:, j], in0=m[:, 1:2], scalar=-1.0, in1=zer[:, 0:1],
                                           op0=ALU.add, op1=ALU.add).then_inc(s["row_meta"], 1)

            def step(f, p, routed=None):
                take_rows(f, p, routed)
                if (y := tile_at(f, 1, p, routed)):
                    g, q, _ = y
                    wait(e, "inner_high", g + 1)
                    e.tensor_tensor(hs[q][:, FF:2 * FF], hf[q], hs[q][:, 0:FF], ALU.subtract).then_inc(s["inner_low"], 1)
                if (y := tile_at(f, 0, p, routed)):
                    g, q, _ = y
                    shared = not y[2]
                    if shared and q == 1:
                        split_low((g - 1) // 2, 1)
                    wait(e, "up_product", g + 1)
                    wait(e, "gate_silu", g + 1)
                    e.tensor_tensor(hf[q], ps[:, UP_BANKS[q], :], sg[q], ALU.mult).then_inc(s["inner_made"], 1)
                    if shared and q == 0 and not (isinstance(g, int) and g == 0):
                        split_low(g // 2, 0)
                    if shared and q == 1 and not by_pool((g - 1) // 2):
                        split_low((g - 1) // 2, 2)
                if (y := tile_at(f, 3, p, routed)):
                    g, q, _ = y
                    if y[2]:
                        r = g - NT
                        wait(e, "gb_weighted", r + 1)
                        e.scalar_tensor_tensor(out=gbw[q].unsqueeze(1), in0=modr[:, 1, 3:4, :], scalar=wrow[:, 1, bass.ds(r, 1)],
                                               in1=gbw[q].unsqueeze(1), op0=ALU.mult, op1=ALU.add).then_inc(s["result_scaled"], 1)
                        wait(e, "down_product", g + 1)
                        wait(e, "result_scaled", g + 1)
                        if isinstance(g, int) and g < NT + 2:
                            e.wait_ge(s_st[q], 16 * NT // 2)
                        else:
                            wait(e, "result_added", 16 * (g - 2 - NT + 1))
                        e.tensor_tensor(yb[q], ps[:, DOWN_BANKS[q], 0:D], gbw[q], ALU.mult).then_inc(s["result_made"], 1)
                    else:
                        wait(e, s_st[q], 8 * (g - q))
                        wait(e, "down_product", g + 1)
                        if isinstance(g, int) and g == 0:
                            e.wait_ge(s["h2_made"], NT)
                        e.tensor_tensor(yb[q], ps[:, DOWN_BANKS[q], 0:D], modr[:, q, 3, :], ALU.mult).then_inc(s["result_scaled"], 1)
                        wait(e, "result_scaled", g + 1)
                        e.tensor_tensor(yb[q].unsqueeze(1), yb[q].unsqueeze(1), xres[:, bass.ds(place(g, q), 1), :],
                                        ALU.add).then_inc(s["result_made"], 1)

            def first_rows():
                e.wait_ge(s["kv_product"], NT)
                step(-1, 1)

            def first_inner():
                e.wait_ge(s["state_used"], NT)
                e.wait_ge(s["kv_updated"], KD * NT)
                step(0, 0)
            steps(e, step_attention, (first_rows, None, first_inner))
            attention_over(e)
            e.wait_ge(s["counts_loaded"], 16)
            todo = routing()
            share = {-1: 8, 0: 9, 1: 6, 2: 6, 3: 6, 4: 2, 5: 2}

            def extra(f):
                for _ in range(share[f]):
                    next(todo, None)
                if f == 0:
                    split_low(0, 0)
            pipeline(e, step, extra, begin=1)
            assert not list(todo)

        @block.tensor
        def _(e):
            e.wait_ge(s["c_silu"], 1)
            e.wait_ge(s["wmod_cols_loaded"], 16)
            for a in range(2):
                for k in range(KD):
                    for kk in range(KD):
                        ins = e.matmul(half(4, (a * KD + k) * B, B), wmod[:, kk, (a * KD + k) * P:(a * KD + k + 1) * P],
                                       cs[:, kk, :], start=kk == 0, stop=kk == KD - 1)
            ins.then_inc(s["mod_products"], 1)

            def turn(i):
                for b in range(B):
                    for j in range(GT):
                        n = GT * (B * i + b) + j
                        e.wait_ge(s["ln1_rows"], n + 1)
                        if n == 3 * GT:
                            e.wait_ge(s["mod_cols"], 1)
                        for k in range(KD):
                            ins = e.transpose(half(TURN_BANKS[B * i + b][k], j * P), xn[:, j, k * P:(k + 1) * P], ident[:])
                        ins.then_inc(s["ln1_turned"], 1)
            e.wait_ge(s["tables_loaded"], 32)
            turn(0)
            turn(1)
            e.wait_ge(s["c_spread"], 1)
            e.wait_ge(s["wmod_rows_loaded"], 16)
            e.wait_ge(s["inputs_high"], 2 * KD * B)
            for b in range(B):
                for a in range(2):
                    for kk in range(KD):
                        ins = e.matmul(ps[:, ROW_BANKS[b][a], :], cbc[:, kk, b, :],
                                       wmod[:, kk, 2 * D + 512 * a:2 * D + 512 * (a + 1)], start=kk == 0, stop=kk == KD - 1)
            ins.then_inc(s["mod_products"], 1)
            e.wait_ge(s["qkvu_low"], KD)

            def project(i):
                for b in range(B):
                    g = i + NT // GT // B * b
                    for j in range(2 * KD):
                        done = B * i + b
                        if isinstance(done, int) and not done:
                            e.wait_ge(s["inputs_high"], 2 * KD * NT // GT)
                        else:
                            e.wait_ge(s["qk_high"], 2 * KD * done - 2 * KD + j + 1)
                        if isinstance(done, int) and j == 0:
                            e.wait_ge(s["inputs_low"], KD * (done + 1))
                        for n in range(3 * KD):
                            kk, (a, w) = n // 3, PASSES[n % 3]
                            ins = e.matmul(ps[:, PROJ_BANKS[j], :], w_hl[:, w, kk, j * P:(j + 1) * P],
                                           h_hl[:, a, kk, bass.ts(g, GT * P)], start=n == 0, stop=n == 3 * KD - 1)
                        ins.then_inc(s["qk_product"], 1)
            project(0)
            e.wait_ge(s["inputs_low"], KD * NT // GT)
            with e.Fori(1, NT // GT // B) as i:
                project(i)
            e.wait_ge(s["mod_rows"], 3 * B)
            e.wait_ge(s["qk_high"], 2 * KD * NT // GT - 2)
            e.wait_ge(s["qk_low"], 2 * KD * B)
            e.wait_ge(s["woutg_made"], B)

            def qk(n, tile, p, j):
                wait(e, "scores_decayed", 4 * n + j - 1)
                if j == 0:
                    wait(e, s_qb[p], 16 * HP * (tile - NC * p + 1))
                k = j // 2
                for i, (a, w) in enumerate(PASSES):
                    ins = e.matmul(ps[:, 2 + j % 2, :].rearrange("p (h n) -> p h n", h=4), k_hl[:, w, k, cols(tile)],
                                   qbd[p][:, k, 4 * (j % 2):4 * (j % 2) + 4, a, :], start=i == 0, stop=i == 2)
                ins.then_inc(s["scores"], 1)

            def inter(n, p):
                wait(e, "squares_summed", n)
                wait(e, "y_gated", n)
                wait(e, "q_decayed", n + 1)
                wait(e, "kv_updated", KD * (n - 1))
                wait(e, "v_low", n + 1)
                for k in range(KD):
                    ins = e.matmul(half(5, k * P), qdec[:, p, k, :], kv[:, p, k, :], start=k == 0, stop=False,
                                   skip_group_check=True)
                ins.then_inc(s["state_used"], 1)

            def values(n, p, j):
                lows_done(e, n, j)
                for h in range(4 * j, 4 * j + 4):
                    for i, (a, v) in enumerate(PASSES):
                        ins = e.matmul(half(5, h * DH, DH), sp[:, a, j, h % 4, :], vp[:, p, v, h * DH:(h + 1) * DH],
                                       start=False, stop=i == 2, skip_group_check=True)
                ins.then_inc(s["values_added"], 1)

            def step_attention(c, b):
                me, va, pr, pp = (late(c, b, k) for k in range(4))
                if me is not None:
                    n, tile, p = me
                    wait(e, "vu_taken", 3 * n)
                    if isinstance(c, int) and n == 2:
                        e.wait_ge(s["qk_low"], 2 * KD * NT // GT)
                    for i in range(3 * KD):
                        k, (a, w) = i // 3, PASSES[i % 3]
                        ins = e.matmul(ps[:, 0, :], h_hl[:, a, k, cols(tile)], w_hl[:, w, k, 2 * D:4 * D],
                                       start=i == 0, stop=i == 3 * KD - 1)
                    ins.then_inc(s["vu_product"], 1)
                    wait(e, "k_decayed", n)
                    for k in range(KD):
                        for a in range(2):
                            ins = e.matmul(half(1, k * P), k_hl[:, a, k, cols(tile)], identb[:], start=a == 0, stop=a == 1)
                    ins.then_inc(s["k_turned"], 1)
                if va is not None:
                    v, _, r = va
                    if isinstance(c, int) and v == 0:
                        e.wait_ge(s["qk_high"], 2 * KD * NT // GT)
                    inter(v, r)
                for j in range(4):
                    if va is not None:
                        values(v, r, j)
                    if me is not None:
                        qk(n, tile, p, j)
                    if j == 0 and pr is not None:
                        m, _, q = pr
                        wait(e, "y_gated", m + 1)
                        wait(e, "x1_made", m)
                        for k in range(KD):
                            ins = e.transpose(half(7, D + k * P), ytok[:, q, k * P:(k + 1) * P], ident[:])
                        ins.then_inc(s["y_turned"], 1)
                    if j == 1 and pr is not None:
                        wait(e, "y_taken", m + 1)
                        for k in range(KD):
                            ins = e.matmul(half(7, 0, D), yT[:, q, k, :], woutg[:, q, k, :], start=k == 0, stop=k == KD - 1)
                        ins.then_inc(s["out_product"], 1)
                    if j == 2 and pp is not None:
                        w, _, r2 = pp
                        wait(e, "h2_made", w + 1)
                        wait(e, "logits_taken", w)
                        for k in range(KD):
                            ins = e.transpose(half(4, k * P), h2[:, r2, k * P:(k + 1) * P], ident[:])
                        ins.then_inc(s["h2_turned"], 1)
                if me is not None:
                    wait(e, "k_decayed", n + 1)
                    wait(e, "kv_masked", n)
                    wait(e, "vu_taken", 3 * n + 1)
                    for k in range(KD):
                        ins = e.matmul(half(6, k * P), kdec[:, p, k * P:(k + 1) * P], vtok[:, p, k * P:(k + 1) * P],
                                       start=True, stop=True)
                    ins.then_inc(s["kv_product"], 1)
                if pp is not None:
                    wait(e, "h2_taken", w + 1)
                    for k in range(KD):
                        ins = e.matmul(half(4, D), h2T[:, r2, k, :], wg[:, k, :], start=k == 0, stop=k == KD - 1)
                    ins.then_inc(s["logit_product"], 1)


            def turn_rows(g, p, routed):
                wait(e, s_xg[p], 8 * (g - p) + 16)
                wait(e, "rows_taken", g)
                for m in range(4):
                    ins = e.transpose(ps[:, 0, 0:D].bitcast(bf16)[:, m * P:(m + 1) * P], xg[p][:, m * P:(m + 1) * P], identb[:])
                ins.then_inc(s["rows_turned"], 1)

            def slot(g, routed):
                if not routed:
                    return SHARED_AT
                return e.value_load(slot_of[0:1, bass.ds(g - NT, 1)], min_val=0, max_val=(NE - 1) * SLOT)

            def gate_up(g, p, routed):
                at_ = slot(g, routed)
                wait(e, "rows_taken", g + 1)
                for part, name, free in ((0, "gate_product", "gate_silu"), (1, "up_product", "inner_made")):
                    wait(e, free, g - 1)
                    n = 0
                    if not routed:
                        for m in range(KF):
                            for n in range(3 * KD):
                                k, (a, w) = n // 3, PASSES[n % 3]
                                off = at_ + weights(part, w) + k * FF + m * P
                                ins = e.matmul(half((GATE_BANKS, UP_BANKS)[part][p], m * P), wx[:, off:off + P],
                                               xT[p][:, (2 * a + k) * P:(2 * a + k + 1) * P],
                                               start=n == 0, stop=n == 3 * KD - 1)
                        ins.then_inc(s[name], 1)
                        continue
                    for k in range(KD):
                        for a, w in PASSES:
                            ins = e.matmul(ps[:, (GATE_BANKS, UP_BANKS)[part][p], :], xT[p][:, (2 * a + k) * P:(2 * a + k + 1) * P],
                                           wx[:, bass.ds(at_ + weights(part, w) + k * FF, FF)],
                                           start=n == 0, stop=n == 3 * KD - 1)
                            n += 1
                    ins.then_inc(s[name], 1)

            def turn_inner(g, p):
                wait(e, "inner_low", g + 1)
                wait(e, "inner_taken", g - NT)
                for m in range(2 * KF):
                    ins = e.transpose(ps[:, 5, :].bitcast(bf16)[:, m * P:(m + 1) * P], hs[p][:, m * P:(m + 1) * P], identb[:])
                ins.then_inc(s["inner_turned"], 1)

            def down(g, p, routed):
                at_ = slot(g, routed)
                inner = hsT[p] if routed else hs[p]
                if routed:
                    wait(e, "inner_taken", g - NT + 1)
                else:
                    wait(e, "inner_low", g + 1)
                wait(e, "result_made", g - 1)
                n = 0
                for k in range(KF):
                    for a, w in PASSES:
                        ins = e.matmul(ps[:, DOWN_BANKS[p], 0:D], inner[:, (KF * a + k) * P:(KF * a + k + 1) * P],
                                       wx[:, bass.ds(at_ + weights(2, w) + k * D, D)],
                                       start=n == 0, stop=n == 3 * KF - 1)
                        n += 1
                ins.then_inc(s["down_product"], 1)

            def step(f, p, routed=None):
                if (y := tile_at(f, -1, p, routed)):
                    turn_rows(*y)
                if (y := tile_at(f, 0, p, routed)):
                    if isinstance(f, int) and f == NT:
                        e.wait_ge(s["expert_low"], NPIECE * NE)
                        e.wait_ge(s["expert_low_pool"], XPOOL + 1)
                        e.wait_ge(s["routing"], RT_DONE)
                    gate_up(*y)
                if (y := tile_at(f, 2, p, routed)):
                    down(*y)
                if (y := tile_at(f, 1, p, routed)) and y[2]:
                    turn_inner(y[0], y[1])

            def rank(f):
                if f != 1:
                    return
                e.wait_ge(s["routing"], RT_PICKED)
                e.matmul(half(5, 0, NT * NE), ustrict[:], picked, start=True, stop=False, skip_group_check=True)
                for k in range(1, NT):
                    e.matmul(half(5, k * NE, (NT - k) * NE), onesb[:], picked[:, 0:(NT - k) * NE],
                             start=False, stop=False, skip_group_check=True)
                for k in range(NT):
                    ins = e.matmul(half(5, NT * NE, NE), onesb[:], picked[:, k * NE:(k + 1) * NE],
                                   start=False, stop=k == NT - 1, skip_group_check=True)
                ins.then_inc(s["ranks"], 1)

            def first_rows():
                e.wait_ge(s["vu_taken"], 3 * NT)
                step(-1, 1)

            def first_gate_up():
                e.wait_ge(s["k_decayed"], NT)
                e.wait_ge(s["scores_decayed"], 4 * NT)
                step(0, 0)

            def second_gate_up():
                e.wait_ge(s["kv_masked"], NT)
                step(1, 1)
            steps(e, step_attention, (first_rows, first_gate_up, second_gate_up))
            attention_over(e)
            e.wait_ge(s["x1_made"], NT)
            pipeline(e, step, rank, begin=2)



KEPT_PARTS = dict(ident=P, ones=P, slr=NH, slc=KD, headm=KD * P, wg=KD * P, rev=NE, tok1=NT, spare_row=1)
KEPT = sum(KEPT_PARTS.values())


def constants():
    f = np.float32
    m = np.arange(P)
    same = (m[:, None] // DH == m[None, :] // DH).astype(f)
    return dict(
        lag=np.maximum(m[None, :] - m[:, None], 0).astype(f),
        causal=(m[None, :] >= m[:, None]).astype(f),
        posn=np.concatenate([np.tile(m + 1, (P, 1)), (P - 1 - m)[:, None]], 1).astype(f),
        headm=np.concatenate([same] * KD, 1),
        ident=np.eye(P, dtype=f),
        ones=np.ones((P, P), f),
        rev=np.tile(NE - np.arange(NE), (P, 1)).astype(f),
        tok1=(np.arange(NT)[None, :] * P + m[:, None] + 1).astype(f),
        spare_row=(B * S + 1 + m)[:, None].astype(f),
        jt=np.arange(NG)[None, :].astype(f),
    )


def layout(i):
    def rows(w):
        return np.ascontiguousarray(w.reshape(-1, P, w.shape[-1]).transpose(1, 0, 2))

    slope = i["L0_attn_slope_rate"].reshape(NH)
    a = dict(
        x=i["L0_attn_x"].reshape(B * S, D),
        cT=rows(i["L0_c"].T),
        slr=np.ascontiguousarray(np.broadcast_to(slope, (P, NH))),
        slc=np.ascontiguousarray(np.repeat(slope, DH).reshape(KD, P).T),
        wmod=rows(i["L0_wmod"]),
        wqkvu=rows(i["L0_attn_W_qkvu"].T),
        wout=rows(i["L0_attn_W_out"].T),
    )
    a["wg"] = np.zeros((P, KD, P), np.float32)
    a["wg"][:, :, 0:NE] = rows(i["L0_ffn_wg"].T)
    gate = [*i["L0_ffn_ex_gate"], i["L0_ffn_sh_gate"]]
    up = [*i["L0_ffn_ex_up"], i["L0_ffn_sh_up"]]
    down = [*i["L0_ffn_ex_down"], i["L0_ffn_sh_down"]]
    a["wexp"] = np.stack([np.stack([rows(w.T).reshape(P, PIECE) for w in three], 1)
                          for three in zip(gate, up, down)])
    a["wg"] = a["wg"].reshape(P, KD * P)
    a.update(constants())
    a["kept"] = np.concatenate([a.pop(n) for n in KEPT_PARTS], 1)
    a["decay_tables"] = np.concatenate([a.pop(n) for n in ("lag", "causal", "posn")], 1)
    return a


def kernel(**inputs):
    import concourse.bacc as bacc
    from concourse.bass_utils import run_bass_kernel_spmd

    nc = bacc.Bacc("TRN2", target_bir_lowering=False, num_devices=1)
    arrays = layout({k: np.asarray(v) for k, v in inputs.items()})
    t = {n: nc.dram_tensor("in_" + n, a.shape, mybir.dt.from_np(a.dtype), kind="ExternalInput").ap()
         for n, a in arrays.items()}
    t["xg"] = nc.dram_tensor("dispatched", [NG * P, ROW // 2], mybir.dt.uint32).ap()
    t["out"] = nc.dram_tensor("out", [ACC, D], mybir.dt.float32, kind="ExternalOutput").ap()
    build(nc, t)
    r = run_bass_kernel_spmd(nc, [{"in_" + n: a for n, a in arrays.items()}], core_ids=[0])
    return r.results[0]["out"][0:B * S].reshape(B, S, D)
```
